# Optimizing a Trainium2 kernel written in Bass

```python
import numpy as np
import jax
import jax.numpy as jnp

def _softmax(x, axis=-1):
    return jax.nn.softmax(x, axis=axis)

def _gelu(x):
    return jax.nn.gelu(x, approximate=True)

def _silu(x):
    return jax.nn.silu(x)

def _sigmoid(x):
    return jax.nn.sigmoid(x)

def _layernorm(x, axis=-1, eps=1e-05):
    m = jnp.mean(x, axis=axis, keepdims=True)
    v = jnp.var(x, axis=axis, keepdims=True)
    return (x - m) / jnp.sqrt(v + eps)

def _scatter_add(tgt, idx, src, axis=0):
    return tgt.at[idx].add(src)

def _segment_sum(src, seg, n):
    return jax.ops.segment_sum(src, seg, n)
kernel_name = 'mk_prb_d4_jaxref_r4_b03d82'

def setup_inputs(seed: int=0):
    np.random.seed(seed)
    _w = jnp.asarray

    def _L0_attn_setup():
        import jax, jax.numpy as jnp
        import numpy as np
        B, T, C = (4, 1024, 256)
        LN_EPS = 1e-05

        def _ln(x, g, b):
            m = x.mean(-1, keepdims=True)
            v = ((x - m) ** 2).mean(-1, keepdims=True)
            return (x - m) / jnp.sqrt(v + LN_EPS) * g + b

        def _shift(x, time_shift):
            b = x.shape[0]
            return jnp.concatenate([jnp.broadcast_to(time_shift, (b, 1, x.shape[2])), x[:, :-1]], axis=1)

        def _wkv(w, u, k, v):
            b, t, c = k.shape
            aa0 = jnp.zeros((b, c), k.dtype)
            bb0 = jnp.ones((b, c), k.dtype)
            pp0 = jnp.full((b, c), -1e+38, k.dtype)

            def step(carry, kv_t):
                aa, bb, pp = carry
                kk, vv = kv_t
                uu_kk = u + kk
                p = jnp.maximum(pp, uu_kk)
                e1 = jnp.exp(pp - p)
                e2 = jnp.exp(uu_kk - p)
                y = (e1 * aa + e2 * vv) / (e1 * bb + e2)
                ww_kk = w + kk
                pu = jnp.maximum(pp + w, ww_kk)
                e1u = jnp.exp(pp + w - pu)
                e2u = jnp.exp(ww_kk - pu)
                aa_n = e1u * aa + e2u * vv
                bb_n = e1u * bb + e2u
                pp_n = pu + jnp.log(bb_n)
                return ((aa_n, bb_n, pp_n), y)
            _, ys = jax.lax.scan(step, (aa0, bb0, pp0), (k.transpose(1, 0, 2), v.transpose(1, 0, 2)))
            return ys.transpose(1, 0, 2)
        key = jax.random.key(seed)
        ks = jax.random.split(key, 10)
        s1 = 1.0 / np.sqrt(C)
        s4 = 1.0 / np.sqrt(4 * C)
        return {'x': jax.random.normal(ks[0], (B, T, C), jnp.float32), 'time_decay': jax.random.normal(ks[1], (C,), jnp.float32), 'time_first': jax.random.normal(ks[2], (C,), jnp.float32), 'time_shift': jnp.zeros((1, 1, C), jnp.float32), 'Wk': jax.random.normal(ks[3], (C, C), jnp.float32) * s1, 'Wv': jax.random.normal(ks[4], (C, C), jnp.float32) * s1, 'Wr': jax.random.normal(ks[5], (C, C), jnp.float32) * s1, 'Wck': jax.random.normal(ks[6], (C, 4 * C), jnp.float32) * s1, 'Wcv': jax.random.normal(ks[7], (4 * C, C), jnp.float32) * s4, 'Wcr': jax.random.normal(ks[8], (C, C), jnp.float32) * s1, 'ln1_g': jnp.ones((C,), jnp.float32), 'ln1_b': jnp.zeros((C,), jnp.float32), 'ln2_g': jnp.ones((C,), jnp.float32), 'ln2_b': jnp.zeros((C,), jnp.float32)}
    _L0_attn_in = _L0_attn_setup()

    def _L0_ffn_setup():
        import jax, jax.numpy as jnp
        import numpy as np
        from jax import lax
        DIM = 256
        INTER = 128
        N_EXPERTS = 16
        TOPK = 4
        ROUTE_SCALE = 2.5
        VOCAB = 8000

        def _silu_and_mul(gu):
            gate, up = jnp.split(gu, 2, axis=-1)
            return jax.nn.silu(gate) * up
        key = jax.random.key(seed)
        ks = jax.random.split(key, 8)
        x = jax.random.normal(ks[0], (2, 128, DIM), dtype=jnp.float32)
        input_ids = jax.random.randint(ks[1], (2, 128), 0, VOCAB)
        s = 0.02
        gate_w = jax.random.normal(ks[2], (N_EXPERTS, DIM), dtype=jnp.float32) * s
        gate_b = jax.random.normal(ks[3], (N_EXPERTS,), dtype=jnp.float32) * s
        w13 = jax.random.normal(ks[4], (N_EXPERTS, 2 * INTER, DIM), dtype=jnp.float32) * s
        w2 = jax.random.normal(ks[5], (N_EXPERTS, DIM, INTER), dtype=jnp.float32) * s
        w13_s = jax.random.normal(ks[6], (2 * INTER, DIM), dtype=jnp.float32) * s
        w2_s = jax.random.normal(ks[7], (DIM, INTER), dtype=jnp.float32) * s
        return {'x': x, 'input_ids': input_ids, 'gate_w': gate_w, 'gate_b': gate_b, 'w13': w13, 'w2': w2, 'w13_s': w13_s, 'w2_s': w2_s}
    _L0_ffn_in = _L0_ffn_setup()

    def _L1_attn_setup():
        import jax, jax.numpy as jnp
        import numpy as np
        HID = 256
        HEADS = 16
        FEAT = 16
        HD = HID // HEADS
        EPS = 1e-05
        LN_EPS = 1e-05
        B, T = (1, 256)
        IU, JU = np.triu_indices(FEAT, 1)

        def _feature_map(x, gamma, beta):
            mu = x.mean(axis=-1, keepdims=True)
            var = ((x - mu) ** 2).mean(axis=-1, keepdims=True)
            xn = (x - mu) / jnp.sqrt(var + LN_EPS) * gamma + beta
            diag = xn * xn
            off = xn[..., IU] * xn[..., JU]
            return jnp.concatenate([diag * FEAT ** (-0.5), off * (2.0 / FEAT) ** 0.5], axis=-1)
        key = jax.random.key(seed)
        ks = jax.random.split(key, 5)
        s = 0.02
        return {'hidden_states': jax.random.normal(ks[0], (B, T, HID), dtype=jnp.float32), 'Wq': jax.random.normal(ks[1], (FEAT * HEADS, HID), dtype=jnp.float32) * s, 'Wk': jax.random.normal(ks[2], (FEAT * HEADS, HID), dtype=jnp.float32) * s, 'Wv': jax.random.normal(ks[3], (HEADS * HD, HID), dtype=jnp.float32) * s, 'Wo': jax.random.normal(ks[4], (HID, HEADS * HD), dtype=jnp.float32) * s, 'gamma': jnp.ones((FEAT,), dtype=jnp.float32), 'beta': jnp.zeros((FEAT,), dtype=jnp.float32)}
    _L1_attn_in = _L1_attn_setup()

    def _L1_ffn_setup():
        import jax, jax.numpy as jnp
        import numpy as np
        THRESH_FACTOR = 0.7

        def ternary_quantize(w):
            delta = THRESH_FACTOR * jnp.mean(jnp.abs(w))
            return jnp.where(w > delta, 1.0, jnp.where(w < -delta, -1.0, 0.0)).astype(w.dtype)
        key = jax.random.key(seed)
        k1, k2, k3 = jax.random.split(key, 3)
        B, S, D_IN, D_OUT = (8, 1024, 256, 256)
        inp = {'input': jax.random.normal(k1, (B, S, D_IN), dtype=jnp.float32), 'weight': jax.random.normal(k2, (D_OUT, D_IN), dtype=jnp.float32) * (1.0 / np.sqrt(D_IN)), 'alpha': jnp.ones((1,), dtype=jnp.float32), 'bias': jax.random.normal(k3, (D_OUT,), dtype=jnp.float32) * (1.0 / np.sqrt(D_IN))}
        return inp
    _L1_ffn_in = _L1_ffn_setup()

    def _L2_attn_setup():
        import jax, jax.numpy as jnp
        import numpy as np
        N_HEAD = 16
        FUTURE_DIM = 4

        def _layernorm(x, g, b, eps=1e-05):
            mu = jnp.mean(x, axis=-1, keepdims=True)
            var = jnp.mean(jnp.square(x - mu), axis=-1, keepdims=True)
            return (x - mu) * jax.lax.rsqrt(var + eps) * g + b

        def _future_attn_head(h, W_qkvf, W_conv, W_proj):
            B, T, D = h.shape
            H, hs, F = (N_HEAD, D // N_HEAD, FUTURE_DIM)
            NEG = jnp.float32(-jnp.inf)
            qkvf = h @ W_qkvf.T
            q, k, v, f = jnp.split(qkvf, 4, axis=-1)
            to_h = lambda t: t.reshape(B, T, H, hs).transpose(0, 2, 1, 3)
            q, k, v, f = (to_h(q), to_h(k), to_h(v), to_h(f))
            attn = jnp.einsum('bhtd,bhsd->bhts', q, k) * hs ** (-0.5)
            rows = jnp.arange(T)[:, None]
            causal_mask = jnp.arange(T)[None, :] <= rows
            causal_attn = jnp.where(causal_mask, attn, 0.0)
            padded_causal = jnp.pad(causal_attn, ((0, 0), (0, 0), (0, 0), (0, F)))
            up_future = jnp.einsum('bhtc,cdf->btfhd', f, W_conv).reshape(B, T, F, D)
            k_future = jnp.einsum('btfc,dc->btfd', up_future, W_qkvf[D:2 * D])
            k_future = k_future.reshape(B, T, F, H, hs).transpose(0, 3, 1, 2, 4)
            future_attention = jnp.einsum('bhtd,bhtfd->bhtf', q, k_future)
            cols_f = rows + 1 + jnp.arange(F)[None, :]
            full_attn = padded_causal.at[:, :, rows, cols_f].set(future_attention)
            full_mask = jnp.arange(T + F)[None, :] <= rows + F
            full_attn = jnp.where(full_mask, full_attn, NEG)
            sm = jax.nn.softmax(full_attn, axis=-1)
            sm_causal = jnp.where(causal_mask, sm[..., :T], 0.0)
            unpadded_future = sm[:, :, rows, cols_f]
            v_future = jnp.einsum('btfc,dc->btfd', up_future, W_qkvf[2 * D:3 * D])
            v_future = v_future.reshape(B, T, F, H, hs).transpose(0, 3, 1, 2, 4)
            future_x = jnp.einsum('bhtf,bhtfd->bhtd', unpadded_future, v_future)
            causal_x = jnp.einsum('bhts,bhsd->bhtd', sm_causal, v)
            new_x = (causal_x + future_x).transpose(0, 2, 1, 3).reshape(B, T, D)
            return new_x @ W_proj.T
        key = jax.random.key(seed)
        ks = jax.random.split(key, 7)
        B, T, D, H, F = (2, 256, 256, N_HEAD, FUTURE_DIM)
        hs = D // H
        s = 0.02
        return {'x': jax.random.normal(ks[0], (B, T, D), jnp.float32), 'W_qkvf': jax.random.normal(ks[1], (4 * D, D), jnp.float32) * s, 'W_conv': jax.random.normal(ks[2], (hs, hs, F), jnp.float32) * s, 'W_proj': jax.random.normal(ks[3], (D, D), jnp.float32) * s, 'W_ff1': jax.random.normal(ks[4], (D, 4 * D), jnp.float32) * s, 'W_ff2': jax.random.normal(ks[5], (4 * D, D), jnp.float32) * s, 'ln1_g': jnp.ones((D,), jnp.float32), 'ln1_b': jnp.zeros((D,), jnp.float32), 'ln2_g': jnp.ones((D,), jnp.float32), 'ln2_b': jnp.zeros((D,), jnp.float32)}
    _L2_attn_in = _L2_attn_setup()

    def _L2_ffn_setup():
        import jax, jax.numpy as jnp
        import numpy as np
        E = 8
        H = 256
        D = 256
        TOP_K = 2
        key = jax.random.key(seed)
        k0, k1, k2, k3 = jax.random.split(key, 4)
        x = jax.random.normal(k0, (1, 512, H), dtype=jnp.float32)
        router_w = jax.random.normal(k1, (E, H), dtype=jnp.float32) * (1.0 / np.sqrt(H))
        up_proj = jax.random.normal(k2, (E, H, 2 * D), dtype=jnp.float32) * (1.0 / np.sqrt(H))
        down_proj = jax.random.normal(k3, (E, D, H), dtype=jnp.float32) * (1.0 / np.sqrt(D))
        return {'x': x, 'router_w': router_w, 'up_proj': up_proj, 'down_proj': down_proj}
    _L2_ffn_in = _L2_ffn_setup()

    def _L3_attn_setup():
        import jax, jax.numpy as jnp
        import numpy as np
        B, S, D = (8, 512, 256)

        def _forward(x, W_qkv, b_qkv, W_vconv):
            b, s, d = x.shape
            qkv = x @ W_qkv + b_qkv
            q, k, v = jnp.split(qkv, 3, axis=-1)
            scores = jnp.einsum('bid,bjd->bij', q, k) * (1.0 / np.sqrt(d))
            mask = jnp.tril(jnp.ones((s, s), bool))
            scores = jnp.where(mask, scores, -jnp.inf)
            A = jax.nn.softmax(scores, axis=-1)
            w0, w1, w2 = (W_vconv[:, 0], W_vconv[:, 1], W_vconv[:, 2])
            v_prev = jnp.pad(v, ((0, 0), (1, 0), (0, 0)))[:, :s]
            v_next = jnp.pad(v, ((0, 0), (0, 1), (0, 0)))[:, 1:]
            C = w0 * v_prev + w1 * v + w2 * v_next
            out = jnp.einsum('bij,bjc->bic', A, C)
            diagA = jnp.diagonal(A, axis1=1, axis2=2)
            out = out - diagA[:, :, None] * (w2 * v_next)
            return out
        key = jax.random.key(seed)
        k0, k1, k2, k3 = jax.random.split(key, 4)
        x = jax.random.normal(k0, (B, S, D), jnp.float32)
        W_qkv = jax.random.normal(k1, (D, 3 * D), jnp.float32) * (1.0 / np.sqrt(D))
        b_qkv = jax.random.normal(k2, (3 * D,), jnp.float32) * 0.02
        W_vconv = jax.random.normal(k3, (D, 3), jnp.float32) * 0.02
        return {'x': x, 'W_qkv': W_qkv, 'b_qkv': b_qkv, 'W_vconv': W_vconv}
    _L3_attn_in = _L3_attn_setup()

    def _L3_ffn_setup():
        import jax, jax.numpy as jnp
        import numpy as np
        D = 256
        H = 16
        HD = D // H
        L = 64
        E = 8
        B, T = (4, 512)
        EPS = 1e-06

        def _glorot(k, shape):
            fan_in, fan_out = (shape[-2], shape[-1])
            lim = np.sqrt(6.0 / (fan_in + fan_out)).astype(np.float32)
            return jax.random.uniform(k, shape, jnp.float32, -lim, lim)

        def _rmsnorm(x, gamma):
            return gamma * x * jax.lax.rsqrt(jnp.mean(x * x, axis=-1, keepdims=True) + EPS)
        key = jax.random.key(seed)
        ks = jax.random.split(key, 8)
        return {'x': jax.random.normal(ks[0], (B, T, D), jnp.float32), 'gamma1': jnp.ones((D,), jnp.float32), 'Wq': _glorot(ks[1], (D, D)), 'bq': jnp.zeros((D,), jnp.float32), 'Wdown': _glorot(ks[2], (D, L)), 'bdown': jnp.zeros((L,), jnp.float32), 'Wup': _glorot(ks[3], (L, 2 * D)), 'bup': jnp.zeros((2 * D,), jnp.float32), 'Wo': _glorot(ks[4], (D, D)), 'bo': jnp.zeros((D,), jnp.float32), 'gamma2': jnp.ones((D,), jnp.float32), 'Wg': _glorot(ks[5], (D, E)), 'bg': jnp.zeros((E,), jnp.float32), 'We': _glorot(ks[6], (E, D, D))}
    _L3_ffn_in = _L3_ffn_setup()
    _d = {'L0_attn_x': _L0_attn_in['x'], 'L0_attn_time_decay': _L0_attn_in['time_decay'], 'L0_attn_time_first': _L0_attn_in['time_first'], 'L0_attn_time_shift': _L0_attn_in['time_shift'], 'L0_attn_Wk': _L0_attn_in['Wk'], 'L0_attn_Wv': _L0_attn_in['Wv'], 'L0_attn_Wr': _L0_attn_in['Wr'], 'L0_attn_Wck': _L0_attn_in['Wck'], 'L0_attn_Wcv': _L0_attn_in['Wcv'], 'L0_attn_Wcr': _L0_attn_in['Wcr'], 'L0_attn_ln1_g': _L0_attn_in['ln1_g'], 'L0_attn_ln1_b': _L0_attn_in['ln1_b'], 'L0_attn_ln2_g': _L0_attn_in['ln2_g'], 'L0_attn_ln2_b': _L0_attn_in['ln2_b'], 'L0_ffn_input_ids': _L0_ffn_in['input_ids'], 'L0_ffn_gate_w': _L0_ffn_in['gate_w'], 'L0_ffn_gate_b': _L0_ffn_in['gate_b'], 'L0_ffn_w13': _L0_ffn_in['w13'], 'L0_ffn_w2': _L0_ffn_in['w2'], 'L0_ffn_w13_s': _L0_ffn_in['w13_s'], 'L0_ffn_w2_s': _L0_ffn_in['w2_s'], 'L1_attn_Wq': _L1_attn_in['Wq'], 'L1_attn_Wk': _L1_attn_in['Wk'], 'L1_attn_Wv': _L1_attn_in['Wv'], 'L1_attn_Wo': _L1_attn_in['Wo'], 'L1_attn_gamma': _L1_attn_in['gamma'], 'L1_attn_beta': _L1_attn_in['beta'], 'L1_ffn_weight': _L1_ffn_in['weight'], 'L1_ffn_alpha': _L1_ffn_in['alpha'], 'L1_ffn_bias': _L1_ffn_in['bias'], 'L2_attn_W_qkvf': _L2_attn_in['W_qkvf'], 'L2_attn_W_conv': _L2_attn_in['W_conv'], 'L2_attn_W_proj': _L2_attn_in['W_proj'], 'L2_attn_W_ff1': _L2_attn_in['W_ff1'], 'L2_attn_W_ff2': _L2_attn_in['W_ff2'], 'L2_attn_ln1_g': _L2_attn_in['ln1_g'], 'L2_attn_ln1_b': _L2_attn_in['ln1_b'], 'L2_attn_ln2_g': _L2_attn_in['ln2_g'], 'L2_attn_ln2_b': _L2_attn_in['ln2_b'], 'L2_ffn_router_w': _L2_ffn_in['router_w'], 'L2_ffn_up_proj': _L2_ffn_in['up_proj'], 'L2_ffn_down_proj': _L2_ffn_in['down_proj'], 'L3_attn_W_qkv': _L3_attn_in['W_qkv'], 'L3_attn_b_qkv': _L3_attn_in['b_qkv'], 'L3_attn_W_vconv': _L3_attn_in['W_vconv'], 'L3_ffn_gamma1': _L3_ffn_in['gamma1'], 'L3_ffn_Wq': _L3_ffn_in['Wq'], 'L3_ffn_bq': _L3_ffn_in['bq'], 'L3_ffn_Wdown': _L3_ffn_in['Wdown'], 'L3_ffn_bdown': _L3_ffn_in['bdown'], 'L3_ffn_Wup': _L3_ffn_in['Wup'], 'L3_ffn_bup': _L3_ffn_in['bup'], 'L3_ffn_Wo': _L3_ffn_in['Wo'], 'L3_ffn_bo': _L3_ffn_in['bo'], 'L3_ffn_gamma2': _L3_ffn_in['gamma2'], 'L3_ffn_Wg': _L3_ffn_in['Wg'], 'L3_ffn_bg': _L3_ffn_in['bg'], 'L3_ffn_We': _L3_ffn_in['We']}
    _x0 = _d['L0_attn_x']
    _d['L0_attn_x'] = jax.random.normal(jax.random.fold_in(jax.random.key(seed), 1), (8, 512, 256), dtype=_x0.dtype)
    del _x0
    return _d

def reference(L0_attn_x, L0_attn_time_decay, L0_attn_time_first, L0_attn_time_shift, L0_attn_Wk, L0_attn_Wv, L0_attn_Wr, L0_attn_Wck, L0_attn_Wcv, L0_attn_Wcr, L0_attn_ln1_g, L0_attn_ln1_b, L0_attn_ln2_g, L0_attn_ln2_b, L0_ffn_input_ids, L0_ffn_gate_w, L0_ffn_gate_b, L0_ffn_w13, L0_ffn_w2, L0_ffn_w13_s, L0_ffn_w2_s, L1_attn_Wq, L1_attn_Wk, L1_attn_Wv, L1_attn_Wo, L1_attn_gamma, L1_attn_beta, L1_ffn_weight, L1_ffn_alpha, L1_ffn_bias, L2_attn_W_qkvf, L2_attn_W_conv, L2_attn_W_proj, L2_attn_W_ff1, L2_attn_W_ff2, L2_attn_ln1_g, L2_attn_ln1_b, L2_attn_ln2_g, L2_attn_ln2_b, L2_ffn_router_w, L2_ffn_up_proj, L2_ffn_down_proj, L3_attn_W_qkv, L3_attn_b_qkv, L3_attn_W_vconv, L3_ffn_gamma1, L3_ffn_Wq, L3_ffn_bq, L3_ffn_Wdown, L3_ffn_bdown, L3_ffn_Wup, L3_ffn_bup, L3_ffn_Wo, L3_ffn_bo, L3_ffn_gamma2, L3_ffn_Wg, L3_ffn_bg, L3_ffn_We):

    def _L0_attn_ref(x, time_decay, time_first, time_shift, Wk, Wv, Wr, Wck, Wcv, Wcr, ln1_g, ln1_b, ln2_g, ln2_b):
        import jax, jax.numpy as jnp
        import numpy as np
        B, T, C = (4, 1024, 256)
        LN_EPS = 1e-05

        def _ln(x, g, b):
            m = x.mean(-1, keepdims=True)
            v = ((x - m) ** 2).mean(-1, keepdims=True)
            return (x - m) / jnp.sqrt(v + LN_EPS) * g + b

        def _shift(x, time_shift):
            b = x.shape[0]
            return jnp.concatenate([jnp.broadcast_to(time_shift, (b, 1, x.shape[2])), x[:, :-1]], axis=1)

        def _wkv(w, u, k, v):
            b, t, c = k.shape
            aa0 = jnp.zeros((b, c), k.dtype)
            bb0 = jnp.ones((b, c), k.dtype)
            pp0 = jnp.full((b, c), -1e+38, k.dtype)

            def step(carry, kv_t):
                aa, bb, pp = carry
                kk, vv = kv_t
                uu_kk = u + kk
                p = jnp.maximum(pp, uu_kk)
                e1 = jnp.exp(pp - p)
                e2 = jnp.exp(uu_kk - p)
                y = (e1 * aa + e2 * vv) / (e1 * bb + e2)
                ww_kk = w + kk
                pu = jnp.maximum(pp + w, ww_kk)
                e1u = jnp.exp(pp + w - pu)
                e2u = jnp.exp(ww_kk - pu)
                aa_n = e1u * aa + e2u * vv
                bb_n = e1u * bb + e2u
                pp_n = pu + jnp.log(bb_n)
                return ((aa_n, bb_n, pp_n), y)
            _, ys = jax.lax.scan(step, (aa0, bb0, pp0), (k.transpose(1, 0, 2), v.transpose(1, 0, 2)))
            return ys.transpose(1, 0, 2)
        h = _ln(x, ln1_g, ln1_b)
        hs = _shift(h, time_shift)
        k = hs @ Wk
        v = hs @ Wv
        r = hs @ Wr
        y = _wkv(time_decay, time_first, k, v)
        x = x + jax.nn.sigmoid(r) * y
        h2 = _ln(x, ln2_g, ln2_b)
        h2s = _shift(h2, time_shift)
        kk = jnp.square(jax.nn.relu(h2s @ Wck))
        kv = kk @ Wcv
        rr = jax.nn.sigmoid(h2s @ Wcr)
        x = x + rr * kv
        return x

    def _L0_ffn_ref(x, input_ids, gate_w, gate_b, w13, w2, w13_s, w2_s):
        import jax, jax.numpy as jnp
        import numpy as np
        from jax import lax
        DIM = 256
        INTER = 128
        N_EXPERTS = 16
        TOPK = 4
        ROUTE_SCALE = 2.5
        VOCAB = 8000

        def _silu_and_mul(gu):
            gate, up = jnp.split(gu, 2, axis=-1)
            return jax.nn.silu(gate) * up
        B, S, D = x.shape
        xt = x.reshape(-1, D)
        T = xt.shape[0]
        scores = jax.nn.sigmoid(xt.astype(jnp.float32) @ gate_w.T)
        biased = scores + gate_b
        _, idx = lax.top_k(biased, TOPK)
        w = jnp.take_along_axis(scores, idx, axis=-1)
        w = w / jnp.sum(w, axis=-1, keepdims=True)
        w = w * ROUTE_SCALE
        comb = jnp.zeros((T, N_EXPERTS), jnp.float32)
        comb = comb.at[jnp.arange(T)[:, None], idx].add(w)
        comb = comb.astype(x.dtype)

        def expert_body(y, args):
            w13_e, w2_e, c_e = args
            h = _silu_and_mul(xt @ w13_e.T)
            return (y + c_e[:, None] * (h @ w2_e.T), None)
        y, _ = lax.scan(expert_body, jnp.zeros_like(xt), (w13, w2, comb.T))
        y = y + _silu_and_mul(xt @ w13_s.T) @ w2_s.T
        return y.astype(x.dtype).reshape(B, S, D)

    def _L1_attn_ref(hidden_states, Wq, Wk, Wv, Wo, gamma, beta):
        import jax, jax.numpy as jnp
        import numpy as np
        HID = 256
        HEADS = 16
        FEAT = 16
        HD = HID // HEADS
        EPS = 1e-05
        LN_EPS = 1e-05
        B, T = (1, 256)
        IU, JU = np.triu_indices(FEAT, 1)

        def _feature_map(x, gamma, beta):
            mu = x.mean(axis=-1, keepdims=True)
            var = ((x - mu) ** 2).mean(axis=-1, keepdims=True)
            xn = (x - mu) / jnp.sqrt(var + LN_EPS) * gamma + beta
            diag = xn * xn
            off = xn[..., IU] * xn[..., JU]
            return jnp.concatenate([diag * FEAT ** (-0.5), off * (2.0 / FEAT) ** 0.5], axis=-1)
        b, t, _ = hidden_states.shape
        q = (hidden_states @ Wq.T).reshape(b, t, HEADS, FEAT).transpose(0, 2, 1, 3)
        k = (hidden_states @ Wk.T).reshape(b, t, HEADS, FEAT).transpose(0, 2, 1, 3)
        v = (hidden_states @ Wv.T).reshape(b, t, HEADS, HD).transpose(0, 2, 1, 3)
        phi_q = _feature_map(q, gamma, beta)
        phi_k = _feature_map(k, gamma, beta)
        kv_cum = jnp.cumsum(phi_k[..., :, None] * v[..., None, :], axis=2)
        num = jnp.einsum('bhtf,bhtfd->bhtd', phi_q, kv_cum)
        den = jnp.einsum('bhtf,bhtf->bht', phi_q, jnp.cumsum(phi_k, axis=2))[..., None] + EPS
        y = (num / den).transpose(0, 2, 1, 3).reshape(b, t, HEADS * HD)
        return y @ Wo.T

    def _L1_ffn_ref(input, weight, alpha, bias):
        import jax, jax.numpy as jnp
        import numpy as np
        THRESH_FACTOR = 0.7

        def ternary_quantize(w):
            delta = THRESH_FACTOR * jnp.mean(jnp.abs(w))
            return jnp.where(w > delta, 1.0, jnp.where(w < -delta, -1.0, 0.0)).astype(w.dtype)
        w_ternary = ternary_quantize(weight)
        w_eff = w_ternary * alpha
        out = jnp.einsum('bsd,od->bso', input, w_eff) + bias
        return out

    def _L2_attn_ref(x, W_qkvf, W_conv, W_proj, W_ff1, W_ff2, ln1_g, ln1_b, ln2_g, ln2_b):
        import jax, jax.numpy as jnp
        import numpy as np
        N_HEAD = 16
        FUTURE_DIM = 4

        def _layernorm(x, g, b, eps=1e-05):
            mu = jnp.mean(x, axis=-1, keepdims=True)
            var = jnp.mean(jnp.square(x - mu), axis=-1, keepdims=True)
            return (x - mu) * jax.lax.rsqrt(var + eps) * g + b

        def _future_attn_head(h, W_qkvf, W_conv, W_proj):
            B, T, D = h.shape
            H, hs, F = (N_HEAD, D // N_HEAD, FUTURE_DIM)
            NEG = jnp.float32(-jnp.inf)
            qkvf = h @ W_qkvf.T
            q, k, v, f = jnp.split(qkvf, 4, axis=-1)
            to_h = lambda t: t.reshape(B, T, H, hs).transpose(0, 2, 1, 3)
            q, k, v, f = (to_h(q), to_h(k), to_h(v), to_h(f))
            attn = jnp.einsum('bhtd,bhsd->bhts', q, k) * hs ** (-0.5)
            rows = jnp.arange(T)[:, None]
            causal_mask = jnp.arange(T)[None, :] <= rows
            causal_attn = jnp.where(causal_mask, attn, 0.0)
            padded_causal = jnp.pad(causal_attn, ((0, 0), (0, 0), (0, 0), (0, F)))
            up_future = jnp.einsum('bhtc,cdf->btfhd', f, W_conv).reshape(B, T, F, D)
            k_future = jnp.einsum('btfc,dc->btfd', up_future, W_qkvf[D:2 * D])
            k_future = k_future.reshape(B, T, F, H, hs).transpose(0, 3, 1, 2, 4)
            future_attention = jnp.einsum('bhtd,bhtfd->bhtf', q, k_future)
            cols_f = rows + 1 + jnp.arange(F)[None, :]
            full_attn = padded_causal.at[:, :, rows, cols_f].set(future_attention)
            full_mask = jnp.arange(T + F)[None, :] <= rows + F
            full_attn = jnp.where(full_mask, full_attn, NEG)
            sm = jax.nn.softmax(full_attn, axis=-1)
            sm_causal = jnp.where(causal_mask, sm[..., :T], 0.0)
            unpadded_future = sm[:, :, rows, cols_f]
            v_future = jnp.einsum('btfc,dc->btfd', up_future, W_qkvf[2 * D:3 * D])
            v_future = v_future.reshape(B, T, F, H, hs).transpose(0, 3, 1, 2, 4)
            future_x = jnp.einsum('bhtf,bhtfd->bhtd', unpadded_future, v_future)
            causal_x = jnp.einsum('bhts,bhsd->bhtd', sm_causal, v)
            new_x = (causal_x + future_x).transpose(0, 2, 1, 3).reshape(B, T, D)
            return new_x @ W_proj.T
        x = x + _future_attn_head(_layernorm(x, ln1_g, ln1_b), W_qkvf, W_conv, W_proj)
        h = _layernorm(x, ln2_g, ln2_b)
        x = x + jax.nn.gelu(h @ W_ff1, approximate=False) @ W_ff2
        return x

    def _L2_ffn_ref(x, router_w, up_proj, down_proj):
        import jax, jax.numpy as jnp
        import numpy as np
        E = 8
        H = 256
        D = 256
        TOP_K = 2
        B, T, _ = x.shape
        xt = x.reshape(-1, H)
        N = xt.shape[0]
        logits = jnp.einsum('nh,eh->ne', xt, router_w)
        probs = jax.nn.softmax(logits, axis=-1)
        scores, expert_idx = jax.lax.top_k(probs, TOP_K)
        scores = scores / jnp.sum(scores, axis=-1, keepdims=True)
        gate = jnp.zeros((N, E), dtype=xt.dtype).at[jnp.arange(N)[:, None], expert_idx].add(scores)
        h = jnp.einsum('nh,ehd->end', xt, up_proj)
        hidden = jax.nn.silu(h[..., :D]) * h[..., D:]
        out_e = jnp.einsum('end,edh->enh', hidden, down_proj)
        out = jnp.einsum('ne,enh->nh', gate, out_e)
        return out.reshape(B, T, H)

    def _L3_attn_ref(x, W_qkv, b_qkv, W_vconv):
        import jax, jax.numpy as jnp
        import numpy as np
        B, S, D = (8, 512, 256)

        def _forward(x, W_qkv, b_qkv, W_vconv):
            b, s, d = x.shape
            qkv = x @ W_qkv + b_qkv
            q, k, v = jnp.split(qkv, 3, axis=-1)
            scores = jnp.einsum('bid,bjd->bij', q, k) * (1.0 / np.sqrt(d))
            mask = jnp.tril(jnp.ones((s, s), bool))
            scores = jnp.where(mask, scores, -jnp.inf)
            A = jax.nn.softmax(scores, axis=-1)
            w0, w1, w2 = (W_vconv[:, 0], W_vconv[:, 1], W_vconv[:, 2])
            v_prev = jnp.pad(v, ((0, 0), (1, 0), (0, 0)))[:, :s]
            v_next = jnp.pad(v, ((0, 0), (0, 1), (0, 0)))[:, 1:]
            C = w0 * v_prev + w1 * v + w2 * v_next
            out = jnp.einsum('bij,bjc->bic', A, C)
            diagA = jnp.diagonal(A, axis1=1, axis2=2)
            out = out - diagA[:, :, None] * (w2 * v_next)
            return out
        return _forward(x, W_qkv, b_qkv, W_vconv)

    def _L3_ffn_ref(x, gamma1, Wq, bq, Wdown, bdown, Wup, bup, Wo, bo, gamma2, Wg, bg, We):
        import jax, jax.numpy as jnp
        import numpy as np
        D = 256
        H = 16
        HD = D // H
        L = 64
        E = 8
        B, T = (4, 512)
        EPS = 1e-06

        def _glorot(k, shape):
            fan_in, fan_out = (shape[-2], shape[-1])
            lim = np.sqrt(6.0 / (fan_in + fan_out)).astype(np.float32)
            return jax.random.uniform(k, shape, jnp.float32, -lim, lim)

        def _rmsnorm(x, gamma):
            return gamma * x * jax.lax.rsqrt(jnp.mean(x * x, axis=-1, keepdims=True) + EPS)
        b, t = (x.shape[0], x.shape[1])
        h = _rmsnorm(x, gamma1)
        q = (h @ Wq + bq).reshape(b, t, H, HD)
        kv = ((h @ Wdown + bdown) @ Wup + bup).reshape(b, t, H, 2 * HD)
        k, v = jnp.split(kv, 2, axis=-1)
        att = jnp.einsum('bthd,btgd->bthg', q, k) / np.sqrt(HD).astype(np.float32)
        att = jax.nn.softmax(att, axis=-1)
        out = jnp.einsum('bthg,btgd->bthd', att, v).reshape(b, t, D)
        x = x + (out @ Wo + bo)
        h2 = _rmsnorm(x, gamma2)
        gate = jax.nn.softmax(h2 @ Wg + bg, axis=-1)
        combined = jnp.einsum('btd,edf,bte->btf', h2, We, gate)
        return x + combined
    x = L0_attn_x
    xn = _layernorm(x, axis=-1)
    x = x + _L0_attn_ref(xn, L0_attn_time_decay, L0_attn_time_first, L0_attn_time_shift, L0_attn_Wk, L0_attn_Wv, L0_attn_Wr, L0_attn_Wck, L0_attn_Wcv, L0_attn_Wcr, L0_attn_ln1_g, L0_attn_ln1_b, L0_attn_ln2_g, L0_attn_ln2_b) + _L0_ffn_ref(xn, L0_ffn_input_ids, L0_ffn_gate_w, L0_ffn_gate_b, L0_ffn_w13, L0_ffn_w2, L0_ffn_w13_s, L0_ffn_w2_s)
    xn = _layernorm(x, axis=-1)
    x = x + _L1_attn_ref(xn, L1_attn_Wq, L1_attn_Wk, L1_attn_Wv, L1_attn_Wo, L1_attn_gamma, L1_attn_beta) + _L1_ffn_ref(xn, L1_ffn_weight, L1_ffn_alpha, L1_ffn_bias)
    xn = _layernorm(x, axis=-1)
    x = x + _L2_attn_ref(xn, L2_attn_W_qkvf, L2_attn_W_conv, L2_attn_W_proj, L2_attn_W_ff1, L2_attn_W_ff2, L2_attn_ln1_g, L2_attn_ln1_b, L2_attn_ln2_g, L2_attn_ln2_b) + _L2_ffn_ref(xn, L2_ffn_router_w, L2_ffn_up_proj, L2_ffn_down_proj)
    xn = _layernorm(x, axis=-1)
    x = x + _L3_attn_ref(xn, L3_attn_W_qkv, L3_attn_b_qkv, L3_attn_W_vconv) + _L3_ffn_ref(xn, L3_ffn_gamma1, L3_ffn_Wq, L3_ffn_bq, L3_ffn_Wdown, L3_ffn_bdown, L3_ffn_Wup, L3_ffn_bup, L3_ffn_Wo, L3_ffn_bo, L3_ffn_gamma2, L3_ffn_Wg, L3_ffn_bg, L3_ffn_We)
    return x

_drawn_inputs = setup_inputs


def setup_inputs(seed=0):
    import zlib

    import numpy as np

    out = dict(_drawn_inputs(seed))
    spreads = {'L0_attn_time_shift': (0.0, 0.592),
     'L0_attn_ln1_g': (1.0, 0.2),
     'L0_attn_ln1_b': (0.0, 0.316),
     'L0_attn_ln2_g': (1.0, 0.2),
     'L0_attn_ln2_b': (0.0, 0.1),
     'L1_attn_gamma': (1.0, 0.6),
     'L1_attn_beta': (0.0, 0.8),
     'L2_attn_ln1_g': (1.0, 0.6),
     'L2_attn_ln1_b': (0.0, 0.8),
     'L2_attn_ln2_g': (1.0, 0.6),
     'L2_attn_ln2_b': (0.0, 0.8),
     'L3_ffn_gamma1': (1.0, 0.6),
     'L3_ffn_bq': (0.0, 0.8),
     'L3_ffn_bdown': (0.0, 0.8),
     'L3_ffn_bup': (0.0, 0.8),
     'L3_ffn_bo': (0.0, 2.0),
     'L3_ffn_gamma2': (1.0, 0.6),
     'L3_ffn_bg': (0.0, 2.0)}
    factors = {'L0_ffn_gate_w': 8.0,
     'L0_ffn_gate_b': 8.0,
     'L0_ffn_w13': 7.965,
     'L0_ffn_w2': 7.946,
     'L0_ffn_w13_s': 8.0,
     'L0_ffn_w2_s': 8.0,
     'L1_attn_Wq': 8.0,
     'L1_attn_Wk': 8.0,
     'L1_attn_Wv': 8.0,
     'L1_attn_Wo': 8.0,
     'L1_ffn_bias': 8.0,
     'L2_attn_W_qkvf': 8.0,
     'L2_attn_W_conv': 8.0,
     'L2_attn_W_proj': 8.0,
     'L2_attn_W_ff1': 6.688,
     'L2_attn_W_ff2': 6.462,
     'L3_attn_W_qkv': 8.0,
     'L3_attn_b_qkv': 60.934,
     'L3_attn_W_vconv': 8.0,
     'L3_ffn_Wq': 5.06,
     'L3_ffn_Wdown': 2.966,
     'L3_ffn_Wup': 3.052,
     'L3_ffn_Wo': 2.961}
    for name, (base, spread) in spreads.items():
        noise = np.random.default_rng([zlib.crc32(name.encode()), seed]).standard_normal(out[name].shape)
        drawn = base * np.exp(spread * noise) if base else spread * noise
        out[name] = jnp.asarray(drawn.astype(out[name].dtype))
    for name, factor in factors.items():
        out[name] = (out[name] * factor).astype(out[name].dtype)
    return out
```

```python
from contextlib import ExitStack

import concourse.bass as bass
from concourse import mybir

F32 = mybir.dt.float32
ALU = mybir.AluOpType
ACT = mybir.ActivationFunctionType
AX = mybir.AxisListType

P = 128
B, T, D = 8, 512, 256
KD = D // P
TT = T // P
NT = B * TT
LN_EPS = 1e-5
ONE = 1
DMA = 16


class Room:

    def __init__(self, nc, stack, phase):
        self.nc, self.stack, self.phase = nc, stack, phase
        self.sems = []
        stack.callback(self.clear)

    def block(self):
        nc = self.nc
        for n, sem in enumerate(self.sems):
            (nc.sync, nc.tensor, nc.scalar, nc.vector, nc.gpsimd)[n % 5].sem_inc(sem, ONE)
        self.nc.all_engine_barrier()
        return self.stack.enter_context(self.nc.Block())

    def clear(self):
        if self.sems:
            nc = self.nc
            for n, sem in enumerate(self.sems):
                (nc.sync, nc.tensor, nc.scalar, nc.vector, nc.gpsimd)[n % 5].sem_clear(sem)
            self.nc.all_engine_barrier()

    def sb(self, name, *shape):
        return self.stack.enter_context(self.nc.sbuf_tensor(f"{self.phase}_{name}", [P, *shape], F32))

    def ps(self, name, *shape):
        return self.stack.enter_context(self.nc.psum_tensor(f"{self.phase}_{name}", [P, *shape], F32))

    def sem(self, name):
        self.sems.append(self.stack.enter_context(self.nc.semaphore(f"{self.phase}_{name}")))
        return self.sems[-1]


def wait_apart(engine, always, sem, value):
    value = ONE + value
    if not isinstance(value, int):
        value = engine.to_reg(value)
    engine.wait_ge(always, 1)
    engine.wait_ge(sem, value)


class LayerNorm:

    def __init__(self, nc, room, name, keep, eps=None):
        self.nc, self.neg_half = nc, keep.neg_half
        self.eps = keep.eps if eps is None else eps
        self.always = keep.always
        self.stats = room.sb(f"{name}_stats", TT, 6)
        self.moments = room.sb(f"{name}_moments", TT, 2)
        self.var_eps = room.sb(f"{name}_var_eps", TT)
        self.rstd = room.sb(f"{name}_rstd", TT)
        self.stats_done = room.sem(f"{name}_stats_done")
        self.moments_done = room.sem(f"{name}_moments_done")
        self.eps_added = room.sem(f"{name}_eps_added")
        self.rstd_done = room.sem(f"{name}_rstd_done")

    def vector_moments(self, dve, x, count):
        for t in range(TT):
            last = self.nc.vector.bn_stats(self.stats[:, t, :], x(t))
        last.then_inc(self.stats_done, 1)
        wait_apart(dve, self.always, self.stats_done, count + 1)
        for t in range(TT):
            last = self.nc.vector.bn_aggr(self.moments[:, t, :], self.stats[:, t, :])
        last.then_inc(self.moments_done, 1)

    def pool_rstd(self, pool, count):
        pool.wait_ge(self.moments_done, ONE + count + 1)
        self.nc.gpsimd.tensor_tensor(self.var_eps[:], self.moments[:, :, 1], self.eps[:, 0:TT],
                                     ALU.add).then_inc(self.eps_added, 1)
        pool.wait_ge(self.eps_added, ONE + count + 1)
        self.nc.gpsimd.tensor_tensor(self.rstd[:], self.var_eps[:], self.neg_half[:, 0:TT],
                                     ALU.pow).then_inc(self.rstd_done, 1)

    def vector_apply(self, dve, x, out, count):
        dve.wait_ge(self.rstd_done, ONE + count + 1)
        for t in range(TT):
            last = self.nc.vector.tensor_scalar(out(t), x(t), self.moments[:, t, 0:1],
                                                self.rstd[:, t:t + 1], ALU.subtract, ALU.mult)
        return last

EXPERTS0, INTER0, TOP0, ROUTE_SCALE = 16, 128, 4, 2.5
RATIO_MAX = 1e24


def layer0_project(nc, io, keep):
    with ExitStack() as stack:
        room = Room(nc, stack, "p0")
        ident, x_res, xnT_all, comb, scan = (
            keep.ident, keep.x_res, keep.xnT_all, keep.comb, keep.scan)
        w_kvr = room.sb("w_kvr", KD, 3 * D)
        w_gate = room.sb("w_gate", KD, EXPERTS0)
        gate_b = room.sb("gate_b", EXPERTS0)
        w13s = room.sb("w13s", KD, 2 * INTER0)
        w2s = room.sb("w2s", D)
        cols = room.sb("cols", KD, 4)
        xn = room.sb("xn", TT, D)
        hn = room.sb("hn", TT, D)
        xnT = room.sb("xnT", KD, T)
        hT = room.sb("hT", KD, T + 1)
        k_sb = room.sb("k_sb", KD, T + 1)
        dk = room.sb("dk", KD, T)
        v_sb = room.sb("v_sb", KD, T)
        r_sb = room.sb("r_sb", KD, T)
        scores = room.sb("scores", TT, EXPERTS0)
        biased = room.sb("biased", TT, EXPERTS0)
        top = room.sb("top", TT, 8)
        picked = room.sb("picked", TT, EXPERTS0)
        picked_sum = room.sb("picked_sum", TT)
        picked_inv = room.sb("picked_inv", TT)
        silu_g = room.sb("silu_g", T)
        hidden = room.sb("hidden", T)
        ps_x = room.ps("ps_x", KD, T)
        ps_h = room.ps("ps_h", KD, T)
        ps_k = room.ps("ps_k", KD, T)
        ps_v = room.ps("ps_v", KD, T)
        ln_a = LayerNorm(nc, room, "ln_a", keep)
        ln_b = LayerNorm(nc, room, "ln_b", keep)
        weights_in, x_in = room.sem("weights_in"), room.sem("x_in")
        xn_saved, v_saved, r_saved = room.sem("xn_saved"), room.sem("v_saved"), room.sem("r_saved")
        setup_done = room.sem("setup_done")
        xn_ready, hn_ready = room.sem("xn_ready"), room.sem("hn_ready")
        xn_turned, hn_turned = room.sem("xn_turned"), room.sem("hn_turned")
        xnT_ready, xnT_kept, hT_ready = room.sem("xnT_ready"), room.sem("xnT_kept"), room.sem("hT_ready")
        projected = room.sem("projected")
        k_out, v_out, r_out = room.sem("k_out"), room.sem("v_out"), room.sem("r_out")
        gated, scores_ready, routed = room.sem("gated"), room.sem("scores_ready"), room.sem("routed")
        route_step = room.sem("route_step")
        dk_ready, decayed = room.sem("dk_ready"), room.sem("decayed")
        up_done, silu_ready = room.sem("up_done"), room.sem("silu_ready")
        hidden_ready, down_done, shared_added = room.sem("hidden_ready"), room.sem("down_done"), room.sem("shared_added")
        block = room.block()

        def x_tiles(i, t):
            return x_res[:, bass.ds(TT * i + t, 1), :].rearrange("p a d -> p (a d)")

        @block.sync
        def _(sp):
            n = 0
            for dst, src in ((w_kvr[:], io.l0_w_kvr),
                             (w_gate[:], io.l0_w_gate), (gate_b[:], io.l0_gate_b), (w13s[:], io.l0_w13s),
                             (w2s[:], io.l0_w2s), (cols[:], io.l0_cols)):
                sp.dma_start(dst, src).then_inc(weights_in, DMA)
                n += 1
            assert n == 6

            def load_x(i):
                sp.dma_start(x_res[:, bass.ds(TT * i, TT), :],
                             io.x[bass.ds(i, 1)].rearrange("a p t d -> p (a t) d")).then_inc(x_in, DMA)

            def save(i):
                sp.wait_ge(hn_ready, ONE + i + 1)
                sp.dma_start(io.xn_scratch[bass.ds(i, 1)].rearrange("a p t d -> p (a t) d"),
                             xn[:]).then_inc(xn_saved, DMA)
                sp.wait_ge(v_out, ONE + i + 1)
                sp.dma_start(io.v_scratch[bass.ds(i, 1)].rearrange("a p k t -> p (a k) t"),
                             v_sb[:]).then_inc(v_saved, DMA)
                sp.wait_ge(r_out, ONE + i + 1)
                sp.dma_start(io.r_scratch[bass.ds(i, 1)].rearrange("a p k t -> p (a k) t"),
                             r_sb[:]).then_inc(r_saved, DMA)

            load_x(0)
            with sp.Fori(0, B - 1) as i:
                sp.wait_ge(x_in, ONE + DMA * (i + 1))
                load_x(i + 1)
                save(i)
            save(B - 1)
            for done in (xn_saved, v_saved, r_saved):
                sp.wait_ge(done, ONE + DMA * B)

        @block.vector
        def _(dve):
            nc.vector.memset(k_sb[:, :, T:T + 1], 0.0).then_inc(setup_done, 1)
            nc.vector.memset(comb[:], 1.0).then_inc(setup_done, 1)
            dve.wait_ge(weights_in, ONE + 6 * DMA)
            nc.vector.tensor_copy(hT[:, :, 0:1], cols[:, :, 2:3]).then_inc(setup_done, 1)
            nc.vector.memset(scan[:, 0, 0, :], 0.0).then_inc(setup_done, 1)
            nc.vector.memset(scan[:, 1, 1, :], 1.0).then_inc(setup_done, 1)

            def norms(i):
                dve.wait_ge(x_in, ONE + DMA * (i + 1))
                ln_a.vector_moments(dve, lambda t: x_tiles(i, t), i)
                dve.wait_ge(xn_turned, ONE + i)
                dve.wait_ge(xn_saved, ONE + DMA * i)
                ln_a.vector_apply(dve, lambda t: x_tiles(i, t), lambda t: xn[:, t, :], i).then_inc(xn_ready, 1)
                dve.wait_ge(xn_ready, ONE + i + 1)
                ln_b.vector_moments(dve, lambda t: xn[:, t, :], i)
                dve.wait_ge(hn_turned, ONE + i)
                ln_b.vector_apply(dve, lambda t: xn[:, t, :], lambda t: hn[:, t, :], i).then_inc(hn_ready, 1)

            def rest(i):
                dve.wait_ge(xnT_ready, ONE + i + 1)
                nc.vector.tensor_copy(xnT_all[:, :, bass.ds(i * T, T)], ps_x[:]).then_inc(xnT_kept, 1)
                dve.wait_ge(scores_ready, ONE + i + 1)
                for t in range(TT):
                    last = nc.vector.tensor_tensor(biased[:, t, :], scores[:, t, :], gate_b[:], ALU.add)
                last.then_inc(route_step, 1)
                dve.wait_ge(route_step, ONE + 4 * i + 1)
                dve.wait_ge(k_out, ONE + i + 1)
                dve.wait_ge(decayed, ONE + i)
                nc.vector.tensor_tensor(dk[:], k_sb[:, :, 0:T], k_sb[:, :, 1:T + 1],
                                        ALU.subtract).then_inc(dk_ready, 1)
                for t in range(TT):
                    last = nc.vector.max(top[:, t, :], biased[:, t, :])
                last.then_inc(route_step, 1)
                dve.wait_ge(route_step, ONE + 4 * i + 2)
                for t in range(TT):
                    last = nc.vector.scalar_tensor_tensor(
                        out=picked[:, t, :], in0=biased[:, t, :], scalar=top[:, t, TOP0 - 1:TOP0],
                        in1=scores[:, t, :], op0=ALU.is_ge, op1=ALU.mult, accum_out=picked_sum[:, t:t + 1])
                last.then_inc(route_step, 1)
                dve.wait_ge(route_step, ONE + 4 * i + 3)
                nc.vector.reciprocal(picked_inv[:], picked_sum[:]).then_inc(route_step, 1)
                dve.wait_ge(route_step, ONE + 4 * i + 4)
                for t in range(TT):
                    last = nc.vector.tensor_scalar(
                        comb[:, bass.ds(TT * i + t, 1), 0:EXPERTS0].rearrange("p a e -> p (a e)"),
                        picked[:, t, :], picked_inv[:, t:t + 1], ROUTE_SCALE, ALU.mult, ALU.mult)
                last.then_inc(routed, 1)
                dve.wait_ge(silu_ready, ONE + i + 1)
                dve.wait_ge(down_done, ONE + i)
                nc.vector.tensor_tensor(hidden[:], silu_g[:], ps_k[:, 1, :], ALU.mult).then_inc(hidden_ready, 1)
                dve.wait_ge(down_done, ONE + i + 1)
                xb = x_res[:, bass.ds(TT * i, TT), :].rearrange("p a d -> p (a d)")
                nc.vector.tensor_tensor(xb, xb, ps_v[:].rearrange("p a d -> p (a d)"), ALU.add).then_inc(shared_added, 1)

            norms(0)
            with dve.Fori(0, B - 1) as i:
                norms(i + 1)
                rest(i)
            rest(B - 1)

        @block.gpsimd
        def _(pool):
            pool.wait_ge(weights_in, ONE + 6 * DMA)
            with pool.Fori(0, B) as i:
                ln_a.pool_rstd(pool, i)
                ln_b.pool_rstd(pool, i)

        @block.scalar
        def _(act):
            act.wait_ge(weights_in, ONE + 6 * DMA)
            act.wait_ge(setup_done, ONE + 5)
            with act.Fori(0, B) as i:
                act.wait_ge(xn_turned, ONE + i + 1)
                act.wait_ge(up_done, ONE + i)
                nc.scalar.copy(xnT[:], ps_x[:]).then_inc(xnT_ready, 1)
                act.wait_ge(hn_turned, ONE + i + 1)
                act.wait_ge(projected, ONE + 3 * i)
                for k in range(KD):
                    last = nc.scalar.activation(hT[:, k, 1:T + 1], ps_h[:, k, :], ACT.Identity,
                                                bias=cols[:, k, 1:2], scale=cols[:, k, 0:1])
                last.then_inc(hT_ready, 1)
                act.wait_ge(projected, ONE + 3 * i + 1)
                act.wait_ge(dk_ready, ONE + i)
                nc.scalar.copy(k_sb[:, :, 0:T], ps_k[:]).then_inc(k_out, 1)
                act.wait_ge(projected, ONE + 3 * i + 2)
                act.wait_ge(v_saved, ONE + DMA * i)
                nc.scalar.copy(v_sb[:], ps_v[:]).then_inc(v_out, 1)
                act.wait_ge(projected, ONE + 3 * i + 3)
                act.wait_ge(r_saved, ONE + DMA * i)
                nc.scalar.activation(r_sb[:], ps_h[:], ACT.Sigmoid).then_inc(r_out, 1)
                act.wait_ge(gated, ONE + i + 1)
                act.wait_ge(routed, ONE + i)
                nc.scalar.activation(scores[:], ps_x[:, 0, 0:TT * EXPERTS0].rearrange("p (t e) -> p t e", t=TT),
                                     ACT.Sigmoid).then_inc(scores_ready, 1)
                act.wait_ge(up_done, ONE + i + 1)
                act.wait_ge(hidden_ready, ONE + i)
                nc.scalar.activation(silu_g[:], ps_k[:, 0, :], ACT.Silu).then_inc(silu_ready, 1)
                act.wait_ge(dk_ready, ONE + i + 1)
                for k in range(KD):
                    last = nc.scalar.activation(
                        scan[:, 1:T + 1, 0, bass.ds(B * k + i, 1)].rearrange("p t a -> p (t a)"), dk[:, k, :],
                        ACT.Exp, bias=cols[:, k, 3:4])
                last.then_inc(decayed, 1)

        @block.tensor
        def _(pe):
            pe.wait_ge(weights_in, ONE + 6 * DMA)
            pe.wait_ge(setup_done, ONE + 5)
            with pe.Fori(0, B) as i:
                pe.wait_ge(xn_ready, ONE + i + 1)
                pe.wait_ge(scores_ready, ONE + i)
                for k in range(KD):
                    for t in range(TT):
                        last = nc.tensor.transpose(ps_x[:, k, t * P:(t + 1) * P], xn[:, t, k * P:(k + 1) * P], ident[:])
                last.then_inc(xn_turned, 1)
                pe.wait_ge(hn_ready, ONE + i + 1)
                pe.wait_ge(r_out, ONE + i)
                for k in range(KD):
                    for t in range(TT):
                        last = nc.tensor.transpose(ps_h[:, k, t * P:(t + 1) * P], hn[:, t, k * P:(k + 1) * P], ident[:])
                last.then_inc(hn_turned, 1)
                pe.wait_ge(hT_ready, ONE + i + 1)
                pe.wait_ge(silu_ready, ONE + i)
                pe.wait_ge(hidden_ready, ONE + i)
                for n, ps in enumerate((ps_k, ps_v, ps_h)):
                    if n == 1:
                        pe.wait_ge(shared_added, ONE + i)
                    for m in range(KD):
                        for k in range(KD):
                            last = nc.tensor.matmul(ps[:, m, :], w_kvr[:, k, n * D + m * P:n * D + (m + 1) * P],
                                                    hT[:, k, 0:T], start=(k == 0), stop=(k == KD - 1))
                    last.then_inc(projected, 1)
                pe.wait_ge(xnT_ready, ONE + i + 1)
                pe.wait_ge(xnT_kept, ONE + i + 1)
                for t in range(TT):
                    for k in range(KD):
                        last = nc.tensor.matmul(ps_x[:, 0, t * EXPERTS0:(t + 1) * EXPERTS0], xnT[:, k, t * P:(t + 1) * P],
                                                w_gate[:, k, :], start=(k == 0), stop=(k == KD - 1))
                last.then_inc(gated, 1)
                pe.wait_ge(k_out, ONE + i + 1)
                for m in range(2):
                    for k in range(KD):
                        last = nc.tensor.matmul(ps_k[:, m, :], w13s[:, k, m * INTER0:(m + 1) * INTER0], xnT[:, k, :],
                                                start=(k == 0), stop=(k == KD - 1))
                last.then_inc(up_done, 1)
                pe.wait_ge(hidden_ready, ONE + i + 1)
                pe.wait_ge(v_out, ONE + i + 1)
                for t in range(TT):
                    last = nc.tensor.matmul(ps_v[:].rearrange("p a b -> p (a b)")[:, t * D:(t + 1) * D],
                                            hidden[:, t * P:(t + 1) * P], w2s[:], start=True, stop=True)
                last.then_inc(down_done, 1)


def layer0_experts(nc, io, keep):
    UNIT_STEPS = T // (EXPERTS0 * B)
    with ExitStack() as stack:
        room = Room(nc, stack, "p1")
        x_res, xnT_all, comb, scan = keep.x_res, keep.xnT_all, keep.comb, keep.scan
        w13 = [room.sb(f"w13_{n}", KD, 2 * INTER0) for n in range(2)]
        w2 = [room.sb(f"w2_{n}", D) for n in range(2)]
        silu_g = [room.sb(f"silu_g{n}", T) for n in range(2)]
        hidden = [room.sb(f"hidden{n}", T) for n in range(2)]
        new = room.sb("new", 2, KD * B)
        ratio = room.sb("ratio", KD * B)
        ps_gu = [room.ps(f"ps_gu{n}", 2, T) for n in range(2)]
        ps_y = [room.ps(f"ps_y{n}", TT, D) for n in range(2)]
        weights_in = [room.sem(f"weights_in{n}") for n in range(2)]
        up_done, silu_ready = room.sem("up_done"), room.sem("silu_ready")
        gu_free, y_free = room.sem("gu_free"), room.sem("y_free")
        down_done = room.sem("down_done")
        step = room.sem("step")
        block = room.block()

        @block.sync
        def _(sp):
            def load(e, n):
                sp.dma_start(w13[n][:], io.l0_w13[bass.ds(e, 1)].rearrange("e p k n -> p (e k) n")).then_inc(weights_in[n], DMA)
                sp.dma_start(w2[n][:], io.l0_w2[bass.ds(e, 1)].rearrange("e p d -> p (e d)")).then_inc(weights_in[n], DMA)

            load(0, 0)
            load(1, 1)
            with sp.Fori(0, EXPERTS0 // 2 - 1) as j:
                for n in range(2):
                    sp.wait_ge(down_done, ONE + B * (2 * j + n + 1) + 2)
                    load(2 * j + 2 + n, n)

        @block.vector
        def _(dve):
            dve.sem_inc(gu_free, 2)
            dve.sem_inc(y_free, 2)

            def recurrence(t):
                nc.vector.scalar_tensor_tensor(
                    out=new[:], in0=scan[:, bass.ds(t, 1), 0, :].broadcast_to([P, 2, KD * B]), scalar=1.0,
                    in1=scan[:, bass.ds(t + 1, 1), :, :].rearrange("p a s c -> p (a s) c"),
                    op0=ALU.add, op1=ALU.mult).then_inc(step, 1)

            def recurrence_close(t):
                dve.wait_ge(step, ONE + 4 * t + 1)
                nc.vector.tensor_scalar(ratio[:], new[:, 0, :], 1.0, RATIO_MAX, ALU.max, ALU.min).then_inc(step, 1)
                nc.vector.scalar_tensor_tensor(
                    out=scan[:, bass.ds(t + 1, 1), 0, :].rearrange("p a c -> p (a c)"), in0=new[:, 0, :],
                    scalar=RATIO_MAX, in1=new[:, 1, :], op0=ALU.min, op1=ALU.mult).then_inc(step, 1)

            def recurrence_invert(t):
                dve.wait_ge(step, ONE + 4 * t + 3)
                nc.vector.reciprocal(scan[:, bass.ds(t + 2, 1), 1, :].rearrange("p a c -> p (a c)"),
                                     ratio[:]).then_inc(step, 1)

            def combine(m, t, e):
                xb = x_res[:, TT * (m % B) + t, :]
                return nc.vector.scalar_tensor_tensor(
                    out=xb, in0=ps_y[m % 2][:, t, :],
                    scalar=comb[:, TT * (m % B) + t, bass.ds(e, 1)],
                    in1=xb, op0=ALU.mult, op1=ALU.add)

            with dve.Fori(0, EXPERTS0 // 2) as j:
                for m in range(2 * B):
                    u = 2 * B * j + m
                    for s in range(UNIT_STEPS):
                        t = UNIT_STEPS * u + s
                        recurrence(t)
                        if m:
                            if s == 0:
                                dve.wait_ge(down_done, ONE + u + 2)
                            last = combine(m - 1, s, 2 * j + (m - 1) // B)
                            if s == UNIT_STEPS - 1:
                                last.then_inc(y_free, 1)
                        recurrence_close(t)
                        if s == 0:
                            dve.wait_ge(silu_ready, ONE + u + 1)
                            dve.wait_ge(down_done, ONE + u + 1)
                        cut = slice(s * P, (s + 1) * P)
                        last = nc.vector.tensor_tensor(hidden[m % 2][:, cut], silu_g[m % 2][:, cut],
                                                       ps_gu[m % 2][:, 1, cut], ALU.mult)
                        if s == UNIT_STEPS - 1:
                            last.then_inc(gu_free, 1)
                        recurrence_invert(t)
                        dve.wait_ge(step, ONE + 4 * t + 4)
                m = 2 * B - 1
                dve.wait_ge(down_done, ONE + 2 * B * j + m + 3)
                for t in range(TT):
                    last = combine(m, t, 2 * j + 1)
                last.then_inc(y_free, 1)

        @block.scalar
        def _(act):
            with act.Fori(0, EXPERTS0 // 2) as j:
                for m in range(2 * B):
                    u = 2 * B * j + m
                    act.wait_ge(up_done, ONE + u + 1)
                    act.wait_ge(gu_free, ONE + u + 1)
                    nc.scalar.activation(silu_g[m % 2][:], ps_gu[m % 2][:, 0, :], ACT.Silu).then_inc(silu_ready, 1)

        @block.tensor
        def _(pe):
            pe.sem_inc(down_done, 2)

            def up(j, m, n):
                pe.wait_ge(gu_free, ONE + 2 * B * j + m + 1)
                for half in range(2):
                    for k in range(KD):
                        last = nc.tensor.matmul(ps_gu[m % 2][:, half, :], w13[n][:, k, half * INTER0:(half + 1) * INTER0],
                                                xnT_all[:, k, (m % B) * T:(m % B + 1) * T],
                                                start=(k == 0), stop=(k == KD - 1))
                last.then_inc(up_done, 1)

            def down(j, m, n):
                pe.wait_ge(gu_free, ONE + 2 * B * j + m + 3)
                pe.wait_ge(y_free, ONE + 2 * B * j + m + 1)
                for t in range(TT):
                    last = nc.tensor.matmul(ps_y[m % 2][:, t, :], hidden[m % 2][:, t * P:(t + 1) * P], w2[n][:],
                                            start=True, stop=True)
                last.then_inc(down_done, 1)

            with pe.Fori(0, EXPERTS0 // 2) as j:
                for m in range(2 * B):
                    if m % B == 0:
                        pe.wait_ge(weights_in[m // B], ONE + 2 * DMA * (j + 1))
                    up(j, m, m // B)
                    if m:
                        down(j, m - 1, (m - 1) // B)
                down(j, 2 * B - 1, 1)


def layer0_mix(nc, io, keep):
    FF = 4 * D
    NF = FF // P
    with ExitStack() as stack:
        room = Room(nc, stack, "p2")
        ident, x_res, scan = keep.ident, keep.x_res, keep.scan
        w_ck = room.sb("w_ck", KD, FF)
        w_cv = room.sb("w_cv", NF, D)
        w_cr = room.sb("w_cr", KD, D)
        cols = room.sb("cols", KD, 4)
        bonus = room.sb("bonus", KD)
        ones = room.sb("ones", 1)
        v_sb = room.sb("v_sb", KD, T)
        r_sb = room.sb("r_sb", KD, T)
        xn = room.sb("xn", TT, D)
        inv = room.sb("inv", KD, T)
        den = room.sb("den", KD, T)
        total = room.sb("total", KD, T + 1)
        y = room.sb("y", KD, T)
        x1 = room.sb("x1", TT, D)
        hn = room.sb("hn", TT, D)
        hT = room.sb("hT", KD, T + 1)
        kk = room.sb("kk", NF, T)
        rr = room.sb("rr", TT, D)
        mixed = room.sb("mixed", TT, D)
        ps_t = room.ps("ps_t", 2 * T)
        ps_kk = [room.ps(f"ps_kk{n}", T) for n in range(2)]
        ps_rr = room.ps("ps_rr", TT, D)
        ps_kv = room.ps("ps_kv", TT, D)
        ln = LayerNorm(nc, room, "ln", keep)
        weights_in, setup_done = room.sem("weights_in"), room.sem("setup_done")
        v_in, r_in, xn_in = room.sem("v_in"), room.sem("r_in"), room.sem("xn_in")
        q_read = room.sem("q_read")
        chain = room.sem("chain")
        y_ready, y_turned, x1_ready = room.sem("y_ready"), room.sem("y_turned"), room.sem("x1_ready")
        hn_ready, hn_turned, hT_ready = room.sem("hn_ready"), room.sem("hn_turned"), room.sem("hT_ready")
        kk_done, kk_relu, kk_ready = room.sem("kk_done"), room.sem("kk_relu"), room.sem("kk_ready")
        rr_done, rr_ready, kv_done = room.sem("rr_done"), room.sem("rr_ready"), room.sem("kv_done")
        mix_step, batch_done = room.sem("mix_step"), room.sem("batch_done")
        CHAIN = 6
        block = room.block()

        def q_at(i, k, first):
            return scan[:, first:first + T, 0, bass.ds(B * k + i, 1)].rearrange("p t a -> p (t a)")

        @block.sync
        def _(sp):
            for dst, src in ((w_ck[:], io.l0_w_ck), (w_cv[:], io.l0_w_cv), (w_cr[:], io.l0_w_cr), (cols[:], io.l0_cols2)):
                sp.dma_start(dst, src).then_inc(weights_in, DMA)
            with sp.Fori(0, B) as i:
                sp.wait_ge(y_ready, ONE + i)
                sp.dma_start(v_sb[:], io.v_scratch[bass.ds(i, 1)].rearrange("a p k t -> p (a k) t")).then_inc(v_in, DMA)
                sp.dma_start(r_sb[:], io.r_scratch[bass.ds(i, 1)].rearrange("a p k t -> p (a k) t")).then_inc(r_in, DMA)
                sp.wait_ge(x1_ready, ONE + i)
                sp.dma_start(xn[:], io.xn_scratch[bass.ds(i, 1)].rearrange("a p t d -> p (a t) d")).then_inc(xn_in, DMA)

        @block.gpsimd
        def _(pool):
            pool.wait_ge(setup_done, ONE + 4)
            with pool.Fori(0, B) as i:
                pool.wait_ge(y_ready, ONE + i)
                for k in range(KD):
                    nc.gpsimd.tensor_tensor(inv[:, k, :], q_at(i, k, 0), ones[:, 0:1].broadcast_to([P, T]), ALU.add)
                    last = nc.gpsimd.tensor_tensor(den[:, k, :], q_at(i, k, 0),
                                                   bonus[:, k:k + 1].broadcast_to([P, T]), ALU.add)
                last.then_inc(q_read, 1)
                ln.pool_rstd(pool, i)
                for n in range(NF):
                    pool.wait_ge(kk_relu, ONE + NF * i + n + 1)
                    nc.gpsimd.tensor_tensor(kk[:, n, :], kk[:, n, :], kk[:, n, :], ALU.mult).then_inc(kk_ready, 1)

        @block.vector
        def _(dve):
            dve.wait_ge(weights_in, ONE + 4 * DMA)
            nc.vector.tensor_copy(hT[:, :, 0:1], cols[:, :, 2:3]).then_inc(setup_done, 1)
            nc.vector.memset(total[:, :, 0:1], 0.0).then_inc(setup_done, 1)
            nc.vector.memset(ones[:], 1.0).then_inc(setup_done, 1)

            def values(i):
                dve.wait_ge(q_read, ONE + i + 1)
                dve.wait_ge(v_in, ONE + DMA * (i + 1))
                nc.vector.reciprocal(inv[:], inv[:]).then_inc(chain, 1)
                dve.wait_ge(chain, ONE + CHAIN * i + 1)
                for k in range(KD):
                    last = nc.vector.tensor_tensor(inv[:, k, :], inv[:, k, :], q_at(i, k, 1), ALU.mult)
                last.then_inc(chain, 1)
                nc.vector.reciprocal(den[:], den[:]).then_inc(chain, 1)
                dve.wait_ge(chain, ONE + CHAIN * i + 2)
                for k in range(KD):
                    last = nc.vector.tensor_tensor_scan(total[:, k, 1:T + 1], v_sb[:, k, :], inv[:, k, :], 0.0,
                                                        ALU.add, ALU.mult)
                last.then_inc(chain, 1)
                dve.wait_ge(chain, ONE + CHAIN * i + 4)
                dve.wait_ge(y_turned, ONE + i)
                for k in range(KD):
                    last = nc.vector.scalar_tensor_tensor(out=y[:, k, :], in0=v_sb[:, k, :], scalar=bonus[:, k:k + 1],
                                                          in1=total[:, k, 0:T], op0=ALU.mult, op1=ALU.add)
                last.then_inc(chain, 1)
                dve.wait_ge(chain, ONE + CHAIN * i + 5)
                nc.vector.tensor_tensor(y[:], y[:], den[:], ALU.mult).then_inc(chain, 1)
                dve.wait_ge(chain, ONE + CHAIN * i + 6)
                dve.wait_ge(r_in, ONE + DMA * (i + 1))
                nc.vector.tensor_tensor(y[:], y[:], r_sb[:], ALU.mult).then_inc(y_ready, 1)

            def rest(i):
                dve.wait_ge(y_turned, ONE + i + 1)
                dve.wait_ge(xn_in, ONE + DMA * (i + 1))
                dve.wait_ge(batch_done, ONE + i)
                nc.vector.tensor_tensor(x1[:].rearrange("p a d -> p (a d)"), ps_t[:],
                                        xn[:].rearrange("p a d -> p (a d)"), ALU.add).then_inc(x1_ready, 1)
                dve.wait_ge(x1_ready, ONE + i + 1)
                ln.vector_moments(dve, lambda t: x1[:, t, :], i)
                dve.wait_ge(hn_turned, ONE + i)
                ln.vector_apply(dve, lambda t: x1[:, t, :], lambda t: hn[:, t, :], i).then_inc(hn_ready, 1)

            def finish(i):
                dve.wait_ge(rr_ready, ONE + i + 1)
                dve.wait_ge(kv_done, ONE + i + 1)
                xb = x_res[:, bass.ds(TT * i, TT), :]
                nc.vector.tensor_tensor(mixed[:], ps_kv[:], rr[:], ALU.mult).then_inc(mix_step, 1)
                nc.vector.tensor_tensor(xb, xb, x1[:], ALU.add).then_inc(mix_step, 1)
                dve.wait_ge(mix_step, ONE + 2 * i + 2)
                nc.vector.tensor_tensor(xb, xb, mixed[:], ALU.add).then_inc(batch_done, 1)

            dve.wait_ge(setup_done, ONE + 4)
            values(0)
            with dve.Fori(0, B - 1) as i:
                rest(i)
                values(i + 1)
                finish(i)
            rest(B - 1)
            finish(B - 1)

        @block.scalar
        def _(act):
            act.wait_ge(weights_in, ONE + 4 * DMA)
            nc.scalar.activation(bonus[:], cols[:, :, 3], ACT.Exp).then_inc(setup_done, 1)
            with act.Fori(0, B) as i:
                act.wait_ge(hn_turned, ONE + i + 1)
                act.wait_ge(rr_done, ONE + i)
                for k in range(KD):
                    last = nc.scalar.activation(hT[:, k, 1:T + 1], ps_t[:, k * T:(k + 1) * T], ACT.Identity,
                                                bias=cols[:, k, 1:2], scale=cols[:, k, 0:1])
                last.then_inc(hT_ready, 1)
                for n in range(NF):
                    act.wait_ge(kk_done, ONE + NF * i + n + 1)
                    if n == 0:
                        act.wait_ge(kv_done, ONE + i)
                    nc.scalar.activation(kk[:, n, :], ps_kk[n % 2][:], ACT.Relu).then_inc(kk_relu, 1)
                act.wait_ge(rr_done, ONE + i + 1)
                act.wait_ge(batch_done, ONE + i)
                nc.scalar.activation(rr[:], ps_rr[:], ACT.Sigmoid).then_inc(rr_ready, 1)

        @block.tensor
        def _(pe):
            pe.wait_ge(weights_in, ONE + 4 * DMA)
            pe.wait_ge(setup_done, ONE + 4)
            with pe.Fori(0, B) as i:
                pe.wait_ge(y_ready, ONE + i + 1)
                pe.wait_ge(hT_ready, ONE + i)
                for t in range(TT):
                    for k in range(KD):
                        last = nc.tensor.transpose(ps_t[:, t * D + k * P:t * D + (k + 1) * P],
                                                   y[:, k, t * P:(t + 1) * P], ident[:])
                last.then_inc(y_turned, 1)
                pe.wait_ge(hn_ready, ONE + i + 1)
                for k in range(KD):
                    for t in range(TT):
                        last = nc.tensor.transpose(ps_t[:, k * T + t * P:k * T + (t + 1) * P],
                                                   hn[:, t, k * P:(k + 1) * P], ident[:])
                last.then_inc(hn_turned, 1)
                pe.wait_ge(hT_ready, ONE + i + 1)
                for n in range(NF):
                    if n >= 2:
                        pe.wait_ge(kk_relu, ONE + NF * i + n - 1)
                    for k in range(KD):
                        last = nc.tensor.matmul(ps_kk[n % 2][:], w_ck[:, k, n * P:(n + 1) * P], hT[:, k, 0:T],
                                                start=(k == 0), stop=(k == KD - 1))
                    last.then_inc(kk_done, 1)
                pe.wait_ge(rr_ready, ONE + i)
                for t in range(TT):
                    for k in range(KD):
                        last = nc.tensor.matmul(ps_rr[:, t, :], hT[:, k, t * P:(t + 1) * P], w_cr[:, k, :],
                                                start=(k == 0), stop=(k == KD - 1))
                last.then_inc(rr_done, 1)
                pe.wait_ge(kk_ready, ONE + NF * (i + 1))
                pe.wait_ge(batch_done, ONE + i)
                for t in range(TT):
                    for n in range(NF):
                        last = nc.tensor.matmul(ps_kv[:, t, :], kk[:, n, t * P:(t + 1) * P], w_cv[:, n, :],
                                                start=(n == 0), stop=(n == NF - 1))
                last.then_inc(kv_done, 1)

HEADS, HD = 16, 16
PER_BLOCK = P // HD
SLOT = 32
GROUP = P // SLOT
SCORE_AT = (0, 512, 1024, 896)
SCORE_LEN = T + 3 * P + 2 * P + P


def causal_scores(nc, ps, key, query, wait_free, signal):
    for bank, tiles in enumerate(((0,), (1, 3), (2,))):
        wait_free(bank)
        for s in tiles:
            at = SCORE_AT[s] - 512 * bank
            last = nc.tensor.matmul(ps[:, bank, at:at + T - s * P], key[:, s * P:(s + 1) * P],
                                    query[:, s * P:T], start=True, stop=True)
        signal(last)


def values_sum(nc, ps, probs, v, h):
    j = h % GROUP
    for s in range(TT):
        last = nc.tensor.matmul(ps[SLOT * j:SLOT * (j + 1), s * P:T], v[:, s, h, :],
                                probs[:, SCORE_AT[s]:SCORE_AT[s] + T - s * P],
                                start=(s == 0), stop=(s == TT - 1))
    return last


def layer1(nc, io, keep):
    with ExitStack() as stack:
        room = Room(nc, stack, "a1")
        ident, x_res = keep.ident, keep.x_res
        w_qkv = room.sb("w_qkv", KD, 3 * D)
        w_o = room.sb("w_o", KD, D)
        weight = room.sb("weight", KD, D)
        w_eff = room.sb("w_eff", KD, D)
        bias = room.sb("bias", D)
        consts = room.sb("consts", 3)
        head_mask = room.sb("head_mask", PER_BLOCK)
        causal = room.sb("causal", P)
        ones = room.sb("ones", P)
        eps = room.sb("eps", TT * 2 * HEADS)
        gain = room.sb("gain", 1 + PER_BLOCK)
        shift = room.sb("shift", 1 + PER_BLOCK)
        abs_w = room.sb("abs_w", KD * D)
        abs_sum = room.sb("abs_sum", 1)
        limit = room.sb("limit", 2)
        ternary = room.sb("ternary", 2, KD * D)
        xn = room.sb("xn", TT, D)
        xnT = room.sb("xnT", KD, T)
        sums = room.sb("sums", TT, 2 * HEADS)
        centred = room.sb("centred", TT, 2 * D)
        squares = room.sb("squares", TT, 2 * D)
        spread = room.sb("spread", TT * 2 * HEADS)
        rstd = room.sb("rstd", TT * 2 * HEADS)
        qT = room.sb("qT", KD, T)
        kT = room.sb("kT", HEADS, T)
        v_sb = room.sb("v_sb", TT, HEADS, SLOT)
        probs = [room.sb(f"probs{n}", SCORE_LEN) for n in range(2)]
        yT = room.sb("yT", HEADS // GROUP, T)
        den = room.sb("den", TT, HEADS)
        y = room.sb("y", TT, D)
        ynT = room.sb("ynT", KD, T)
        ps_a = room.ps("ps_a", 2, T)
        ps_s = room.ps("ps_s", 3, T)
        ps_y = room.ps("ps_y", 2, T)
        ln = LayerNorm(nc, room, "ln", keep)
        weights_in, setup = room.sem("weights_in"), room.sem("setup")
        abs_done, abs_summed, limit_done = room.sem("abs_done"), room.sem("abs_summed"), room.sem("limit_done")
        xn_ready, xn_turned, xnT_ready = room.sem("xn_ready"), room.sem("xn_turned"), room.sem("xnT_ready")
        qk_done, v_done, v_ready = room.sem("qk_done"), room.sem("v_done"), room.sem("v_ready")
        qk_sum, qk_centred = room.sem("qk_sum"), room.sem("qk_centred")
        squared, spread_done, spread_eps, rstd_done = (room.sem("squared"), room.sem("spread_done"),
                                                       room.sem("spread_eps"), room.sem("rstd_done"))
        qk_ready, q_turned, k_turned = room.sem("qk_ready"), room.sem("q_turned"), room.sem("k_turned")
        qT_ready = room.sem("qT_ready")
        k0_ready, k1_ready = room.sem("k0_ready"), room.sem("k1_ready")
        scored, score_squared, masked = room.sem("scored"), room.sem("score_squared"), room.sem("masked")
        head_done, group_out = room.sem("head_done"), room.sem("group_out")
        y_back, den_step, y_ready = room.sem("y_back"), room.sem("den_step"), room.sem("y_ready")
        y_turned, ynT_ready = room.sem("y_turned"), room.sem("ynT_ready")
        out_done, bias_added, x_added = room.sem("out_done"), room.sem("bias_added"), room.sem("x_added")
        block = room.block()
        SETUP = 8

        @block.sync
        def _(sp):
            n = 0
            for dst, src in ((w_qkv[:], io.l1_w_qkv), (w_o[:], io.l1_w_o), (weight[:], io.l1_weight),
                             (bias[:], io.l1_bias), (consts[:], io.l1_consts), (head_mask[:], io.head_mask),
                             (causal[:], io.causal)):
                sp.dma_start(dst, src).then_inc(weights_in, DMA)
                n += 1
            assert n == 7

        @block.gpsimd
        def _(pool):
            pool.wait_ge(weights_in, ONE + 7 * DMA)
            with pool.Fori(0, B) as i:
                ln.pool_rstd(pool, i)
                pool.wait_ge(spread_done, ONE + i + 1)
                nc.gpsimd.tensor_tensor(spread[:], spread[:], eps[:], ALU.add).then_inc(spread_eps, 1)
                pool.wait_ge(spread_eps, ONE + i + 1)
                nc.gpsimd.tensor_tensor(rstd[:], spread[:], keep.neg_half[:, 0:TT * 2 * HEADS],
                                        ALU.pow).then_inc(rstd_done, 1)
                xb = x_res[:, bass.ds(TT * i, TT), :]
                pool.wait_ge(xn_ready, ONE + i + 1)
                nc.gpsimd.tensor_tensor(xb, xb, bias[:].rearrange("p (a d) -> p a d", a=1).broadcast_to([P, TT, D]),
                                        ALU.add).then_inc(bias_added, 1)
                for h in range(HEADS):
                    pool.wait_ge(score_squared, ONE + 3 * (HEADS * i + h + 1))
                    pr = probs[h % 2]
                    lead = pr[:, 0:SCORE_LEN].rearrange("p (a c) -> p a c", c=256)[:, 0:5:2, 0:P]
                    nc.gpsimd.tensor_tensor(lead, lead, causal[:].rearrange("p (a c) -> p a c", a=1).broadcast_to([P, 3, P]),
                                            ALU.mult)
                    nc.gpsimd.tensor_tensor(pr[:, 896:1024], pr[:, 896:1024], causal[:], ALU.mult).then_inc(masked, 1)

        @block.vector
        def _(dve):
            nc.vector.memset(ones[:], 1.0).then_inc(setup, 1)
            nc.vector.memset(eps[:], HD * LN_EPS).then_inc(setup, 1)
            nc.vector.memset(v_sb[:], 0.0).then_inc(setup, 1)
            dve.wait_ge(setup, ONE + 3)
            nc.vector.memset(v_sb[:, :, :, HD:HD + 1], 1.0).then_inc(setup, 1)
            dve.wait_ge(weights_in, ONE + 7 * DMA)
            nc.vector.tensor_scalar(gain[:, 0:1], consts[:, 0:1], HD ** 0.5, None, ALU.mult).then_inc(setup, 1)
            nc.vector.tensor_scalar(gain[:, 1:], head_mask[:], consts[:, 0:1], HD ** 0.5, ALU.mult, ALU.mult).then_inc(setup, 1)
            nc.vector.tensor_copy(shift[:, 0:1], consts[:, 1:2]).then_inc(setup, 1)
            nc.vector.tensor_scalar(shift[:, 1:], head_mask[:], consts[:, 1:2], None, ALU.mult).then_inc(setup, 1)
            dve.wait_ge(abs_summed, ONE + 1)
            nc.vector.tensor_scalar(limit[:, 0:1], ps_a[:, 0, 0:1], 0.7 / (D * D), None, ALU.mult).then_inc(limit_done, 1)
            nc.vector.tensor_scalar(limit[:, 1:2], ps_a[:, 0, 0:1], -0.7 / (D * D), None, ALU.mult).then_inc(limit_done, 1)
            dve.wait_ge(limit_done, ONE + 2)
            w_row = weight[:].rearrange("p k d -> p (k d)")
            nc.vector.tensor_scalar(ternary[:, 0, :], w_row, limit[:, 0:1], consts[:, 2:3], ALU.is_gt, ALU.mult).then_inc(limit_done, 1)
            nc.vector.tensor_scalar(ternary[:, 1, :], w_row, limit[:, 1:2], consts[:, 2:3], ALU.is_lt, ALU.mult).then_inc(limit_done, 1)
            dve.wait_ge(limit_done, ONE + 4)
            nc.vector.tensor_tensor(w_eff[:].rearrange("p k d -> p (k d)"), ternary[:, 0, :], ternary[:, 1, :],
                                    ALU.subtract).then_inc(limit_done, 1)

            def norms(i):
                def x_tile(t):
                    return x_res[:, bass.ds(TT * i + t, 1), :].rearrange("p a d -> p (a d)")
                ln.vector_moments(dve, x_tile, i)
                dve.wait_ge(xn_turned, ONE + i)
                ln.vector_apply(dve, x_tile, lambda t: xn[:, t, :], i).then_inc(xn_ready, 1)

            def head_norms(i):
                for t in range(TT):
                    dve.wait_ge(qk_done, ONE + TT * i + t + 1)
                    qk = ps_s[:, t % 2, :].rearrange("p (h c) -> p h c", c=HD)
                    nc.vector.tensor_reduce(sums[:, t, :], qk, AX.X, ALU.add).then_inc(qk_sum, 1)
                    dve.wait_ge(qk_sum, ONE + TT * i + t + 1)
                    if t == 0:
                        dve.wait_ge(k_turned, ONE + i)
                        dve.wait_ge(squared, ONE + i)
                    nc.vector.scalar_tensor_tensor(
                        out=centred[:, t, :].rearrange("p (h c) -> p h c", c=HD),
                        in0=sums[:, t, :].rearrange("p (h a) -> p h a", a=1).broadcast_to([P, 2 * HEADS, HD]),
                        scalar=-1.0 / HD, in1=qk, op0=ALU.mult, op1=ALU.add).then_inc(qk_centred, 1)
                dve.wait_ge(squared, ONE + i + 1)
                nc.vector.tensor_reduce(spread[:], squares[:].rearrange("p t (h c) -> p (t h) c", c=HD),
                                        AX.X, ALU.add).then_inc(spread_done, 1)
                dve.wait_ge(rstd_done, ONE + i + 1)
                rows = centred[:].rearrange("p t (h c) -> p (t h) c", c=HD)
                nc.vector.tensor_tensor(rows, rows, rstd[:].rearrange("p (h a) -> p h a", a=1)
                                        .broadcast_to([P, TT * 2 * HEADS, HD]), ALU.mult).then_inc(qk_ready, 1)

            def late_keys(i):
                dve.wait_ge(k_turned, ONE + i + 1)
                dve.wait_ge(scored, ONE + 3 * HEADS * i)
                for h in range(PER_BLOCK, HEADS):
                    m = 1 + h - PER_BLOCK
                    nc.vector.tensor_scalar(kT[:, h, :], ps_a[:, 1, :], gain[:, m:m + 1], shift[:, m:m + 1],
                                            ALU.mult, ALU.add).then_inc(k1_ready, 1)

            def finish(i):
                for t in range(TT):
                    dve.wait_ge(y_back, ONE + TT * i + t + 1)
                    sums_t = ps_a[:, t % 2, :].rearrange("p (h c) -> p h c", c=SLOT)
                    nc.vector.tensor_scalar(den[:, t, :], sums_t[:, :, HD], LN_EPS, None, ALU.add).then_inc(den_step, 1)
                    dve.wait_ge(den_step, ONE + 2 * (TT * i + t) + 1)
                    nc.vector.reciprocal(den[:, t, :], den[:, t, :]).then_inc(den_step, 1)
                    dve.wait_ge(den_step, ONE + 2 * (TT * i + t) + 2)
                    nc.vector.tensor_tensor(y[:, t, :].rearrange("p (h c) -> p h c", c=HD), sums_t[:, :, 0:HD],
                                            den[:, t, :].rearrange("p (h a) -> p h a", a=1).broadcast_to([P, HEADS, HD]),
                                            ALU.mult).then_inc(y_ready, 1)
                dve.wait_ge(out_done, ONE + i + 1)
                dve.wait_ge(bias_added, ONE + i + 1)
                xb = x_res[:, bass.ds(TT * i, TT), :].rearrange("p a d -> p (a d)")
                nc.vector.tensor_tensor(xb, xb, ps_a[:].rearrange("p a d -> p (a d)"), ALU.add).then_inc(x_added, 1)

            norms(0)
            with dve.Fori(0, B - 1) as i:
                head_norms(i)
                late_keys(i)
                norms(i + 1)
                finish(i)
            head_norms(B - 1)
            late_keys(B - 1)
            finish(B - 1)

        @block.scalar
        def _(act):
            act.wait_ge(weights_in, ONE + 7 * DMA)
            nc.scalar.activation(abs_w[:], weight[:].rearrange("p k d -> p (k d)"), ACT.Abs,
                                 accum_out=abs_sum[:]).then_inc(abs_done, 1)
            act.wait_ge(setup, ONE + SETUP)
            with act.Fori(0, B) as i:
                act.wait_ge(xn_turned, ONE + i + 1)
                nc.scalar.copy(xnT[:], ps_a[:]).then_inc(xnT_ready, 1)
                for t in range(TT):
                    act.wait_ge(v_done, ONE + TT * i + t + 1)
                    nc.scalar.copy(v_sb[:, t, :, 0:HD], ps_s[:, 2, 0:D].rearrange("p (h c) -> p h c", c=HD)).then_inc(v_ready, 1)
                act.wait_ge(qk_centred, ONE + TT * (i + 1))
                nc.scalar.activation(squares[:], centred[:], ACT.Square).then_inc(squared, 1)
                act.wait_ge(q_turned, ONE + i + 1)
                nc.scalar.activation(qT[:], ps_y[:], ACT.Identity, bias=shift[:, 0:1], scale=gain[:, 0:1]).then_inc(qT_ready, 1)
                act.wait_ge(k_turned, ONE + i + 1)
                for h in range(PER_BLOCK):
                    nc.scalar.activation(kT[:, h, :], ps_a[:, 0, :], ACT.Identity, bias=shift[:, 1 + h:2 + h],
                                         scale=gain[:, 1 + h:2 + h]).then_inc(k0_ready, 1)
                for h in range(HEADS):
                    if h >= 2:
                        act.wait_ge(head_done, ONE + HEADS * i + h - 1)
                    pr = probs[h % 2]
                    for bank, width in enumerate((T, T, 2 * P)):
                        act.wait_ge(scored, ONE + 3 * (HEADS * i + h) + bank + 1)
                        nc.scalar.activation(pr[:, 512 * bank:512 * bank + width], ps_s[:, bank, 0:width],
                                             ACT.Square, scale=HD ** -0.5).then_inc(score_squared, 1)
                    if h % GROUP == 0 and h:
                        act.wait_ge(head_done, ONE + HEADS * i + h)
                        g = h // GROUP - 1
                        nc.scalar.copy(yT[:, g, :], ps_y[:, g % 2, :]).then_inc(group_out, 1)
                act.wait_ge(head_done, ONE + HEADS * (i + 1))
                g = HEADS // GROUP - 1
                nc.scalar.copy(yT[:, g, :], ps_y[:, g % 2, :]).then_inc(group_out, 1)
                act.wait_ge(y_turned, ONE + i + 1)
                nc.scalar.copy(ynT[:], ps_s[:, 0:2, :]).then_inc(ynT_ready, 1)

        @block.tensor
        def _(pe):
            G = HEADS // GROUP
            pe.wait_ge(abs_done, ONE + 1)
            pe.wait_ge(setup, ONE + SETUP)
            nc.tensor.matmul(ps_a[:, 0, 0:1], ones[:], abs_sum[:], start=True, stop=True).then_inc(abs_summed, 1)
            pe.wait_ge(limit_done, ONE + 5)
            with pe.Fori(0, B) as i:
                pe.wait_ge(xn_ready, ONE + i + 1)
                pe.wait_ge(x_added, ONE + i)
                for k in range(KD):
                    for t in range(TT):
                        last = nc.tensor.transpose(ps_a[:, k, t * P:(t + 1) * P], xn[:, t, k * P:(k + 1) * P], ident[:])
                last.then_inc(xn_turned, 1)
                pe.wait_ge(xnT_ready, ONE + i + 1)
                pe.wait_ge(ynT_ready, ONE + i)
                for t in range(TT):
                    if t >= 2:
                        pe.wait_ge(qk_centred, ONE + TT * i + t - 1)
                    for k in range(KD):
                        last = nc.tensor.matmul(ps_s[:, t % 2, :], xnT[:, k, t * P:(t + 1) * P], w_qkv[:, k, 0:2 * D],
                                                start=(k == 0), stop=(k == KD - 1))
                    last.then_inc(qk_done, 1)
                    if t >= 1:
                        pe.wait_ge(v_ready, ONE + TT * i + t)
                    for k in range(KD):
                        last = nc.tensor.matmul(ps_s[:, 2, 0:D], xnT[:, k, t * P:(t + 1) * P], w_qkv[:, k, 2 * D:3 * D],
                                                start=(k == 0), stop=(k == KD - 1))
                    last.then_inc(v_done, 1)
                pe.wait_ge(qk_ready, ONE + i + 1)
                for k in range(KD):
                    for t in range(TT):
                        last = nc.tensor.transpose(ps_y[:, k, t * P:(t + 1) * P], centred[:, t, k * P:(k + 1) * P], ident[:])
                last.then_inc(q_turned, 1)
                for k in range(KD):
                    for t in range(TT):
                        last = nc.tensor.transpose(ps_a[:, k, t * P:(t + 1) * P],
                                                   centred[:, t, D + k * P:D + (k + 1) * P], ident[:])
                last.then_inc(k_turned, 1)
                pe.wait_ge(qT_ready, ONE + i + 1)
                pe.wait_ge(v_ready, ONE + TT * (i + 1))

                def attend(h):
                    pe.wait_ge(masked, ONE + HEADS * i + h + 1)
                    if h % GROUP == 0 and h >= 2 * GROUP:
                        pe.wait_ge(group_out, ONE + G * i + h // GROUP - 1)
                    values_sum(nc, ps_y[:, (h // GROUP) % 2, :], probs[h % 2], v_sb, h).then_inc(head_done, 1)

                for h in range(HEADS):
                    if h < PER_BLOCK:
                        pe.wait_ge(k0_ready, ONE + PER_BLOCK * i + h + 1)
                    else:
                        pe.wait_ge(k1_ready, ONE + PER_BLOCK * i + h - PER_BLOCK + 1)
                    causal_scores(nc, ps_s, kT[:, h, :], qT[:, h // PER_BLOCK, :],
                                  lambda bank: pe.wait_ge(score_squared, ONE + 3 * (HEADS * i + h - 1) + bank + 1) if h else None,
                                  lambda last: last.then_inc(scored, 1))
                    if h:
                        attend(h - 1)
                attend(HEADS - 1)
                pe.wait_ge(group_out, ONE + G * (i + 1))
                pe.wait_ge(k1_ready, ONE + PER_BLOCK * (i + 1))
                for t in range(TT):
                    if t >= 2:
                        pe.wait_ge(y_ready, ONE + TT * i + t - 1)
                    for g in range(G):
                        last = nc.tensor.transpose(ps_a[:, t % 2, g * P:(g + 1) * P], yT[:, g, t * P:(t + 1) * P], ident[:])
                    last.then_inc(y_back, 1)
                pe.wait_ge(y_ready, ONE + TT * (i + 1))
                for k in range(KD):
                    for t in range(TT):
                        last = nc.tensor.transpose(ps_s[:, k, t * P:(t + 1) * P], y[:, t, k * P:(k + 1) * P], ident[:])
                last.then_inc(y_turned, 1)
                pe.wait_ge(ynT_ready, ONE + i + 1)
                out = ps_a[:].rearrange("p a (b d) -> p (a b) d", d=D)
                for t in range(TT):
                    for k in range(KD):
                        nc.tensor.matmul(out[:, t, :], xnT[:, k, t * P:(t + 1) * P], w_eff[:, k, :], start=(k == 0), stop=False)
                    for k in range(KD):
                        last = nc.tensor.matmul(out[:, t, :], ynT[:, k, t * P:(t + 1) * P], w_o[:, k, :],
                                                start=False, stop=(k == KD - 1))
                last.then_inc(out_done, 1)

FUTURE = 4
EXPERTS2 = 8
NEG = -1e30
QUERY_AT = (896, 1024, 512, 0)
BANK_TILES = ((3,), (2, 0), (1,))


def layer2_attend(nc, io, keep):
    with ExitStack() as stack:
        room = Room(nc, stack, "a2")
        ident, x_res = keep.ident, keep.x_res
        w_fqvk = room.sb("w_fqvk", KD, 4 * D)
        w_proj = room.sb("w_proj", KD, D)
        conv = room.sb("conv", FUTURE, P)
        cols = room.sb("cols", KD, 2)
        head_mask = room.sb("head_mask", PER_BLOCK)
        hide_later = room.sb("hide_later", P)
        xn = room.sb("xn", TT, D)
        hn = room.sb("hn", TT, D)
        hT = room.sb("hT", KD, T)
        fT = room.sb("fT", KD, T)
        qT = room.sb("qT", KD, T)
        kT = room.sb("kT", HEADS, T)
        q_tok = room.sb("q_tok", TT, D)
        v_sb = room.sb("v_sb", TT, HEADS, SLOT)
        upT = room.sb("upT", FUTURE, KD, T)
        prod = [room.sb(f"prod{n}", D) for n in range(2)]
        v_future = room.sb("v_future", TT, FUTURE, D)
        future = room.sb("future", TT, HEADS, FUTURE)
        neg_fmax = room.sb("neg_fmax", HEADS, TT)
        row_max = room.sb("row_max", HEADS, TT)
        neg_max = room.sb("neg_max", HEADS, TT)
        probs = [room.sb(f"probs{n}", SCORE_LEN) for n in range(2)]
        probsT = [room.sb(f"probsT{n}", SCORE_LEN) for n in range(2)]
        yT = room.sb("yT", HEADS // GROUP, T)
        future_sum = room.sb("future_sum", TT, HEADS)
        future_x = room.sb("future_x", TT, D)
        den = room.sb("den", TT, HEADS)
        y = room.sb("y", TT, D)
        ynT = room.sb("ynT", KD, T)
        x1 = room.sb("x1", TT, D)
        ps_a = room.ps("ps_a", 3, T)
        ps_s = room.ps("ps_s", 3, T)
        ps_y = room.ps("ps_y", 2, T)
        ln_a = LayerNorm(nc, room, "ln_a", keep)
        ln_b = LayerNorm(nc, room, "ln_b", keep)
        weights_in, setup, conv_zeroed = room.sem("weights_in"), room.sem("setup"), room.sem("conv_zeroed")
        xn_ready, hn_ready, hn_turned = room.sem("xn_ready"), room.sem("hn_ready"), room.sem("hn_turned")
        hT_ready = room.sem("hT_ready")
        q_done, k_done, f_done = room.sem("q_done"), room.sem("k_done"), room.sem("f_done")
        qT_ready, fT_ready = room.sem("qT_ready"), room.sem("fT_ready")
        k0_ready, k1_ready = room.sem("k0_ready"), room.sem("k1_ready")
        qv_done, qv_ready = room.sem("qv_done"), room.sem("qv_ready")
        up_done, up_ready = room.sem("up_done"), room.sem("up_ready")
        kvf_done, vf_ready = room.sem("kvf_done"), room.sem("vf_ready")
        prod_done, logit_done, fmax_done = room.sem("prod_done"), room.sem("logit_done"), room.sem("fmax_done")
        scored, hidden_later = room.sem("scored"), room.sem("hidden_later")
        maxed, neg_max_ready = room.sem("maxed"), room.sem("neg_max_ready")
        exped, turned, turned_out = room.sem("exped"), room.sem("turned"), room.sem("turned_out")
        odd_turned_out = room.sem("odd_turned_out")
        head_done, group_out = room.sem("head_done"), room.sem("group_out")
        shifted, future_exped = room.sem("shifted"), room.sem("future_exped")
        weighted, future_step = room.sem("weighted"), room.sem("future_step")
        y_back, den_step, y_ready = room.sem("y_back"), room.sem("den_step"), room.sem("y_ready")
        y_turned, ynT_ready, out_done = room.sem("y_turned"), room.sem("ynT_ready"), room.sem("out_done")
        x1_ready, x1_saved = room.sem("x1_ready"), room.sem("x1_saved")
        xn_kept = room.sem("xn_kept")
        TURN_BACK_AT, DIVIDE_AT, TURN_AT, OUTPUT_AT = (3, 4, 6, 8), (4, 5, 7, 9), 10, 13
        block = room.block()
        G = HEADS // GROUP
        NLOAD = 5 + PER_BLOCK

        @block.sync
        def _(sp):
            n = 0
            for dst, src in ((w_fqvk[:], io.l2_w_fqvk), (w_proj[:], io.l2_w_proj), (cols[:], io.l2_cols),
                             (head_mask[:], io.head_mask), (hide_later[:], io.hide_later)):
                sp.dma_start(dst, src).then_inc(weights_in, DMA)
                n += 1
            sp.wait_ge(conv_zeroed, ONE + 1)
            for h in range(PER_BLOCK):
                rows = slice(h * HD, (h + 1) * HD)
                sp.dma_start(conv[rows, :, rows], io.l2_conv).then_inc(weights_in, DMA)
                n += 1
            assert n == NLOAD
            with sp.Fori(0, B) as i:
                sp.wait_ge(x1_ready, ONE + i + 1)
                sp.dma_start(io.x1_scratch[bass.ds(i, 1)].rearrange("a p t d -> p (a t) d"), x1[:]).then_inc(x1_saved, DMA)
            sp.wait_ge(x1_saved, ONE + DMA * B)

        @block.gpsimd
        def _(pool):
            nc.gpsimd.memset(conv[:], 0.0).then_inc(conv_zeroed, 1)

            def norms(i):
                ln_a.pool_rstd(pool, i)
                ln_b.pool_rstd(pool, i)

            def keep_xn(i):
                wait_apart(pool, keep.always, xn_ready, i + 1)
                wait_apart(pool, keep.always, x1_saved, DMA * i)
                nc.gpsimd.tensor_copy(x1[:], xn[:]).then_inc(xn_kept, 1)

            def weigh(i):
                pool.wait_ge(future_exped, ONE + i + 1)
                for t in range(TT):
                    vf = v_future[:, t].rearrange("p f (h d) -> p f h d", d=HD)
                    for f in range(FUTURE):
                        last = nc.gpsimd.tensor_tensor(
                            vf[:, f], vf[:, f],
                            future[:, t, :, f:f + 1].broadcast_to([P, HEADS, HD]), ALU.mult)
                last.then_inc(weighted, 1)

            norms(0)
            keep_xn(0)
            with pool.Fori(0, B - 1) as i:
                norms(i + 1)
                weigh(i)
                keep_xn(i + 1)
            weigh(B - 1)

        @block.vector
        def _(dve):
            nc.vector.memset(v_sb[:], 0.0).then_inc(setup, 1)
            dve.wait_ge(setup, ONE + 1)
            nc.vector.memset(v_sb[:, :, :, HD:HD + 1], 1.0).then_inc(setup, 1)
            dve.wait_ge(weights_in, ONE + NLOAD * DMA)

            def x_tile(i, t):
                return x_res[:, bass.ds(TT * i + t, 1), :].rearrange("p a d -> p (a d)")

            def norm_a(i):
                ln_a.vector_moments(dve, lambda t: x_tile(i, t), i)

            def norm_b(i):
                dve.wait_ge(xn_kept, ONE + i)
                ln_a.vector_apply(dve, lambda t: x_tile(i, t), lambda t: xn[:, t, :], i).then_inc(xn_ready, 1)
                dve.wait_ge(xn_ready, ONE + i + 1)
                ln_b.vector_moments(dve, lambda t: xn[:, t, :], i)

            def norm_c(i):
                dve.wait_ge(hn_turned, ONE + i)
                ln_b.vector_apply(dve, lambda t: xn[:, t, :], lambda t: hn[:, t, :], i).then_inc(hn_ready, 1)

            def prepare(i, before):
                dve.wait_ge(k_done, ONE + i + 1)
                dve.wait_ge(scored, ONE + 3 * HEADS * i)
                for h in range(PER_BLOCK, HEADS):
                    nc.vector.tensor_scalar(kT[:, h, :], ps_y[:, 1, :], head_mask[:, h - PER_BLOCK:h - PER_BLOCK + 1],
                                            None, ALU.mult).then_inc(k1_ready, 1)
                if before:
                    future_sums(i - 1)
                for t in range(TT):
                    for f in range(FUTURE):
                        n = FUTURE * t + f
                        at = FUTURE * TT * i + n
                        dve.wait_ge(kvf_done, ONE + at + 1)
                        if n == 0:
                            dve.wait_ge(qv_ready, ONE + 2 * TT * (i + 1))
                            dve.wait_ge(weighted, ONE + i)
                            dve.wait_ge(future_step, ONE + 2 * i)
                        if n >= 2:
                            dve.wait_ge(logit_done, ONE + at - 1)
                        nc.vector.tensor_tensor(prod[n % 2][:], ps_a[:, n % 3, D:2 * D], q_tok[:, t, :],
                                                ALU.mult).then_inc(prod_done, 1)
                        if n >= 1:
                            logit(i, n - 1)
                        if before and n in DIVIDE_AT:
                            divide(i - 1, DIVIDE_AT.index(n))
                logit(i, FUTURE * TT - 1)
                if before:
                    add_output(i - 1)
                dve.wait_ge(logit_done, ONE + FUTURE * TT * (i + 1))
                dve.wait_ge(neg_max_ready, ONE + 3 * HEADS * i)
                nc.vector.tensor_reduce(neg_fmax[:].rearrange("p h t -> p t h"), future[:], AX.X, ALU.max,
                                        negate=True).then_inc(fmax_done, 1)

            def logit(i, n):
                dve.wait_ge(prod_done, ONE + FUTURE * TT * i + n + 1)
                nc.vector.tensor_reduce(future[:, n // FUTURE, :, n % FUTURE],
                                        prod[n % 2][:].rearrange("p (h d) -> p h d", d=HD),
                                        AX.X, ALU.add).then_inc(logit_done, 1)

            def head_max(i, h):
                u = HEADS * i + h
                flat = ps_s[:].rearrange("p a c -> p (a c)")

                def hide(bank, at, blocks):
                    dve.wait_ge(scored, ONE + 3 * u + bank + 1)
                    there = flat[:, at:at + blocks * P].rearrange("p (a c) -> p a c", c=P)
                    nc.vector.tensor_tensor(there, there, hide_later[:].rearrange("p (a c) -> p a c", a=1)
                                            .broadcast_to([P, blocks, P]), ALU.add).then_inc(hidden_later, 1)

                def maxima(bank, tiles):
                    dve.wait_ge(hidden_later, ONE + 3 * u + bank + 1)
                    for t in tiles:
                        last = nc.vector.tensor_reduce(row_max[:, h, t:t + 1], flat[:, QUERY_AT[t]:QUERY_AT[t] + (t + 1) * P],
                                                       AX.X, ALU.max)
                    last.then_inc(maxed, 1)

                def negate(bank, tiles):
                    dve.wait_ge(maxed, ONE + 3 * u + bank + 1)
                    nc.vector.scalar_tensor_tensor(out=neg_max[:, h, tiles], in0=row_max[:, h, tiles], scalar=-HD ** -0.5,
                                                   in1=neg_fmax[:, h, tiles], op0=ALU.mult, op1=ALU.min
                                                   ).then_inc(neg_max_ready, 1)

                hide(0, QUERY_AT[3] + 3 * P, 1)
                if h == 0:
                    dve.wait_ge(shifted, ONE + i)
                    dve.wait_ge(exped, ONE + 4 * HEADS * i)
                    dve.wait_ge(fmax_done, ONE + i + 1)
                maxima(0, (3,))
                hide(1, QUERY_AT[2] + 2 * P, 2)
                negate(0, slice(3, 4))
                maxima(1, (2, 0))
                hide(2, QUERY_AT[1] + P, 1)
                negate(1, slice(0, 3, 2))
                maxima(2, (1,))
                negate(2, slice(1, 2))

            def head_copy(i, h):
                u = HEADS * i + h
                dve.wait_ge(turned, ONE + 3 * u + 2)
                if h >= 2:
                    dve.wait_ge(head_done, ONE + u - 1)
                nc.vector.tensor_copy(probsT[h % 2][:, 512:1024], ps_a[:, 1, :]).then_inc(odd_turned_out, 1)

            def future_exponents(i):
                dve.wait_ge(neg_max_ready, ONE + 3 * HEADS * (i + 1))
                nc.vector.tensor_tensor(
                    future[:].rearrange("p t h f -> p t h f"), future[:],
                    neg_max[:].rearrange("p h (t a) -> p t h a", a=1).broadcast_to([P, TT, HEADS, FUTURE]),
                    ALU.add).then_inc(shifted, 1)

            def future_sums(i):
                dve.wait_ge(future_exped, ONE + i + 1)
                nc.vector.tensor_reduce(future_sum[:], future[:], AX.X, ALU.add).then_inc(future_step, 1)
                dve.wait_ge(weighted, ONE + i + 1)
                for t in range(TT):
                    last = nc.vector.tensor_reduce(future_x[:, t, :], v_future[:, t].rearrange("p f d -> p d f"),
                                                   AX.X, ALU.add)
                last.then_inc(future_step, 1)

            def divide(i, t):
                at = 3 * (TT * i + t)
                if t == 0:
                    dve.wait_ge(future_step, ONE + 2 * i + 2)
                dve.wait_ge(y_back, ONE + TT * i + t + 1)
                sums_t = ps_y[:, t % 2, :].rearrange("p (h c) -> p h c", c=SLOT)
                rows = y[:, t, :].rearrange("p (h c) -> p h c", c=HD)
                nc.vector.tensor_tensor(den[:, t, :], sums_t[:, :, HD], future_sum[:, t, :], ALU.add).then_inc(den_step, 1)
                nc.vector.tensor_tensor(rows, sums_t[:, :, 0:HD], future_x[:, t, :].rearrange("p (h c) -> p h c", c=HD),
                                        ALU.add).then_inc(den_step, 1)
                dve.wait_ge(den_step, ONE + at + 1)
                nc.vector.reciprocal(den[:, t, :], den[:, t, :]).then_inc(den_step, 1)
                dve.wait_ge(den_step, ONE + at + 3)
                nc.vector.tensor_tensor(rows, rows, den[:, t, :].rearrange("p (h a) -> p h a", a=1)
                                        .broadcast_to([P, HEADS, HD]), ALU.mult).then_inc(y_ready, 1)

            def add_output(i):
                dve.wait_ge(out_done, ONE + i + 1)
                dve.wait_ge(xn_kept, ONE + i + 1)
                nc.vector.tensor_tensor(x1[:].rearrange("p t d -> p (t d)"), ps_y[:].rearrange("p a d -> p (a d)"),
                                        x1[:].rearrange("p t d -> p (t d)"), ALU.add).then_inc(x1_ready, 1)

            def heads(i, after):
                head_max(i, 0)
                for h in range(1, HEADS):
                    head_max(i, h)
                    head_copy(i, h - 1)
                    if after and h in (4, 7, 10):
                        (norm_a, norm_b, norm_c)[(h - 4) // 3](i + 1)
                future_exponents(i)
                head_copy(i, HEADS - 1)

            norm_a(0)
            norm_b(0)
            norm_c(0)
            prepare(0, False)
            with dve.Fori(0, B - 1) as i:
                heads(i, True)
                prepare(i + 1, True)
            heads(B - 1, False)
            future_sums(B - 1)
            for t in range(TT):
                divide(B - 1, t)
            add_output(B - 1)

        @block.scalar
        def _(act):
            act.wait_ge(weights_in, ONE + NLOAD * DMA)
            act.wait_ge(setup, ONE + 2)

            def output_rows(i):
                act.wait_ge(y_turned, ONE + i + 1)
                nc.scalar.copy(ynT[:], ps_s[:, 0:2, :]).then_inc(ynT_ready, 1)

            def front(i, before):
                act.wait_ge(hn_turned, ONE + i + 1)
                for k in range(KD):
                    last = nc.scalar.activation(hT[:, k, :], ps_a[:, k, :], ACT.Identity, bias=cols[:, k, 1:2],
                                                scale=cols[:, k, 0:1])
                last.then_inc(hT_ready, 1)
                act.wait_ge(q_done, ONE + i + 1)
                nc.scalar.copy(qT[:], ps_s[:, 0:2, :]).then_inc(qT_ready, 1)
                act.wait_ge(f_done, ONE + i + 1)
                nc.scalar.copy(fT[:], ps_a[:, 0:2, :]).then_inc(fT_ready, 1)
                act.wait_ge(k_done, ONE + i + 1)
                for h in range(PER_BLOCK):
                    nc.scalar.activation(kT[:, h, :], ps_y[:, 0, :], ACT.Copy, scale=head_mask[:, h:h + 1]).then_inc(k0_ready, 1)
                for t in range(TT):
                    act.wait_ge(qv_done, ONE + TT * i + t + 1)
                    nc.scalar.copy(q_tok[:, t, :], ps_s[:, t % 3, 0:D]).then_inc(qv_ready, 1)
                    nc.scalar.copy(v_sb[:, t, :, 0:HD], ps_s[:, t % 3, D:2 * D].rearrange("p (h c) -> p h c", c=HD)).then_inc(qv_ready, 1)
                for f in range(FUTURE):
                    act.wait_ge(up_done, ONE + FUTURE * i + f + 1)
                    nc.scalar.copy(upT[:, f], ps_y[:] if f % 2 == 0 else ps_s[:, 0:2, :]).then_inc(up_ready, 1)
                for t in range(TT):
                    for f in range(FUTURE):
                        n = FUTURE * t + f
                        act.wait_ge(prod_done, ONE + FUTURE * TT * i + n + 1)
                        if before and n == 0:
                            act.wait_ge(future_step, ONE + 2 * i)
                        nc.scalar.copy(v_future[:, t, f, :], ps_a[:, n % 3, 0:D]).then_inc(vf_ready, 1)
                        if before and n == TURN_AT:
                            output_rows(i - 1)

            def heads(i):
                def exponents(h):
                    u = HEADS * i + h
                    pr = probs[h % 2]
                    if h >= 2:
                        act.wait_ge(turned, ONE + 3 * (u - 1))
                    for bank, tiles in enumerate(BANK_TILES):
                        act.wait_ge(neg_max_ready, ONE + 3 * u + bank + 1)
                        for t in tiles:
                            at = QUERY_AT[t]
                            nc.scalar.activation(pr[:, at:at + (t + 1) * P],
                                                 ps_s[:].rearrange("p a c -> p (a c)")[:, at:at + (t + 1) * P],
                                                 ACT.Exp, bias=neg_max[:, h, t:t + 1], scale=HD ** -0.5).then_inc(exped, 1)

                def copies(h):
                    u = HEADS * i + h
                    if h >= 2:
                        act.wait_ge(head_done, ONE + u - 1)
                    for bank, width in ((0, T), (2, 2 * P)):
                        act.wait_ge(turned, ONE + 3 * u + bank + 1)
                        nc.scalar.copy(probsT[h % 2][:, 512 * bank:512 * bank + width], ps_a[:, bank, 0:width]).then_inc(turned_out, 1)

                def group(g):
                    act.wait_ge(head_done, ONE + HEADS * i + GROUP * (g + 1))
                    nc.scalar.copy(yT[:, g, :], ps_y[:, g % 2, :]).then_inc(group_out, 1)

                exponents(0)
                for h in range(1, HEADS):
                    exponents(h)
                    copies(h - 1)
                    if h >= 5 and (h - 1) % GROUP == 0:
                        group((h - 1) // GROUP - 1)
                copies(HEADS - 1)
                act.wait_ge(shifted, ONE + i + 1)
                nc.scalar.activation(future[:], future[:], ACT.Exp).then_inc(future_exped, 1)
                group(G - 1)

            front(0, False)
            with act.Fori(0, B - 1) as i:
                heads(i)
                front(i + 1, True)
            heads(B - 1)
            output_rows(B - 1)

        @block.tensor
        def _(pe):
            pe.wait_ge(weights_in, ONE + NLOAD * DMA)
            pe.wait_ge(setup, ONE + 2)
            w_f, w_q, w_vk = 0, D, 2 * D

            def turn_back(i, t):
                if t >= 2:
                    pe.wait_ge(y_ready, ONE + TT * i + t - 1)
                for g in range(G):
                    last = nc.tensor.transpose(ps_y[:, t % 2, g * P:(g + 1) * P], yT[:, g, t * P:(t + 1) * P], ident[:])
                last.then_inc(y_back, 1)

            def turn_rows(i):
                pe.wait_ge(y_ready, ONE + TT * (i + 1))
                for k in range(KD):
                    for t in range(TT):
                        last = nc.tensor.transpose(ps_s[:, k, t * P:(t + 1) * P], y[:, t, k * P:(k + 1) * P], ident[:])
                last.then_inc(y_turned, 1)

            def output(i):
                pe.wait_ge(ynT_ready, ONE + i + 1)
                out = ps_y[:].rearrange("p a (b d) -> p (a b) d", d=D)
                for t in range(TT):
                    for k in range(KD):
                        last = nc.tensor.matmul(out[:, t, :], ynT[:, k, t * P:(t + 1) * P], w_proj[:, k, :],
                                                start=(k == 0), stop=(k == KD - 1))
                last.then_inc(out_done, 1)

            def front(i, before):
                pe.wait_ge(hn_ready, ONE + i + 1)
                for k in range(KD):
                    for t in range(TT):
                        last = nc.tensor.transpose(ps_a[:, k, t * P:(t + 1) * P], hn[:, t, k * P:(k + 1) * P], ident[:])
                last.then_inc(hn_turned, 1)
                pe.wait_ge(hT_ready, ONE + i + 1)
                pe.wait_ge(group_out, ONE + G * i)
                for done, ps, w0 in ((q_done, ps_s, w_q), (k_done, ps_y, w_vk + D), (f_done, ps_a, w_f)):
                    for m in range(KD):
                        for k in range(KD):
                            last = nc.tensor.matmul(ps[:, m, :], w_fqvk[:, k, w0 + m * P:w0 + (m + 1) * P], hT[:, k, :],
                                                    start=(k == 0), stop=(k == KD - 1))
                    last.then_inc(done, 1)
                pe.wait_ge(qT_ready, ONE + i + 1)
                for t in range(TT):
                    if t == 3:
                        pe.wait_ge(qv_ready, ONE + 2 * (TT * i + 1))
                    for k in range(KD):
                        last = nc.tensor.matmul(ps_s[:, t % 3, :], hT[:, k, t * P:(t + 1) * P], w_fqvk[:, k, w_q:w_q + 2 * D],
                                                start=(k == 0), stop=(k == KD - 1))
                    last.then_inc(qv_done, 1)
                pe.wait_ge(fT_ready, ONE + i + 1)
                pe.wait_ge(k0_ready, ONE + PER_BLOCK * (i + 1))
                pe.wait_ge(k1_ready, ONE + PER_BLOCK * (i + 1))
                for f in range(FUTURE):
                    if f == 1:
                        pe.wait_ge(qv_ready, ONE + 2 * TT * (i + 1))
                    if f >= 2:
                        pe.wait_ge(up_ready, ONE + FUTURE * i + f - 1)
                    ps = ps_y if f % 2 == 0 else ps_s
                    for m in range(KD):
                        last = nc.tensor.matmul(ps[:, m, :], conv[:, f, :], fT[:, m, :], start=True, stop=True)
                    last.then_inc(up_done, 1)
                for t in range(TT):
                    for f in range(FUTURE):
                        n = FUTURE * t + f
                        if t == 0:
                            pe.wait_ge(up_ready, ONE + FUTURE * i + f + 1)
                        if n >= 3:
                            pe.wait_ge(vf_ready, ONE + FUTURE * TT * i + n - 2)
                        for k in range(KD):
                            last = nc.tensor.matmul(ps_a[:, n % 3, :], upT[:, f, k, t * P:(t + 1) * P],
                                                    w_fqvk[:, k, w_vk:w_vk + 2 * D], start=(k == 0), stop=(k == KD - 1))
                        last.then_inc(kvf_done, 1)
                        if before:
                            if n == TURN_BACK_AT[0]:
                                pe.wait_ge(up_ready, ONE + FUTURE * (i + 1))
                            if n in TURN_BACK_AT:
                                turn_back(i - 1, TURN_BACK_AT.index(n))
                            if n == TURN_AT:
                                turn_rows(i - 1)
                            if n == OUTPUT_AT:
                                output(i - 1)

            def heads(i, before):
                def score(h):
                    for bank, tiles in enumerate(BANK_TILES):
                        if h:
                            pe.wait_ge(exped, ONE + 4 * (HEADS * i + h - 1) + (1, 3, 4)[bank])
                        for t in tiles:
                            at = QUERY_AT[t] - 512 * bank
                            last = nc.tensor.matmul(ps_s[:, bank, at:at + (t + 1) * P],
                                                    qT[:, h // PER_BLOCK, t * P:(t + 1) * P], kT[:, h, 0:(t + 1) * P],
                                                    start=True, stop=True)
                        last.then_inc(scored, 1)

                def turn(h):
                    u = HEADS * i + h
                    if h == 0:
                        pe.wait_ge(vf_ready, ONE + FUTURE * TT * (i + 1))
                    for bank, tiles in enumerate(((0,), (1, 3), (2,))):
                        if h:
                            if bank == 1:
                                pe.wait_ge(odd_turned_out, ONE + u)
                            else:
                                pe.wait_ge(turned_out, ONE + (2 * u - (1 if bank == 0 else 0)))
                        if bank == 0:
                            pe.wait_ge(exped, ONE + 4 * (u + 1))
                        for s in tiles:
                            for t in range(s, TT):
                                at = SCORE_AT[s] - 512 * bank + (t - s) * P
                                last = nc.tensor.transpose(ps_a[:, bank, at:at + P],
                                                           probs[h % 2][:, QUERY_AT[t] + s * P:QUERY_AT[t] + (s + 1) * P],
                                                           ident[:])
                        last.then_inc(turned, 1)

                def attend(h):
                    u = HEADS * i + h
                    pe.wait_ge(turned_out, ONE + 2 * (u + 1))
                    pe.wait_ge(odd_turned_out, ONE + u + 1)
                    if h % GROUP == 0 and h >= 2 * GROUP:
                        pe.wait_ge(group_out, ONE + G * i + h // GROUP - 1)
                    values_sum(nc, ps_y[:, (h // GROUP) % 2, :], probsT[h % 2], v_sb, h).then_inc(head_done, 1)

                pe.wait_ge(up_ready, ONE + FUTURE * (i + 1))
                score(0)
                for h in range(HEADS):
                    if h + 1 < HEADS:
                        score(h + 1)
                    turn(h)
                    if h == 1 and before:
                        pe.wait_ge(x1_ready, ONE + i)
                    if h:
                        attend(h - 1)
                attend(HEADS - 1)

            front(0, False)
            heads(0, False)
            with pe.Fori(1, B) as i:
                front(i, True)
                heads(i, True)
            pe.wait_ge(group_out, ONE + G * B)
            for t in range(TT):
                turn_back(B - 1, t)
            turn_rows(B - 1)
            output(B - 1)


def layer2_mix(nc, io, keep):
    FF = 4 * D
    NF = FF // P
    with ExitStack() as stack:
        room = Room(nc, stack, "b2")
        ident, x_res = keep.ident, keep.x_res
        w_router = room.sb("w_router", KD, EXPERTS2)
        w_up = room.sb("w_up", EXPERTS2, KD, 2 * D)
        w_down = room.sb("w_down", EXPERTS2, KD, D)
        w_ff1 = room.sb("w_ff1", KD, FF)
        w_ff2 = room.sb("w_ff2", NF, D)
        cols = room.sb("cols", KD, 2)
        xn = room.sb("xn", TT, D)
        x1 = room.sb("x1", TT, D)
        hn = room.sb("hn", TT, D)
        xnT = room.sb("xnT", KD, T)
        hT = room.sb("hT", KD, T)
        top_logit = room.sb("top_logit", TT)
        logits = room.sb("logits", TT, EXPERTS2)
        top = room.sb("top", TT, 8)
        picked = room.sb("picked", TT, EXPERTS2)
        picked_sum = room.sb("picked_sum", TT)
        gate = room.sb("gate", TT, EXPERTS2)
        silu_g = [room.sb(f"silu_g{n}", T) for n in range(2)]
        hidden = [room.sb(f"hidden{n}", KD, T) for n in range(2)]
        gelu = room.sb("gelu", NF, T)
        ps_a = room.ps("ps_a", 2, T)
        ps_gu = [room.ps(f"ps_gu{n}", 2, T) for n in range(2)]
        ps_y = room.ps("ps_y", TT, D)
        ln_a = LayerNorm(nc, room, "ln_a", keep)
        ln_b = LayerNorm(nc, room, "ln_b", keep)
        weights_in, x1_in = room.sem("weights_in"), room.sem("x1_in")
        xn_ready, hn_ready = room.sem("xn_ready"), room.sem("hn_ready")
        xn_turned, hn_turned = room.sem("xn_turned"), room.sem("hn_turned")
        xnT_ready, hT_ready = room.sem("xnT_ready"), room.sem("hT_ready")
        routed_logits, route_step, exped = room.sem("routed_logits"), room.sem("route_step"), room.sem("exped")
        up_done, silu_ready, hidden_ready = room.sem("up_done"), room.sem("silu_ready"), room.sem("hidden_ready")
        down_done, expert_added = room.sem("down_done"), room.sem("expert_added")
        ff1_done, gelu_ready, ff2_done = room.sem("ff1_done"), room.sem("gelu_ready"), room.sem("ff2_done")
        mlp_added, batch_done = room.sem("mlp_added"), room.sem("batch_done")
        block = room.block()
        NLOAD = 6
        STEPS = 6

        @block.sync
        def _(sp):
            n = 0
            for dst, src in ((w_router[:], io.l2_w_router), (w_up[:], io.l2_w_up), (w_down[:], io.l2_w_down),
                             (w_ff1[:], io.l2_w_ff1), (w_ff2[:], io.l2_w_ff2), (cols[:], io.l2_cols2)):
                sp.dma_start(dst, src).then_inc(weights_in, DMA)
                n += 1
            assert n == NLOAD
            with sp.Fori(0, B) as i:
                sp.wait_ge(batch_done, ONE + i)
                sp.dma_start(x1[:], io.x1_scratch[bass.ds(i, 1)].rearrange("a p t d -> p (a t) d")).then_inc(x1_in, DMA)

        @block.gpsimd
        def _(pool):
            with pool.Fori(0, B) as i:
                ln_a.pool_rstd(pool, i)
                ln_b.pool_rstd(pool, i)

        @block.vector
        def _(dve):
            dve.wait_ge(weights_in, ONE + NLOAD * DMA)

            def norm_x(i):
                def x_tile(t):
                    return x_res[:, bass.ds(TT * i + t, 1), :].rearrange("p a d -> p (a d)")
                ln_a.vector_moments(dve, x_tile, i)
                dve.wait_ge(xn_turned, ONE + i)
                ln_a.vector_apply(dve, x_tile, lambda t: xn[:, t, :], i).then_inc(xn_ready, 1)

            def norm_x1(i):
                dve.wait_ge(x1_in, ONE + DMA * (i + 1))
                ln_b.vector_moments(dve, lambda t: x1[:, t, :], i)
                dve.wait_ge(hn_turned, ONE + i)
                ln_b.vector_apply(dve, lambda t: x1[:, t, :], lambda t: hn[:, t, :], i).then_inc(hn_ready, 1)

            def route(i):
                at = STEPS * i
                dve.wait_ge(routed_logits, ONE + i + 1)
                raw = ps_a[:, 0, 0:TT * EXPERTS2].rearrange("p (t e) -> p t e", t=TT)
                nc.vector.tensor_reduce(top_logit[:], raw, AX.X, ALU.max).then_inc(route_step, 1)
                dve.wait_ge(route_step, ONE + at + 1)
                nc.vector.tensor_tensor(logits[:], raw, top_logit[:].rearrange("p (t a) -> p t a", a=1)
                                        .broadcast_to([P, TT, EXPERTS2]), ALU.subtract).then_inc(route_step, 1)
                wait_apart(dve, keep.always, exped, i + 1)
                for t in range(TT):
                    last = nc.vector.max(top[:, t, :], logits[:, t, :])
                last.then_inc(route_step, 1)
                dve.wait_ge(route_step, ONE + at + 3)
                for t in range(TT):
                    last = nc.vector.scalar_tensor_tensor(
                        out=picked[:, t, :], in0=logits[:, t, :], scalar=top[:, t, 1:2], in1=logits[:, t, :],
                        op0=ALU.is_ge, op1=ALU.mult, accum_out=picked_sum[:, t:t + 1])
                last.then_inc(route_step, 1)
                dve.wait_ge(route_step, ONE + at + 4)
                nc.vector.reciprocal(picked_sum[:], picked_sum[:]).then_inc(route_step, 1)
                dve.wait_ge(route_step, ONE + at + 5)
                nc.vector.tensor_tensor(gate[:], picked[:], picked_sum[:].rearrange("p (t a) -> p t a", a=1)
                                        .broadcast_to([P, TT, EXPERTS2]), ALU.mult).then_inc(route_step, 1)
                dve.wait_ge(route_step, ONE + at + 6)

            def experts(i):
                def combine(e):
                    dve.wait_ge(down_done, ONE + EXPERTS2 * i + e + 1)
                    if e == 0:
                        dve.wait_ge(batch_done, ONE + i)
                    else:
                        dve.wait_ge(expert_added, ONE + EXPERTS2 * i + e)
                    for t in range(TT):
                        xb = x_res[:, bass.ds(TT * i + t, 1), :].rearrange("p a d -> p (a d)")
                        last = nc.vector.scalar_tensor_tensor(out=xb, in0=ps_y[:, t, :], scalar=gate[:, t, e:e + 1],
                                                              in1=xb, op0=ALU.mult, op1=ALU.add)
                    last.then_inc(expert_added, 1)

                for e in range(EXPERTS2):
                    for m in range(KD):
                        at = KD * (EXPERTS2 * i + e) + m
                        dve.wait_ge(silu_ready, ONE + at + 1)
                        if m == 0 and e >= 2:
                            dve.wait_ge(down_done, ONE + EXPERTS2 * i + e - 1)
                        nc.vector.tensor_tensor(hidden[e % 2][:, m, :], silu_g[m][:], ps_gu[m][:, 1, :],
                                                ALU.mult).then_inc(hidden_ready, 1)
                    if e:
                        combine(e - 1)
                combine(EXPERTS2 - 1)

            def finish(i):
                xb = x_res[:, bass.ds(TT * i, TT), :]
                dve.wait_ge(expert_added, ONE + EXPERTS2 * (i + 1))
                dve.wait_ge(ff2_done, ONE + i + 1)
                nc.vector.tensor_tensor(xb, xb, ps_y[:], ALU.add).then_inc(mlp_added, 1)
                dve.wait_ge(mlp_added, ONE + i + 1)
                nc.vector.tensor_tensor(xb, xb, x1[:], ALU.add).then_inc(batch_done, 1)

            norm_x(0)
            norm_x1(0)
            with dve.Fori(0, B - 1) as i:
                route(i)
                experts(i)
                norm_x(i + 1)
                finish(i)
                norm_x1(i + 1)
            route(B - 1)
            experts(B - 1)
            finish(B - 1)

        @block.scalar
        def _(act):
            act.wait_ge(weights_in, ONE + NLOAD * DMA)
            with act.Fori(0, B) as i:
                act.wait_ge(xn_turned, ONE + i + 1)
                nc.scalar.copy(xnT[:], ps_a[:]).then_inc(xnT_ready, 1)
                act.wait_ge(hn_turned, ONE + i + 1)
                for k in range(KD):
                    last = nc.scalar.activation(hT[:, k, :], ps_gu[0][:, k, :], ACT.Identity, bias=cols[:, k, 1:2],
                                                scale=cols[:, k, 0:1])
                last.then_inc(hT_ready, 1)
                act.wait_ge(route_step, ONE + STEPS * i + 2)
                nc.scalar.activation(logits[:], logits[:], ACT.Exp).then_inc(exped, 1)
                for e in range(EXPERTS2):
                    for m in range(KD):
                        at = KD * (EXPERTS2 * i + e) + m
                        act.wait_ge(up_done, ONE + at + 1)
                        if e:
                            act.wait_ge(hidden_ready, ONE + at - 1)
                        nc.scalar.activation(silu_g[m][:], ps_gu[m][:, 0, :], ACT.Silu).then_inc(silu_ready, 1)
                for n in range(NF):
                    act.wait_ge(ff1_done, ONE + NF * i + n + 1)
                    nc.scalar.activation(gelu[:, n, :], ps_gu[n % 2][:, (n // 2) % 2, :], ACT.Gelu).then_inc(gelu_ready, 1)

        @block.tensor
        def _(pe):
            pe.wait_ge(weights_in, ONE + NLOAD * DMA)
            with pe.Fori(0, B) as i:
                pe.wait_ge(xn_ready, ONE + i + 1)
                for k in range(KD):
                    for t in range(TT):
                        last = nc.tensor.transpose(ps_a[:, k, t * P:(t + 1) * P], xn[:, t, k * P:(k + 1) * P], ident[:])
                last.then_inc(xn_turned, 1)
                pe.wait_ge(hn_ready, ONE + i + 1)
                pe.wait_ge(gelu_ready, ONE + NF * i)
                for k in range(KD):
                    for t in range(TT):
                        last = nc.tensor.transpose(ps_gu[0][:, k, t * P:(t + 1) * P], hn[:, t, k * P:(k + 1) * P], ident[:])
                last.then_inc(hn_turned, 1)
                pe.wait_ge(xnT_ready, ONE + i + 1)
                for t in range(TT):
                    for k in range(KD):
                        last = nc.tensor.matmul(ps_a[:, 0, t * EXPERTS2:(t + 1) * EXPERTS2], xnT[:, k, t * P:(t + 1) * P],
                                                w_router[:, k, :], start=(k == 0), stop=(k == KD - 1))
                last.then_inc(routed_logits, 1)
                pe.wait_ge(hT_ready, ONE + i + 1)

                def up(e):
                    for m in range(KD):
                        if e:
                            pe.wait_ge(hidden_ready, ONE + KD * (EXPERTS2 * i + e - 1) + m + 1)
                        for half in range(2):
                            for k in range(KD):
                                last = nc.tensor.matmul(ps_gu[m][:, half, :], w_up[:, e, k, half * D + m * P:half * D + (m + 1) * P],
                                                        xnT[:, k, :], start=(k == 0), stop=(k == KD - 1))
                        last.then_inc(up_done, 1)

                def down(e):
                    pe.wait_ge(hidden_ready, ONE + KD * (EXPERTS2 * i + e + 1))
                    if e:
                        pe.wait_ge(expert_added, ONE + EXPERTS2 * i + e)
                    else:
                        pe.wait_ge(mlp_added, ONE + i)
                    for t in range(TT):
                        for k in range(KD):
                            last = nc.tensor.matmul(ps_y[:, t, :], hidden[e % 2][:, k, t * P:(t + 1) * P], w_down[:, e, k, :],
                                                    start=(k == 0), stop=(k == KD - 1))
                    last.then_inc(down_done, 1)

                for e in range(EXPERTS2):
                    up(e)
                    if e:
                        down(e - 1)

                for n in range(NF):
                    if n == 0:
                        pe.wait_ge(hidden_ready, ONE + KD * EXPERTS2 * (i + 1))
                    if n >= 4:
                        pe.wait_ge(gelu_ready, ONE + NF * i + n - 3)
                    for k in range(KD):
                        last = nc.tensor.matmul(ps_gu[n % 2][:, (n // 2) % 2, :], w_ff1[:, k, n * P:(n + 1) * P], hT[:, k, :],
                                                start=(k == 0), stop=(k == KD - 1))
                    last.then_inc(ff1_done, 1)
                    if n == 0:
                        down(EXPERTS2 - 1)
                pe.wait_ge(gelu_ready, ONE + NF * (i + 1))
                pe.wait_ge(expert_added, ONE + EXPERTS2 * (i + 1))
                for t in range(TT):
                    for n in range(NF):
                        last = nc.tensor.matmul(ps_y[:, t, :], gelu[:, n, t * P:(t + 1) * P], w_ff2[:, n, :],
                                                start=(n == 0), stop=(n == NF - 1))
                last.then_inc(ff2_done, 1)

EXPERTS3, LATENT = 8, 64
RMS_EPS = 1e-6


def layer3_attend(nc, io, keep):
    with ExitStack() as stack:
        room = Room(nc, stack, "a3")
        ident, x_res = keep.ident, keep.x_res
        w_qkv = room.sb("w_qkv", KD, 3 * D)
        cols = room.sb("cols", KD, 6)
        hide_later = room.sb("hide_later", P)
        xn = room.sb("xn", TT, D)
        xnT = room.sb("xnT", KD, T)
        qT = room.sb("qT", KD, T)
        kT = room.sb("kT", KD, T)
        vT = room.sb("vT", KD, T + 2)
        mixT = room.sb("mixT", KD, T)
        nextT = room.sb("nextT", KD, T)
        mix = room.sb("mix", TT, D)
        nxt = room.sb("nxt", TT, D)
        row_max = room.sb("row_max", TT)
        neg_max = room.sb("neg_max", TT)
        row_sum = room.sb("row_sum", TT)
        row_inv = room.sb("row_inv", TT)
        neg_diag = room.sb("neg_diag", TT)
        scrap = room.sb("scrap", TT, P)
        probs = room.sb("probs", SCORE_LEN)
        probsT = room.sb("probsT", SCORE_LEN)
        summed = room.sb("summed", TT, D)
        ps_a = room.ps("ps_a", 3, T)
        ps_s = room.ps("ps_s", 3, T)
        ps_o = room.ps("ps_o", 2, T)
        ln = LayerNorm(nc, room, "ln", keep)
        weights_in, setup, xn_saved = room.sem("weights_in"), room.sem("setup"), room.sem("xn_saved")
        xn_ready, xn_turned, xnT_ready = room.sem("xn_ready"), room.sem("xn_turned"), room.sem("xnT_ready")
        q_done, k_done, v_done = room.sem("q_done"), room.sem("k_done"), room.sem("v_done")
        qT_ready, kT_ready, vT_ready = room.sem("qT_ready"), room.sem("kT_ready"), room.sem("vT_ready")
        mix_step, mixT_ready = room.sem("mix_step"), room.sem("mixT_ready")
        mix_turned, next_turned = room.sem("mix_turned"), room.sem("next_turned")
        mix_ready, next_ready = room.sem("mix_ready"), room.sem("next_ready")
        scored, hidden_later, maxed, neg_max_ready = (room.sem("scored"), room.sem("hidden_later"),
                                                      room.sem("maxed"), room.sem("neg_max_ready"))
        exped, diag_done, turned = room.sem("exped"), room.sem("diag_done"), room.sem("turned")
        turned_out, odd_turned_out = room.sem("turned_out"), room.sem("odd_turned_out")
        inverted, out_done, out_step = room.sem("inverted"), room.sem("out_done"), room.sem("out_step")
        batch_done = room.sem("batch_done")
        block = room.block()
        NLOAD = 3

        @block.sync
        def _(sp):
            n = 0
            for dst, src in ((w_qkv[:], io.l3_w_qkv), (cols[:], io.l3_cols), (hide_later[:], io.hide_later)):
                sp.dma_start(dst, src).then_inc(weights_in, DMA)
                n += 1
            assert n == NLOAD
            with sp.Fori(0, B) as i:
                sp.wait_ge(xn_ready, ONE + i + 1)
                sp.dma_start(io.xn3_scratch[bass.ds(i, 1)].rearrange("a p t d -> p (a t) d"), xn[:]).then_inc(xn_saved, DMA)
            sp.wait_ge(xn_saved, ONE + DMA * B)

        @block.gpsimd
        def _(pool):
            with pool.Fori(0, B) as i:
                ln.pool_rstd(pool, i)

        @block.vector
        def _(dve):
            nc.vector.memset(vT[:, :, 0:1], 0.0).then_inc(setup, 1)
            nc.vector.memset(vT[:, :, T + 1:T + 2], 0.0).then_inc(setup, 1)
            dve.wait_ge(weights_in, ONE + NLOAD * DMA)
            dve.wait_ge(setup, ONE + 2)
            flat = ps_s[:].rearrange("p a c -> p (a c)")

            def norms(i):
                def x_tile(t):
                    return x_res[:, bass.ds(TT * i + t, 1), :].rearrange("p a d -> p (a d)")
                ln.vector_moments(dve, x_tile, i)
                dve.wait_ge(xn_turned, ONE + i)
                dve.wait_ge(xn_saved, ONE + DMA * i)
                ln.vector_apply(dve, x_tile, lambda t: xn[:, t, :], i).then_inc(xn_ready, 1)

            def convolve(i):
                dve.wait_ge(vT_ready, ONE + i + 1)
                dve.wait_ge(next_turned, ONE + i)
                for k in range(KD):
                    nc.vector.tensor_scalar(mixT[:, k, :], vT[:, k, 1:T + 1], cols[:, k, 4:5], None, ALU.mult)
                    last = nc.vector.tensor_scalar(nextT[:, k, :], vT[:, k, 2:T + 2], cols[:, k, 5:6], None, ALU.mult)
                last.then_inc(mix_step, 1)
                dve.wait_ge(mix_step, ONE + 2 * i + 1)
                for k in range(KD):
                    last = nc.vector.scalar_tensor_tensor(out=mixT[:, k, :], in0=vT[:, k, 0:T], scalar=cols[:, k, 3:4],
                                                          in1=mixT[:, k, :], op0=ALU.mult, op1=ALU.add)
                last.then_inc(mix_step, 1)
                dve.wait_ge(mix_step, ONE + 2 * i + 2)
                nc.vector.tensor_tensor(mixT[:], mixT[:], nextT[:], ALU.add).then_inc(mixT_ready, 1)

            def maxima(i):
                dve.wait_ge(scored, ONE + 3 * (i + 1))
                lead = flat[:, 384:384 + 3 * 384].rearrange("p (a c) -> p a c", c=384)[:, :, 0:P]
                nc.vector.tensor_tensor(lead, lead, hide_later[:].rearrange("p (a c) -> p a c", a=1)
                                        .broadcast_to([P, 3, P]), ALU.add)
                at = QUERY_AT[0]
                nc.vector.tensor_tensor(flat[:, at:at + P], flat[:, at:at + P], hide_later[:], ALU.add).then_inc(hidden_later, 1)
                dve.wait_ge(hidden_later, ONE + i + 1)
                for t in range(TT):
                    last = nc.vector.tensor_reduce(row_max[:, t:t + 1], flat[:, QUERY_AT[t]:QUERY_AT[t] + (t + 1) * P],
                                                   AX.X, ALU.max)
                last.then_inc(maxed, 1)
                dve.wait_ge(maxed, ONE + i + 1)
                nc.vector.tensor_scalar(neg_max[:], row_max[:], -D ** -0.5, None, ALU.mult).then_inc(neg_max_ready, 1)

            def combine(i):
                dve.wait_ge(next_turned, ONE + i + 1)
                nc.vector.tensor_copy(nxt[:].rearrange("p t d -> p (t d)"),
                                      ps_a[:, 0:2, :].rearrange("p a d -> p (a d)")).then_inc(next_ready, 1)
                dve.wait_ge(exped, ONE + TT * (i + 1))
                for t in range(TT):
                    at = QUERY_AT[t] + t * P
                    last = nc.vector.scalar_tensor_tensor(out=scrap[:, t, :], in0=probs[:, at:at + P], scalar=-1.0,
                                                          in1=ident[:], op0=ALU.mult, op1=ALU.mult,
                                                          accum_out=neg_diag[:, t:t + 1])
                last.then_inc(diag_done, 1)
                nc.vector.reciprocal(row_inv[:], row_sum[:]).then_inc(inverted, 1)
                dve.wait_ge(turned, ONE + 3 * i + 2)
                nc.vector.tensor_copy(probsT[:, 512:1024], ps_a[:, 1, :]).then_inc(odd_turned_out, 1)

            def finish(i):
                dve.wait_ge(diag_done, ONE + i + 1)
                dve.wait_ge(next_ready, ONE + i + 1)
                dve.wait_ge(inverted, ONE + i + 1)
                dve.wait_ge(out_done, ONE + i + 1)
                out = ps_o[:].rearrange("p a (b d) -> p (a b) d", d=D)
                for t in range(TT):
                    last = nc.vector.scalar_tensor_tensor(out=summed[:, t, :], in0=nxt[:, t, :], scalar=neg_diag[:, t:t + 1],
                                                          in1=out[:, t, :], op0=ALU.mult, op1=ALU.add)
                last.then_inc(out_step, 1)
                dve.wait_ge(out_step, ONE + i + 1)
                for t in range(TT):
                    xb = x_res[:, bass.ds(TT * i + t, 1), :].rearrange("p a d -> p (a d)")
                    last = nc.vector.scalar_tensor_tensor(out=xb, in0=summed[:, t, :], scalar=row_inv[:, t:t + 1],
                                                          in1=xb, op0=ALU.mult, op1=ALU.add)
                last.then_inc(batch_done, 1)

            norms(0)
            with dve.Fori(0, B - 1) as i:
                convolve(i)
                maxima(i)
                combine(i)
                norms(i + 1)
                finish(i)
            convolve(B - 1)
            maxima(B - 1)
            combine(B - 1)
            finish(B - 1)

        @block.scalar
        def _(act):
            act.wait_ge(weights_in, ONE + NLOAD * DMA)
            act.wait_ge(setup, ONE + 2)
            with act.Fori(0, B) as i:
                act.wait_ge(xn_turned, ONE + i + 1)
                nc.scalar.copy(xnT[:], ps_a[:, 0:2, :]).then_inc(xnT_ready, 1)
                for done, ready, ps, out, c, at in ((q_done, qT_ready, ps_s, qT, 0, 0), (v_done, vT_ready, ps_o, vT, 2, 1),
                                                    (k_done, kT_ready, ps_a, kT, 1, 0)):
                    act.wait_ge(done, ONE + i + 1)
                    if out is vT:
                        act.wait_ge(mixT_ready, ONE + i)
                    for k in range(KD):
                        last = nc.scalar.activation(out[:, k, at:at + T], ps[:, k, :], ACT.Identity, bias=cols[:, k, c:c + 1])
                    last.then_inc(ready, 1)
                act.wait_ge(neg_max_ready, ONE + i + 1)
                act.wait_ge(turned, ONE + 3 * i)
                act.wait_ge(diag_done, ONE + i)
                act.wait_ge(inverted, ONE + i)
                for tiles in BANK_TILES:
                    for t in tiles:
                        at = QUERY_AT[t]
                        nc.scalar.activation(probs[:, at:at + (t + 1) * P],
                                             ps_s[:].rearrange("p a c -> p (a c)")[:, at:at + (t + 1) * P],
                                             ACT.Exp, bias=neg_max[:, t:t + 1], scale=D ** -0.5,
                                             accum_out=row_sum[:, t:t + 1]).then_inc(exped, 1)
                act.wait_ge(mix_turned, ONE + i + 1)
                nc.scalar.copy(mix[:].rearrange("p t d -> p (t d)"), ps_o[:].rearrange("p a d -> p (a d)")).then_inc(mix_ready, 1)
                for bank, width in ((0, T), (2, 2 * P)):
                    act.wait_ge(turned, ONE + 3 * i + bank + 1)
                    nc.scalar.copy(probsT[:, 512 * bank:512 * bank + width], ps_a[:, bank, 0:width]).then_inc(turned_out, 1)

        @block.tensor
        def _(pe):
            pe.wait_ge(weights_in, ONE + NLOAD * DMA)
            with pe.Fori(0, B) as i:
                pe.wait_ge(xn_ready, ONE + i + 1)
                pe.wait_ge(turned_out, ONE + 2 * i)
                pe.wait_ge(odd_turned_out, ONE + i)
                for k in range(KD):
                    for t in range(TT):
                        last = nc.tensor.transpose(ps_a[:, k, t * P:(t + 1) * P], xn[:, t, k * P:(k + 1) * P], ident[:])
                last.then_inc(xn_turned, 1)
                pe.wait_ge(xnT_ready, ONE + i + 1)
                for done, ps, c in ((q_done, ps_s, 0), (v_done, ps_o, 2), (k_done, ps_a, 1)):
                    if c == 0:
                        pe.wait_ge(exped, ONE + TT * i)
                    if c == 2:
                        pe.wait_ge(batch_done, ONE + i)
                    for m in range(KD):
                        for k in range(KD):
                            last = nc.tensor.matmul(ps[:, m, :], w_qkv[:, k, c * D + m * P:c * D + (m + 1) * P], xnT[:, k, :],
                                                    start=(k == 0), stop=(k == KD - 1))
                    last.then_inc(done, 1)
                pe.wait_ge(qT_ready, ONE + i + 1)
                pe.wait_ge(kT_ready, ONE + i + 1)
                for bank, tiles in enumerate(BANK_TILES):
                    for t in tiles:
                        at = QUERY_AT[t] - 512 * bank
                        for k in range(KD):
                            last = nc.tensor.matmul(ps_s[:, bank, at:at + (t + 1) * P], qT[:, k, t * P:(t + 1) * P],
                                                    kT[:, k, 0:(t + 1) * P], start=(k == 0), stop=(k == KD - 1))
                    last.then_inc(scored, 1)
                pe.wait_ge(mixT_ready, ONE + i + 1)
                for ps, rows, done in ((ps_o, mixT, mix_turned), (ps_a, nextT, next_turned)):
                    for t in range(TT):
                        for k in range(KD):
                            at = (t % 2) * D + k * P
                            last = nc.tensor.transpose(ps[:, t // 2, at:at + P], rows[:, k, t * P:(t + 1) * P], ident[:])
                    last.then_inc(done, 1)
                pe.wait_ge(exped, ONE + TT * (i + 1))
                pe.wait_ge(next_ready, ONE + i + 1)
                for bank, tiles in enumerate(((0,), (1, 3), (2,))):
                    for s in tiles:
                        for t in range(s, TT):
                            at = SCORE_AT[s] - 512 * bank + (t - s) * P
                            last = nc.tensor.transpose(ps_a[:, bank, at:at + P],
                                                       probs[:, QUERY_AT[t] + s * P:QUERY_AT[t] + (s + 1) * P], ident[:])
                    last.then_inc(turned, 1)
                pe.wait_ge(mix_ready, ONE + i + 1)
                pe.wait_ge(turned_out, ONE + 2 * (i + 1))
                pe.wait_ge(odd_turned_out, ONE + i + 1)
                out = ps_o[:].rearrange("p a (b d) -> p (a b) d", d=D)
                for t in range(TT):
                    for s in range(t + 1):
                        at = SCORE_AT[s] + (t - s) * P
                        last = nc.tensor.matmul(out[:, t, :], probsT[:, at:at + P], mix[:, s, :], start=(s == 0), stop=(s == t))
                last.then_inc(out_done, 1)


def layer3_mix(nc, io, keep):
    with ExitStack() as stack:
        room = Room(nc, stack, "b3")
        ident, x_res = keep.ident, keep.x_res
        w_q = room.sb("w_q", KD, D)
        w_down = room.sb("w_down", KD, P)
        w_up = room.sb("w_up", 2 * D)
        w_o = room.sb("w_o", KD, D)
        w_g = room.sb("w_g", KD, EXPERTS3)
        w_e = room.sb("w_e", KD, EXPERTS3 * D)
        rows = room.sb("rows", 2 * D + EXPERTS3)
        cols = room.sb("cols", KD, 2)
        b_down = room.sb("b_down", 1)
        gains = room.sb("gains", KD, 2)
        eps = room.sb("eps", TT)
        xn = room.sb("xn", TT, D)
        xn_again = room.sb("xn_again", TT, D)
        x1 = room.sb("x1", TT, D)
        hn = [room.sb(f"hn{n}", TT, D) for n in range(2)]
        hT = [room.sb(f"hT{n}", KD, T) for n in range(2)]
        downT = room.sb("downT", T)
        q = room.sb("q", TT, D)
        kv = room.sb("kv", TT, 2 * D)
        prod = [room.sb(f"prod{n}", HEADS * HEADS * HD) for n in range(3)]
        att = room.sb("att", TT, HEADS * HEADS)
        att_max = room.sb("att_max", TT * HEADS)
        att_inv = room.sb("att_inv", TT * HEADS)
        y = room.sb("y", TT, D)
        ynT = room.sb("ynT", KD, T)
        squares = room.sb("squares", 2, TT, D)
        square_sum = room.sb("square_sum", 2, TT)
        spread = room.sb("spread", 2, TT)
        rstd = room.sb("rstd", 2, TT)
        gate = room.sb("gate", TT, EXPERTS3)
        gate_max = room.sb("gate_max", TT)
        ps_t = room.ps("ps_t", 2, T)
        ps_q = room.ps("ps_q", TT, D)
        ps_kv = [room.ps(f"ps_kv{n}", T) for n in range(2)]
        ps_e = [room.ps(f"ps_e{n}", T) for n in range(2)]
        weights_in, setup, zeroed, xn_in = room.sem("weights_in"), room.sem("setup"), room.sem("zeroed"), room.sem("xn_in")
        xn_again_in = room.sem("xn_again_in")
        square_done = [room.sem(f"square_done{n}") for n in range(2)]
        eps_added = [room.sem(f"eps_added{n}") for n in range(2)]
        rstd_done = [room.sem(f"rstd_done{n}") for n in range(2)]
        h1_ready, h1_turned, h1T_ready = room.sem("h1_ready"), room.sem("h1_turned"), room.sem("h1T_ready")
        h2_ready, h2_turned, h2T_ready = room.sem("h2_ready"), room.sem("h2_turned"), room.sem("h2T_ready")
        q_done, q_ready = room.sem("q_done"), room.sem("q_ready")
        down_done, downT_ready = room.sem("down_done"), room.sem("downT_ready")
        kv_done, kv_ready = room.sem("kv_done"), room.sem("kv_ready")
        qk_multiplied, qk_summed = room.sem("qk_multiplied"), room.sem("qk_summed")
        soft_step, exped = room.sem("soft_step"), room.sem("exped")
        av_multiplied, av_summed = room.sem("av_multiplied"), room.sem("av_summed")
        y_ready, y_turned, ynT_ready, o_done = room.sem("y_ready"), room.sem("y_turned"), room.sem("ynT_ready"), room.sem("o_done")
        x1_step, x1_ready = room.sem("x1_step"), room.sem("x1_ready")
        gate_logits, gate_step, gate_exped = room.sem("gate_logits"), room.sem("gate_step"), room.sem("gate_exped")
        x1_added, expert_done, expert_added = room.sem("x1_added"), room.sem("expert_done"), room.sem("expert_added")
        block = room.block()
        NLOAD = 9
        PAIRS = EXPERTS3 // 2

        @block.sync
        def _(sp):
            n = 0
            for dst, src in ((w_q[:], io.l3_w_q), (w_up[:], io.l3_w_up), (w_o[:], io.l3_w_o), (w_g[:], io.l3_w_g),
                             (w_e[:], io.l3_w_e), (rows[:], io.l3_rows), (cols[:], io.l3_cols2), (b_down[:], io.l3_b_down),
                             (w_down[:], io.l3_w_down)):
                sp.dma_start(dst, src).then_inc(weights_in, DMA)
                n += 1
            assert n == NLOAD

            def load_xn(i):
                sp.wait_ge(h1_ready, ONE + i)
                sp.dma_start(xn[:], io.xn3_scratch[bass.ds(i, 1)].rearrange("a p t d -> p (a t) d")).then_inc(xn_in, DMA)

            def load_xn_again(i):
                sp.wait_ge(x1_ready, ONE + i)
                sp.dma_start(xn_again[:], io.xn3_scratch[bass.ds(i, 1)].rearrange("a p t d -> p (a t) d")).then_inc(
                    xn_again_in, DMA)

            load_xn(0)
            with sp.Fori(0, B - 1) as i:
                load_xn(i + 1)
                load_xn_again(i)
            load_xn_again(B - 1)

        @block.gpsimd
        def _(pool):
            nc.gpsimd.memset(eps[:], D * RMS_EPS).then_inc(zeroed, 1)
            pool.wait_ge(zeroed, ONE + 1)

            def rms(i, n):
                pool.wait_ge(square_done[n], ONE + i + 1)
                nc.gpsimd.tensor_tensor(spread[:, n, :], square_sum[:, n, :], eps[:], ALU.add).then_inc(eps_added[n], 1)
                pool.wait_ge(eps_added[n], ONE + i + 1)
                nc.gpsimd.tensor_tensor(rstd[:, n, :], spread[:, n, :], keep.neg_half[:, 0:TT],
                                        ALU.pow).then_inc(rstd_done[n], 1)

            def products(i, before, after):
                pool.wait_ge(q_ready, ONE + i + 1)
                for t in range(TT):
                    if before and t == 2:
                        rms(i - 1, 1)
                    pool.wait_ge(kv_ready, ONE + TT * i + t + 1)
                    if t == 0 and before:
                        pool.wait_ge(av_summed, ONE + TT * i - 1)
                    if t == 1:
                        pool.wait_ge(av_summed, ONE + TT * i)
                    if t == 3:
                        pool.wait_ge(qk_summed, ONE + TT * i + 1)
                    nc.gpsimd.tensor_tensor(
                        prod[t % 3][:].rearrange("p (h g d) -> p h g d", h=HEADS, g=HEADS),
                        q[:, t, :].rearrange("p (h a d) -> p h a d", a=1, d=HD).broadcast_to([P, HEADS, HEADS, HD]),
                        kv[:, t, :].rearrange("p (a g c) -> p a g c", a=1, c=2 * HD)[:, :, :, 0:HD]
                        .broadcast_to([P, HEADS, HEADS, HD]), ALU.mult).then_inc(qk_multiplied, 1)
                if after:
                    rms(i + 1, 0)
                for t in range(TT):
                    pool.wait_ge(exped, ONE + 2 * i + t // 2 + 1)
                    if t == 3:
                        pool.wait_ge(av_summed, ONE + TT * i + 1)
                    else:
                        pool.wait_ge(qk_summed, ONE + TT * i + t + 2)
                    nc.gpsimd.tensor_tensor(
                        prod[(TT + t) % 3][:].rearrange("p (h d g) -> p h d g", h=HEADS, d=HD),
                        att[:, t, :].rearrange("p (h a g) -> p h a g", a=1, g=HEADS).broadcast_to([P, HEADS, HD, HEADS]),
                        kv[:, t, :].rearrange("p (a g c) -> p a c g", a=1, c=2 * HD)[:, :, HD:2 * HD, :]
                        .broadcast_to([P, HEADS, HD, HEADS]), ALU.mult).then_inc(av_multiplied, 1)

            rms(0, 0)
            products(0, False, True)
            with pool.Fori(1, B - 1) as i:
                products(i, True, True)
            products(B - 1, True, False)
            rms(B - 1, 1)

        @block.vector
        def _(dve):
            dve.wait_ge(weights_in, ONE + NLOAD * DMA)
            nc.vector.tensor_scalar(gains[:], cols[:], D ** 0.5, None, ALU.mult).then_inc(setup, 1)
            b_q, b_o, b_g = rows[:, 0:D], rows[:, D:2 * D], rows[:, 2 * D:]

            def wide(row, n):
                return row.rearrange("p (a d) -> p a d", a=1).broadcast_to([P, TT, n])

            def normalise(i, n, x, ready, turned):
                dve.wait_ge(rstd_done[n], ONE + i + 1)
                dve.wait_ge(turned, ONE + i)
                for t in range(TT):
                    last = nc.vector.tensor_scalar(hn[n][:, t, :], x[:, t, :], rstd[:, n, t:t + 1], None, ALU.mult)
                last.then_inc(ready, 1)

            def heads(i, before, after):
                at = 6 * i
                grid = att[:].rearrange("p (u t) (h g) -> p u (t h) g", u=2, g=HEADS)
                half_max = att_max[:].rearrange("p (u h a) -> p u h a", u=2, a=1)

                def sum_qk(t):
                    dve.wait_ge(qk_multiplied, ONE + TT * i + t + 1)
                    nc.vector.tensor_reduce(att[:, t, :], prod[t % 3][:].rearrange("p (h d) -> p h d", d=HD),
                                            AX.X, ALU.add).then_inc(qk_summed, 1)

                def subtract_max(half):
                    dve.wait_ge(qk_summed, ONE + TT * i + 2 * half + 2)
                    nc.vector.tensor_reduce(att_max[:, 2 * HEADS * half:2 * HEADS * (half + 1)], grid[:, half], AX.X,
                                            ALU.max).then_inc(soft_step, 1)
                    dve.wait_ge(soft_step, ONE + at + 2 * half + 1)
                    nc.vector.tensor_tensor(grid[:, half], grid[:, half], half_max[:, half]
                                            .broadcast_to([P, 2 * HEADS, HEADS]), ALU.subtract).then_inc(soft_step, 1)

                def sum_av(t):
                    dve.wait_ge(av_multiplied, ONE + TT * i + t + 1)
                    nc.vector.tensor_reduce(y[:, t, :], prod[(TT + t) % 3][:].rearrange("p (h g) -> p h g", g=HEADS),
                                            AX.X, ALU.add).then_inc(av_summed, 1)

                def last_experts(start, stop):
                    if before:
                        add_experts(i - 1, start, stop)

                sum_qk(0)
                if before:
                    normalise(i - 1, 1, x1, h2_ready, h2_turned)
                sum_qk(1)
                if before:
                    gates(i - 1)
                subtract_max(0)
                last_experts(0, 3)
                sum_qk(2)
                last_experts(3, 7)
                sum_qk(3)
                subtract_max(1)
                last_experts(7, 11)
                if after:
                    first(i + 1)
                dve.wait_ge(exped, ONE + 2 * (i + 1))
                nc.vector.tensor_reduce(att_inv[:], att[:].rearrange("p t (h g) -> p (t h) g", g=HEADS), AX.X,
                                        ALU.add).then_inc(soft_step, 1)
                dve.wait_ge(soft_step, ONE + at + 5)
                nc.vector.reciprocal(att_inv[:], att_inv[:]).then_inc(soft_step, 1)
                dve.wait_ge(y_turned, ONE + i)
                sum_av(0)
                last_experts(11, PAIRS * TT)
                sum_av(1)
                sum_av(2)
                if after:
                    queries(i + 1)
                sum_av(3)
                dve.wait_ge(av_summed, ONE + TT * (i + 1))
                dve.wait_ge(soft_step, ONE + at + 6)
                yr = y[:].rearrange("p t (h d) -> p (t h) d", d=HD)
                nc.vector.tensor_tensor(yr, yr, att_inv[:].rearrange("p (h a) -> p h a", a=1)
                                        .broadcast_to([P, TT * HEADS, HD]), ALU.mult).then_inc(y_ready, 1)
                output(i)

            def queries(i):
                dve.wait_ge(q_done, ONE + i + 1)
                dve.wait_ge(qk_multiplied, ONE + TT * i)
                nc.vector.tensor_tensor(q[:], ps_q[:], wide(b_q, D), ALU.add).then_inc(q_ready, 1)

            def output(i):
                dve.wait_ge(o_done, ONE + i + 1)
                dve.wait_ge(square_done[1], ONE + i)
                nc.vector.tensor_tensor(x1[:], ps_q[:], wide(b_o, D), ALU.add).then_inc(x1_step, 1)
                dve.wait_ge(x1_step, ONE + i + 1)
                dve.wait_ge(xn_again_in, ONE + DMA * (i + 1))
                nc.vector.tensor_tensor(x1[:], x1[:], xn_again[:], ALU.add).then_inc(x1_ready, 1)
                dve.wait_ge(x1_ready, ONE + i + 1)
                xb = x_res[:, bass.ds(TT * i, TT), :]
                nc.vector.tensor_tensor(xb, xb, x1[:], ALU.add).then_inc(x1_added, 1)

            def gates(i):
                at = 6 * i
                dve.wait_ge(gate_logits, ONE + i + 1)
                raw = ps_t[:, 0, 0:TT * EXPERTS3].rearrange("p (t e) -> p t e", t=TT)
                nc.vector.tensor_tensor(gate[:], raw, wide(b_g, EXPERTS3), ALU.add).then_inc(gate_step, 1)
                dve.wait_ge(gate_step, ONE + at + 1)
                nc.vector.tensor_reduce(gate_max[:], gate[:], AX.X, ALU.max).then_inc(gate_step, 1)
                dve.wait_ge(gate_step, ONE + at + 2)

                def by_tile():
                    return gate_max[:].rearrange("p (t a) -> p t a", a=1).broadcast_to([P, TT, EXPERTS3])
                nc.vector.tensor_tensor(gate[:], gate[:], by_tile(), ALU.subtract).then_inc(gate_step, 1)
                dve.wait_ge(gate_exped, ONE + i + 1)
                nc.vector.tensor_reduce(gate_max[:], gate[:], AX.X, ALU.add).then_inc(gate_step, 1)
                dve.wait_ge(gate_step, ONE + at + 4)
                nc.vector.reciprocal(gate_max[:], gate_max[:]).then_inc(gate_step, 1)
                dve.wait_ge(gate_step, ONE + at + 5)
                nc.vector.tensor_tensor(gate[:], gate[:], by_tile(), ALU.mult).then_inc(gate_step, 1)

            def add_experts(i, start, stop):
                dve.wait_ge(x1_added, ONE + i + 1)
                dve.wait_ge(gate_step, ONE + 6 * (i + 1))
                for n in range(start, stop):
                    pair, t = n // TT, n % TT
                    done = PAIRS * TT * i + n
                    dve.wait_ge(expert_done, ONE + done + 1)
                    xb = x_res[:, bass.ds(TT * i + t, 1), :].rearrange("p a d -> p (a d)")
                    for e in range(2):
                        if n or e:
                            dve.wait_ge(expert_added, ONE + 2 * done + e)
                        nc.vector.scalar_tensor_tensor(out=xb, in0=ps_e[n % 2][:, e * D:(e + 1) * D],
                                                       scalar=gate[:, t, 2 * pair + e:2 * pair + e + 1], in1=xb,
                                                       op0=ALU.mult, op1=ALU.add).then_inc(expert_added, 1)

            def first(i):
                normalise(i, 0, xn, h1_ready, h1_turned)

            first(0)
            queries(0)
            heads(0, False, True)
            with dve.Fori(1, B - 1) as i:
                heads(i, True, True)
            heads(B - 1, True, False)
            normalise(B - 1, 1, x1, h2_ready, h2_turned)
            gates(B - 1)
            add_experts(B - 1, 0, PAIRS * TT)

        @block.scalar
        def _(act):
            act.wait_ge(weights_in, ONE + NLOAD * DMA)
            act.wait_ge(setup, ONE + 1)

            def squares_of(x, n, i):
                act.wait_ge(square_done[n], ONE + i)
                act.wait_ge(rstd_done[n], ONE + i)
                for t in range(TT):
                    last = nc.scalar.activation(squares[:, n, t, :], x[:, t, :], ACT.Square, accum_out=square_sum[:, n, t:t + 1])
                last.then_inc(square_done[n], 1)

            def turned_out(i, n, turned, ready):
                act.wait_ge(turned, ONE + i + 1)
                for k in range(KD):
                    last = nc.scalar.activation(hT[n][:, k, :], ps_t[:, k, :], ACT.Copy, scale=gains[:, k, n:n + 1])
                last.then_inc(ready, 1)

            def squares_of_xn(i):
                act.wait_ge(xn_in, ONE + DMA * (i + 1))
                squares_of(xn, 0, i)

            def first(i):
                turned_out(i, 0, h1_turned, h1T_ready)
                act.wait_ge(down_done, ONE + i + 1)
                nc.scalar.activation(downT[:], ps_kv[0][:], ACT.Identity, bias=b_down[:, 0:1]).then_inc(downT_ready, 1)
                for t in range(TT):
                    act.wait_ge(kv_done, ONE + TT * i + t + 1)
                    if isinstance(i, int) and i == 0:
                        nc.scalar.copy(kv[:, t, :], ps_kv[(t + 1) % 2][:]).then_inc(kv_ready, 1)
                        continue
                    act.wait_ge(av_multiplied, ONE + TT * (i - 1) + t + 1)
                    nc.scalar.copy(kv[:, t, :], ps_kv[(t + 1) % 2][:]).then_inc(kv_ready, 1)

            def gates(i):
                turned_out(i, 1, h2_turned, h2T_ready)
                act.wait_ge(gate_step, ONE + 6 * i + 3)
                nc.scalar.activation(gate[:], gate[:], ACT.Exp).then_inc(gate_exped, 1)

            def exp_half(i, half):
                act.wait_ge(soft_step, ONE + 6 * i + 2 * half + 2)
                nc.scalar.activation(att[:, 2 * half:2 * half + 2, :], att[:, 2 * half:2 * half + 2, :], ACT.Exp,
                                     scale=HD ** -0.5).then_inc(exped, 1)

            def heads(i, before, after):
                if before:
                    gates(i - 1)
                exp_half(i, 0)
                if after:
                    squares_of_xn(i + 1)
                exp_half(i, 1)
                if after:
                    first(i + 1)
                act.wait_ge(y_turned, ONE + i + 1)
                nc.scalar.copy(ynT[:], ps_t[:]).then_inc(ynT_ready, 1)
                act.wait_ge(x1_ready, ONE + i + 1)
                squares_of(x1, 1, i)

            squares_of_xn(0)
            first(0)
            heads(0, False, True)
            with act.Fori(1, B - 1) as i:
                heads(i, True, True)
            heads(B - 1, True, False)
            gates(B - 1)

        @block.tensor
        def _(pe):
            pe.wait_ge(weights_in, ONE + NLOAD * DMA)

            def turn(rows_of, done):
                for k in range(KD):
                    for t in range(TT):
                        last = nc.tensor.transpose(ps_t[:, k, t * P:(t + 1) * P], rows_of[:, t, k * P:(k + 1) * P], ident[:])
                last.then_inc(done, 1)

            def project(rows_T, w, done):
                for t in range(TT):
                    for k in range(KD):
                        last = nc.tensor.matmul(ps_q[:, t, :], rows_T[:, k, t * P:(t + 1) * P], w[:, k, :],
                                                start=(k == 0), stop=(k == KD - 1))
                last.then_inc(done, 1)

            def first(i):
                pe.wait_ge(h1_ready, ONE + i + 1)
                turn(hn[0], h1_turned)
                pe.wait_ge(h1T_ready, ONE + i + 1)
                pe.wait_ge(kv_ready, ONE + TT * i)
                for k in range(KD):
                    last = nc.tensor.matmul(ps_kv[0][:], w_down[:, k, :], hT[0][:, k, :], start=(k == 0), stop=(k == KD - 1))
                last.then_inc(down_done, 1)
                pe.wait_ge(q_ready, ONE + i)
                project(hT[0], w_q, q_done)
                pe.wait_ge(downT_ready, ONE + i + 1)
                for t in range(TT):
                    if t >= 2:
                        pe.wait_ge(kv_ready, ONE + TT * i + t - 1)
                    nc.tensor.matmul(ps_kv[(t + 1) % 2][:], downT[:, t * P:(t + 1) * P], w_up[:],
                                     start=True, stop=True).then_inc(kv_done, 1)

            def heads(i, before, after):
                if before:
                    gates(i - 1)
                    experts(i - 1)
                if after:
                    first(i + 1)
                pe.wait_ge(y_ready, ONE + i + 1)
                turn(y, y_turned)
                pe.wait_ge(ynT_ready, ONE + i + 1)
                pe.wait_ge(q_ready, ONE + i + (2 if after else 1))
                project(ynT, w_o, o_done)

            def gates(i):
                pe.wait_ge(h2_ready, ONE + i + 1)
                turn(hn[1], h2_turned)
                pe.wait_ge(h2T_ready, ONE + i + 1)
                for t in range(TT):
                    for k in range(KD):
                        last = nc.tensor.matmul(ps_t[:, 0, t * EXPERTS3:(t + 1) * EXPERTS3], hT[1][:, k, t * P:(t + 1) * P],
                                                w_g[:, k, :], start=(k == 0), stop=(k == KD - 1))
                last.then_inc(gate_logits, 1)

            def experts(i):
                pe.wait_ge(gate_step, ONE + 6 * i + 1)
                for n in range(PAIRS * TT):
                    pair, t = n // TT, n % TT
                    done = PAIRS * TT * i + n
                    if n >= 2:
                        pe.wait_ge(expert_added, ONE + 2 * (done - 1))
                    else:
                        pe.wait_ge(expert_added, ONE + 2 * PAIRS * TT * i)
                    for k in range(KD):
                        last = nc.tensor.matmul(ps_e[n % 2][:], hT[1][:, k, t * P:(t + 1) * P],
                                                w_e[:, k, 2 * pair * D:2 * (pair + 1) * D], start=(k == 0), stop=(k == KD - 1))
                    last.then_inc(expert_done, 1)

            first(0)
            heads(0, False, True)
            with pe.Fori(1, B - 1) as i:
                heads(i, True, True)
            heads(B - 1, True, False)
            gates(B - 1)
            experts(B - 1)


class Names:
    pass


def build_program(nc, io):
    with ExitStack() as stack:
        keep = Names()
        room = Room(nc, stack, "all")
        keep.ident = room.sb("ident", P)
        keep.neg_half = room.sb("neg_half", 2 * P)
        keep.eps = room.sb("eps", TT)
        keep.always = room.sem("always")
        keep.x_res = room.sb("x_res", NT, D)
        load_constants(nc, io, keep)
        with ExitStack() as layer0:
            room0 = Room(nc, layer0, "l0")
            keep.scan = room0.sb("scan", T + 2, 2, KD * B)
            keep.comb = room0.sb("comb", NT, EXPERTS0 + 1)
            with ExitStack() as both:
                keep.xnT_all = Room(nc, both, "l0x").sb("xnT_all", KD, B * T)
                layer0_project(nc, io, keep)
                layer0_experts(nc, io, keep)
            layer0_mix(nc, io, keep)
        layer1(nc, io, keep)
        layer2(nc, io, keep)
        layer3(nc, io, keep)
        store_output(nc, io, keep)


def load_constants(nc, io, keep):
    with ExitStack() as stack:
        room = Room(nc, stack, "constants")
        loaded = room.sem("loaded")
        block = room.block()

        @block.sync
        def _(sp):
            sp.dma_start(keep.ident[:], io.ident).then_inc(loaded, DMA)
            sp.wait_ge(loaded, ONE + DMA)

        @block.gpsimd
        def _(pool):
            nc.gpsimd.memset(keep.neg_half[:], -0.5)
            nc.gpsimd.memset(keep.eps[:], LN_EPS).then_inc(keep.always, 1)


def layer2(nc, io, keep):
    layer2_attend(nc, io, keep)
    layer2_mix(nc, io, keep)


def layer3(nc, io, keep):
    layer3_attend(nc, io, keep)
    layer3_mix(nc, io, keep)


def store_output(nc, io, keep):
    with ExitStack() as stack:
        room = Room(nc, stack, "out")
        stored = room.sem("stored")
        block = room.block()

        @block.sync
        def _(sp):
            sp.dma_start(io.out.rearrange("b p t d -> p b t d"),
                         keep.x_res[:].rearrange("p (b t) d -> p b t d", b=B)).then_inc(stored, DMA)
            sp.wait_ge(stored, ONE + DMA)


def kernel(**a):
    from collections import namedtuple
    import numpy as np
    import concourse.bacc as bacc
    from concourse.bass_utils import run_bass_kernel_spmd as run

    a = {n: np.asarray(v) for n, v in a.items()}
    f4 = np.float32

    def k_major(w):
        return np.ascontiguousarray(w.reshape(-1, P, w.shape[-1]).transpose(1, 0, 2))

    def columns(*rows):
        return np.ascontiguousarray(np.stack([r.reshape(-1, P).T for r in rows], -1))

    def all_rows(row):
        return np.ascontiguousarray(np.broadcast_to(row, (P, row.size)))

    x = a["L0_attn_x"].reshape(B, TT, P, D).transpose(0, 2, 1, 3)
    data = {
        "x": x,
        "ident": np.eye(P, dtype=f4),
        "l0_w_kvr": k_major(np.concatenate([a["L0_attn_Wk"], a["L0_attn_Wv"], a["L0_attn_Wr"]], 1)),
        "l0_w_gate": k_major(a["L0_ffn_gate_w"].T),
        "l0_gate_b": all_rows(a["L0_ffn_gate_b"]),
        "l0_w13s": k_major(a["L0_ffn_w13_s"].T),
        "l0_w2s": a["L0_ffn_w2_s"].T,
        "l0_cols": columns(a["L0_attn_ln1_g"], a["L0_attn_ln1_b"], a["L0_attn_time_shift"].reshape(D), a["L0_attn_time_decay"]),
        "l0_w13": a["L0_ffn_w13"].transpose(0, 2, 1).reshape(EXPERTS0, KD, P, 2 * INTER0).transpose(0, 2, 1, 3),
        "l0_w2": a["L0_ffn_w2"].transpose(0, 2, 1),
        "l0_w_ck": k_major(a["L0_attn_Wck"]),
        "l0_w_cv": k_major(a["L0_attn_Wcv"]),
        "l0_w_cr": k_major(a["L0_attn_Wcr"]),
        "l0_cols2": columns(a["L0_attn_ln2_g"], a["L0_attn_ln2_b"], a["L0_attn_time_shift"].reshape(D), a["L0_attn_time_first"]),
    }
    by_head = np.arange(P) // HD
    data.update({
        "head_mask": (by_head[:, None] == np.arange(PER_BLOCK)[None, :]).astype(f4),
        "causal": np.triu(np.ones((P, P), f4)),
        "l1_w_qkv": k_major(np.concatenate([a["L1_attn_Wq"], a["L1_attn_Wk"], a["L1_attn_Wv"]], 0).T),
        "l1_w_o": k_major(a["L1_attn_Wo"].T),
        "l1_weight": k_major(a["L1_ffn_weight"].T),
        "l1_bias": all_rows(a["L1_ffn_bias"]),
        "l1_consts": np.stack([np.tile(a["L1_attn_gamma"], P // HD), np.tile(a["L1_attn_beta"], P // HD),
                               np.repeat(a["L1_ffn_alpha"], P)], -1),
    })
    w_q, w_k, w_v, w_f = np.split(a["L2_attn_W_qkvf"], 4, 0)
    data.update({
        "hide_later": np.triu(np.full((P, P), NEG, f4), 1),
        "l2_w_fqvk": k_major(np.concatenate([w_f, w_q, w_v, w_k], 0).T),
        "l2_w_proj": k_major(a["L2_attn_W_proj"].T),
        "l2_conv": a["L2_attn_W_conv"].transpose(0, 2, 1),
        "l2_cols": columns(a["L2_attn_ln1_g"], a["L2_attn_ln1_b"]),
        "l2_w_router": k_major(a["L2_ffn_router_w"].T),
        "l2_w_up": a["L2_ffn_up_proj"].reshape(EXPERTS2, KD, P, 2 * D).transpose(2, 0, 1, 3),
        "l2_w_down": a["L2_ffn_down_proj"].reshape(EXPERTS2, KD, P, D).transpose(2, 0, 1, 3),
        "l2_w_ff1": k_major(a["L2_attn_W_ff1"]),
        "l2_w_ff2": k_major(a["L2_attn_W_ff2"]),
        "l2_cols2": columns(a["L2_attn_ln2_g"], a["L2_attn_ln2_b"]),
    })
    zeros = np.zeros((P - LATENT - 1, 2 * D), f4)
    data.update({
        "l3_w_qkv": k_major(a["L3_attn_W_qkv"]),
        "l3_cols": columns(*np.split(a["L3_attn_b_qkv"], 3), *a["L3_attn_W_vconv"].T),
        "l3_w_q": k_major(a["L3_ffn_Wq"]),
        "l3_w_down": k_major(np.concatenate([a["L3_ffn_Wdown"], np.zeros((D, P - LATENT), f4)], 1)),
        "l3_w_up": np.concatenate([a["L3_ffn_Wup"], a["L3_ffn_bup"][None], zeros], 0),
        "l3_b_down": np.concatenate([a["L3_ffn_bdown"], np.ones(1, f4), zeros[:, 0]])[:, None],
        "l3_w_o": k_major(a["L3_ffn_Wo"]),
        "l3_w_g": k_major(a["L3_ffn_Wg"]),
        "l3_w_e": k_major(a["L3_ffn_We"].transpose(1, 0, 2).reshape(D, EXPERTS3 * D)),
        "l3_rows": all_rows(np.concatenate([a["L3_ffn_bq"], a["L3_ffn_bo"], a["L3_ffn_bg"]])),
        "l3_cols2": columns(a["L3_ffn_gamma1"], a["L3_ffn_gamma2"]),
    })
    nc = bacc.Bacc("TRN2", target_bir_lowering=False, num_devices=1)
    data = {name: np.ascontiguousarray(value) for name, value in data.items()}
    shapes = {"out": (B, P, TT, D), "xn_scratch": (B, P, TT, D), "x1_scratch": (B, P, TT, D),
              "xn3_scratch": (B, P, TT, D), "v_scratch": (B, P, KD, T), "r_scratch": (B, P, KD, T)}
    dram = {name: nc.dram_tensor(name, value.shape, F32, kind="ExternalInput").ap() for name, value in data.items()}
    dram["out"] = nc.dram_tensor("out", shapes.pop("out"), F32, kind="ExternalOutput").ap()
    dram.update({name: nc.dram_tensor(name, shape, F32).ap() for name, shape in shapes.items()})
    io = namedtuple("Dram", dram)(**dram)
    build_program(nc, io)
    got = run(nc, [data], core_ids=[0]).results[0]["out"]
    return got.reshape(B, P, TT, D).transpose(0, 2, 1, 3).reshape(B, T, D)
```

```python
from contextlib import ExitStack

import concourse.bass as bass
from concourse import mybir

F32 = mybir.dt.float32
ALU = mybir.AluOpType
ACT = mybir.ActivationFunctionType
AX = mybir.AxisListType

P = 128
B, T, D = 8, 512, 256
KD = D // P
TT = T // P
NT = B * TT
LN_EPS = 1e-5
ONE = 1
DMA = 16


class Room:

    def __init__(self, nc, stack, phase):
        self.nc, self.stack, self.phase = nc, stack, phase
        self.sems = []
        stack.callback(self.clear)

    def block(self):
        nc = self.nc
        for n, sem in enumerate(self.sems):
            (nc.sync, nc.tensor, nc.scalar, nc.vector, nc.gpsimd)[n % 5].sem_inc(sem, ONE)
        self.nc.all_engine_barrier()
        return self.stack.enter_context(self.nc.Block())

    def clear(self):
        if self.sems:
            nc = self.nc
            for n, sem in enumerate(self.sems):
                (nc.sync, nc.tensor, nc.scalar, nc.vector, nc.gpsimd)[n % 5].sem_clear(sem)
            self.nc.all_engine_barrier()

    def sb(self, name, *shape):
        return self.stack.enter_context(self.nc.sbuf_tensor(f"{self.phase}_{name}", [P, *shape], F32))

    def ps(self, name, *shape):
        return self.stack.enter_context(self.nc.psum_tensor(f"{self.phase}_{name}", [P, *shape], F32))

    def sem(self, name):
        self.sems.append(self.stack.enter_context(self.nc.semaphore(f"{self.phase}_{name}")))
        return self.sems[-1]


def wait_apart(engine, always, sem, value):
    value = ONE + value
    if not isinstance(value, int):
        value = engine.to_reg(value)
    engine.wait_ge(always, 1)
    engine.wait_ge(sem, value)


class LayerNorm:

    def __init__(self, nc, room, name, keep, eps=None):
        self.nc, self.neg_half = nc, keep.neg_half
        self.eps = keep.eps if eps is None else eps
        self.always = keep.always
        self.stats = room.sb(f"{name}_stats", TT, 6)
        self.moments = room.sb(f"{name}_moments", TT, 2)
        self.var_eps = room.sb(f"{name}_var_eps", TT)
        self.rstd = room.sb(f"{name}_rstd", TT)
        self.stats_done = room.sem(f"{name}_stats_done")
        self.moments_done = room.sem(f"{name}_moments_done")
        self.eps_added = room.sem(f"{name}_eps_added")
        self.rstd_done = room.sem(f"{name}_rstd_done")

    def vector_moments(self, dve, x, count):
        for t in range(TT):
            last = self.nc.vector.bn_stats(self.stats[:, t, :], x(t))
        last.then_inc(self.stats_done, 1)
        wait_apart(dve, self.always, self.stats_done, count + 1)
        for t in range(TT):
            last = self.nc.vector.bn_aggr(self.moments[:, t, :], self.stats[:, t, :])
        last.then_inc(self.moments_done, 1)

    def pool_rstd(self, pool, count):
        pool.wait_ge(self.moments_done, ONE + count + 1)
        self.nc.gpsimd.tensor_tensor(self.var_eps[:], self.moments[:, :, 1], self.eps[:, 0:TT],
                                     ALU.add).then_inc(self.eps_added, 1)
        pool.wait_ge(self.eps_added, ONE + count + 1)
        self.nc.gpsimd.tensor_tensor(self.rstd[:], self.var_eps[:], self.neg_half[:, 0:TT],
                                     ALU.pow).then_inc(self.rstd_done, 1)

    def vector_apply(self, dve, x, out, count):
        dve.wait_ge(self.rstd_done, ONE + count + 1)
        for t in range(TT):
            last = self.nc.vector.tensor_scalar(out(t), x(t), self.moments[:, t, 0:1],
                                                self.rstd[:, t:t + 1], ALU.subtract, ALU.mult)
        return last

EXPERTS0, INTER0, TOP0, ROUTE_SCALE = 16, 128, 4, 2.5
RATIO_MAX = 1e24


def layer0_project(nc, io, keep):
    with ExitStack() as stack:
        room = Room(nc, stack, "p0")
        ident, x_res, xnT_all, comb, scan = (
            keep.ident, keep.x_res, keep.xnT_all, keep.comb, keep.scan)
        w_kvr = room.sb("w_kvr", KD, 3 * D)
        w_gate = room.sb("w_gate", KD, EXPERTS0)
        gate_b = room.sb("gate_b", EXPERTS0)
        w13s = room.sb("w13s", KD, 2 * INTER0)
        w2s = room.sb("w2s", D)
        cols = room.sb("cols", KD, 4)
        xn = room.sb("xn", TT, D)
        hn = room.sb("hn", TT, D)
        xnT = room.sb("xnT", KD, T)
        hT = room.sb("hT", KD, T + 1)
        k_sb = room.sb("k_sb", KD, T + 1)
        dk = room.sb("dk", KD, T)
        v_sb = room.sb("v_sb", KD, T)
        r_sb = room.sb("r_sb", KD, T)
        scores = room.sb("scores", TT, EXPERTS0)
        biased = room.sb("biased", TT, EXPERTS0)
        top = room.sb("top", TT, 8)
        picked = room.sb("picked", TT, EXPERTS0)
        picked_sum = room.sb("picked_sum", TT)
        picked_inv = room.sb("picked_inv", TT)
        silu_g = room.sb("silu_g", T)
        hidden = room.sb("hidden", T)
        ps_x = room.ps("ps_x", KD, T)
        ps_h = room.ps("ps_h", KD, T)
        ps_k = room.ps("ps_k", KD, T)
        ps_v = room.ps("ps_v", KD, T)
        ln_a = LayerNorm(nc, room, "ln_a", keep)
        ln_b = LayerNorm(nc, room, "ln_b", keep)
        weights_in, cols_in, x_in = room.sem("weights_in"), room.sem("cols_in"), room.sem("x_in")
        xn_saved, v_saved, r_saved = room.sem("xn_saved"), room.sem("v_saved"), room.sem("r_saved")
        setup_done = room.sem("setup_done")
        xn_ready, hn_ready = room.sem("xn_ready"), room.sem("hn_ready")
        xn_turned, hn_turned = room.sem("xn_turned"), room.sem("hn_turned")
        xnT_ready, xnT_kept, hT_ready = room.sem("xnT_ready"), room.sem("xnT_kept"), room.sem("hT_ready")
        projected = room.sem("projected")
        k_out, v_out, r_out = room.sem("k_out"), room.sem("v_out"), room.sem("r_out")
        gated, scores_ready, routed = room.sem("gated"), room.sem("scores_ready"), room.sem("routed")
        route_step = room.sem("route_step")
        dk_ready, decayed = room.sem("dk_ready"), room.sem("decayed")
        up_done, silu_ready = room.sem("up_done"), room.sem("silu_ready")
        hidden_ready, down_done, shared_added = room.sem("hidden_ready"), room.sem("down_done"), room.sem("shared_added")
        block = room.block()

        def x_tiles(i, t):
            return x_res[:, bass.ds(TT * i + t, 1), :].rearrange("p a d -> p (a d)")

        @block.sync
        def _(sp):
            def load_x(i):
                sp.dma_start(x_res[:, bass.ds(TT * i, TT), :],
                             io.x[bass.ds(i, 1)].rearrange("a p t d -> p (a t) d")).then_inc(x_in, DMA)

            load_x(0)
            sp.dma_start(cols[:], io.l0_cols).then_inc(cols_in, DMA)
            n = 0
            for dst, src in ((w_kvr[:], io.l0_w_kvr),
                             (w_gate[:], io.l0_w_gate), (gate_b[:], io.l0_gate_b), (w13s[:], io.l0_w13s),
                             (w2s[:], io.l0_w2s)):
                sp.dma_start(dst, src).then_inc(weights_in, DMA)
                n += 1
            assert n == 5

            def save(i):
                sp.wait_ge(hn_ready, ONE + i + 1)
                sp.dma_start(io.xn_scratch[bass.ds(i, 1)].rearrange("a p t d -> p (a t) d"),
                             xn[:]).then_inc(xn_saved, DMA)
                sp.wait_ge(v_out, ONE + i + 1)
                sp.dma_start(io.v_scratch[bass.ds(i, 1)].rearrange("a p k t -> p (a k) t"),
                             v_sb[:]).then_inc(v_saved, DMA)
                sp.wait_ge(r_out, ONE + i + 1)
                sp.dma_start(io.r_scratch[bass.ds(i, 1)].rearrange("a p k t -> p (a k) t"),
                             r_sb[:]).then_inc(r_saved, DMA)

            with sp.Fori(0, B - 1) as i:
                sp.wait_ge(x_in, ONE + DMA * (i + 1))
                load_x(i + 1)
                save(i)
            save(B - 1)
            for done in (xn_saved, v_saved, r_saved):
                sp.wait_ge(done, ONE + DMA * B)

        @block.vector
        def _(dve):
            nc.vector.memset(k_sb[:, :, T:T + 1], 0.0).then_inc(setup_done, 1)
            nc.vector.memset(comb[:], 1.0).then_inc(setup_done, 1)
            dve.wait_ge(cols_in, ONE + DMA)
            nc.vector.tensor_copy(hT[:, :, 0:1], cols[:, :, 2:3]).then_inc(setup_done, 1)
            nc.vector.memset(scan[:, 0, 0, :], 0.0).then_inc(setup_done, 1)
            nc.vector.memset(scan[:, 1, 1, :], 1.0).then_inc(setup_done, 1)

            def norms(i):
                dve.wait_ge(x_in, ONE + DMA * (i + 1))
                ln_a.vector_moments(dve, lambda t: x_tiles(i, t), i)
                dve.wait_ge(xn_turned, ONE + i)
                dve.wait_ge(xn_saved, ONE + DMA * i)
                ln_a.vector_apply(dve, lambda t: x_tiles(i, t), lambda t: xn[:, t, :], i).then_inc(xn_ready, 1)
                dve.wait_ge(xn_ready, ONE + i + 1)
                ln_b.vector_moments(dve, lambda t: xn[:, t, :], i)
                dve.wait_ge(hn_turned, ONE + i)
                ln_b.vector_apply(dve, lambda t: xn[:, t, :], lambda t: hn[:, t, :], i).then_inc(hn_ready, 1)

            def rest(i):
                dve.wait_ge(xnT_ready, ONE + i + 1)
                nc.vector.tensor_copy(xnT_all[:, :, bass.ds(i * T, T)], ps_x[:]).then_inc(xnT_kept, 1)
                dve.wait_ge(scores_ready, ONE + i + 1)
                for t in range(TT):
                    last = nc.vector.tensor_tensor(biased[:, t, :], scores[:, t, :], gate_b[:], ALU.add)
                last.then_inc(route_step, 1)
                dve.wait_ge(route_step, ONE + 4 * i + 1)
                dve.wait_ge(k_out, ONE + i + 1)
                dve.wait_ge(decayed, ONE + i)
                nc.vector.tensor_tensor(dk[:], k_sb[:, :, 0:T], k_sb[:, :, 1:T + 1],
                                        ALU.subtract).then_inc(dk_ready, 1)
                for t in range(TT):
                    last = nc.vector.max(top[:, t, :], biased[:, t, :])
                last.then_inc(route_step, 1)
                dve.wait_ge(route_step, ONE + 4 * i + 2)
                for t in range(TT):
                    last = nc.vector.scalar_tensor_tensor(
                        out=picked[:, t, :], in0=biased[:, t, :], scalar=top[:, t, TOP0 - 1:TOP0],
                        in1=scores[:, t, :], op0=ALU.is_ge, op1=ALU.mult, accum_out=picked_sum[:, t:t + 1])
                last.then_inc(route_step, 1)
                dve.wait_ge(route_step, ONE + 4 * i + 3)
                nc.vector.reciprocal(picked_inv[:], picked_sum[:]).then_inc(route_step, 1)
                dve.wait_ge(route_step, ONE + 4 * i + 4)
                for t in range(TT):
                    last = nc.vector.tensor_scalar(
                        comb[:, bass.ds(TT * i + t, 1), 0:EXPERTS0].rearrange("p a e -> p (a e)"),
                        picked[:, t, :], picked_inv[:, t:t + 1], ROUTE_SCALE, ALU.mult, ALU.mult)
                last.then_inc(routed, 1)
                dve.wait_ge(silu_ready, ONE + i + 1)
                dve.wait_ge(down_done, ONE + i)
                nc.vector.tensor_tensor(hidden[:], silu_g[:], ps_k[:, 1, :], ALU.mult).then_inc(hidden_ready, 1)
                dve.wait_ge(down_done, ONE + i + 1)
                xb = x_res[:, bass.ds(TT * i, TT), :].rearrange("p a d -> p (a d)")
                nc.vector.tensor_tensor(xb, xb, ps_v[:].rearrange("p a d -> p (a d)"), ALU.add).then_inc(shared_added, 1)

            norms(0)
            with dve.Fori(0, B - 1) as i:
                norms(i + 1)
                rest(i)
            rest(B - 1)

        @block.gpsimd
        def _(pool):
            with pool.Fori(0, B) as i:
                ln_a.pool_rstd(pool, i)
                ln_b.pool_rstd(pool, i)

        @block.scalar
        def _(act):
            act.wait_ge(cols_in, ONE + DMA)
            act.wait_ge(setup_done, ONE + 5)

            def rows_turned(i):
                act.wait_ge(hn_turned, ONE + i + 1)
                act.wait_ge(projected, ONE + 3 * i)
                for k in range(KD):
                    last = nc.scalar.activation(hT[:, k, 1:T + 1], ps_h[:, k, :], ACT.Identity,
                                                bias=cols[:, k, 1:2], scale=cols[:, k, 0:1])
                last.then_inc(hT_ready, 1)
                act.wait_ge(xn_turned, ONE + i + 1)
                act.wait_ge(up_done, ONE + i)
                nc.scalar.copy(xnT[:], ps_x[:]).then_inc(xnT_ready, 1)

            def results(i):
                act.wait_ge(projected, ONE + 3 * i + 1)
                act.wait_ge(dk_ready, ONE + i)
                nc.scalar.copy(k_sb[:, :, 0:T], ps_k[:]).then_inc(k_out, 1)
                act.wait_ge(projected, ONE + 3 * i + 2)
                act.wait_ge(v_saved, ONE + DMA * i)
                nc.scalar.copy(v_sb[:], ps_v[:]).then_inc(v_out, 1)
                act.wait_ge(projected, ONE + 3 * i + 3)
                act.wait_ge(r_saved, ONE + DMA * i)
                nc.scalar.activation(r_sb[:], ps_h[:], ACT.Sigmoid).then_inc(r_out, 1)
                act.wait_ge(gated, ONE + i + 1)
                act.wait_ge(routed, ONE + i)
                nc.scalar.activation(scores[:], ps_x[:, 0, 0:TT * EXPERTS0].rearrange("p (t e) -> p t e", t=TT),
                                     ACT.Sigmoid).then_inc(scores_ready, 1)
                act.wait_ge(up_done, ONE + i + 1)
                act.wait_ge(hidden_ready, ONE + i)
                nc.scalar.activation(silu_g[:], ps_k[:, 0, :], ACT.Silu).then_inc(silu_ready, 1)

            def decays(i):
                act.wait_ge(dk_ready, ONE + i + 1)
                for k in range(KD):
                    last = nc.scalar.activation(
                        scan[:, 1:T + 1, 0, bass.ds(B * k + i, 1)].rearrange("p t a -> p (t a)"), dk[:, k, :],
                        ACT.Exp, bias=cols[:, k, 3:4])
                last.then_inc(decayed, 1)

            rows_turned(0)
            results(0)
            with act.Fori(1, B) as i:
                rows_turned(i)
                decays(i - 1)
                results(i)
            decays(B - 1)

        @block.tensor
        def _(pe):
            pe.wait_ge(weights_in, ONE + 5 * DMA)
            pe.wait_ge(setup_done, ONE + 5)

            def turn_rows(i):
                pe.wait_ge(xn_ready, ONE + i + 1)
                pe.wait_ge(scores_ready, ONE + i)
                for k in range(KD):
                    for t in range(TT):
                        last = nc.tensor.transpose(ps_x[:, k, t * P:(t + 1) * P], xn[:, t, k * P:(k + 1) * P], ident[:])
                last.then_inc(xn_turned, 1)
                pe.wait_ge(hn_ready, ONE + i + 1)
                pe.wait_ge(r_out, ONE + i)
                for k in range(KD):
                    for t in range(TT):
                        last = nc.tensor.transpose(ps_h[:, k, t * P:(t + 1) * P], hn[:, t, k * P:(k + 1) * P], ident[:])
                last.then_inc(hn_turned, 1)

            def products(i):
                pe.wait_ge(hT_ready, ONE + i + 1)
                pe.wait_ge(silu_ready, ONE + i)
                pe.wait_ge(hidden_ready, ONE + i)
                for n, ps in enumerate((ps_k, ps_v, ps_h)):
                    if n == 1:
                        pe.wait_ge(shared_added, ONE + i)
                    for m in range(KD):
                        for k in range(KD):
                            last = nc.tensor.matmul(ps[:, m, :], w_kvr[:, k, n * D + m * P:n * D + (m + 1) * P],
                                                    hT[:, k, 0:T], start=(k == 0), stop=(k == KD - 1))
                    last.then_inc(projected, 1)
                pe.wait_ge(xnT_ready, ONE + i + 1)
                pe.wait_ge(xnT_kept, ONE + i + 1)
                for t in range(TT):
                    for k in range(KD):
                        last = nc.tensor.matmul(ps_x[:, 0, t * EXPERTS0:(t + 1) * EXPERTS0], xnT[:, k, t * P:(t + 1) * P],
                                                w_gate[:, k, :], start=(k == 0), stop=(k == KD - 1))
                last.then_inc(gated, 1)
                pe.wait_ge(k_out, ONE + i + 1)
                for m in range(2):
                    for k in range(KD):
                        last = nc.tensor.matmul(ps_k[:, m, :], w13s[:, k, m * INTER0:(m + 1) * INTER0], xnT[:, k, :],
                                                start=(k == 0), stop=(k == KD - 1))
                last.then_inc(up_done, 1)

            def shared_down(i):
                pe.wait_ge(hidden_ready, ONE + i + 1)
                pe.wait_ge(v_out, ONE + i + 1)
                for t in range(TT):
                    last = nc.tensor.matmul(ps_v[:].rearrange("p a b -> p (a b)")[:, t * D:(t + 1) * D],
                                            hidden[:, t * P:(t + 1) * P], w2s[:], start=True, stop=True)
                last.then_inc(down_done, 1)

            turn_rows(0)
            products(0)
            with pe.Fori(1, B) as i:
                turn_rows(i)
                shared_down(i - 1)
                products(i)
            shared_down(B - 1)


def layer0_experts(nc, io, keep):
    UNIT_STEPS = T // (EXPERTS0 * B)
    with ExitStack() as stack:
        room = Room(nc, stack, "p1")
        x_res, xnT_all, comb, scan = keep.x_res, keep.xnT_all, keep.comb, keep.scan
        w13 = [room.sb(f"w13_{n}", KD, 2 * INTER0) for n in range(2)]
        w2 = [room.sb(f"w2_{n}", D) for n in range(2)]
        silu_g = [room.sb(f"silu_g{n}", T) for n in range(2)]
        up_rows = [room.sb(f"up_rows{n}", T) for n in range(2)]
        hidden = [room.sb(f"hidden{n}", T) for n in range(2)]
        new = room.sb("new", 2, KD * B)
        ratio = room.sb("ratio", KD * B)
        ps_gu = [room.ps(f"ps_gu{n}", 2, T) for n in range(2)]
        ps_y = [room.ps(f"ps_y{n}", TT, D) for n in range(2)]
        weights_in = [room.sem(f"weights_in{n}") for n in range(2)]
        up_done, silu_ready = room.sem("up_done"), room.sem("silu_ready")
        hidden_ready = room.sem("hidden_ready")
        gu_free, y_free = room.sem("gu_free"), room.sem("y_free")
        down_done = room.sem("down_done")
        step = room.sem("step")
        block = room.block()

        @block.sync
        def _(sp):
            def load(e, n):
                sp.dma_start(w13[n][:], io.l0_w13[bass.ds(e, 1)].rearrange("e p k n -> p (e k) n")).then_inc(weights_in[n], DMA)
                sp.dma_start(w2[n][:], io.l0_w2[bass.ds(e, 1)].rearrange("e p d -> p (e d)")).then_inc(weights_in[n], DMA)

            load(0, 0)
            load(1, 1)
            with sp.Fori(0, EXPERTS0 // 2 - 1) as j:
                for n in range(2):
                    sp.wait_ge(down_done, ONE + B * (2 * j + n + 1) + 2)
                    load(2 * j + 2 + n, n)

        @block.vector
        def _(dve):
            dve.sem_inc(y_free, 2)

            def recurrence(t):
                nc.vector.scalar_tensor_tensor(
                    out=new[:], in0=scan[:, bass.ds(t, 1), 0, :].broadcast_to([P, 2, KD * B]), scalar=1.0,
                    in1=scan[:, bass.ds(t + 1, 1), :, :].rearrange("p a s c -> p (a s) c"),
                    op0=ALU.add, op1=ALU.mult).then_inc(step, 1)

            def recurrence_close(t):
                dve.wait_ge(step, ONE + 4 * t + 1)
                nc.vector.tensor_scalar(ratio[:], new[:, 0, :], 1.0, RATIO_MAX, ALU.max, ALU.min).then_inc(step, 1)
                nc.vector.scalar_tensor_tensor(
                    out=scan[:, bass.ds(t + 1, 1), 0, :].rearrange("p a c -> p (a c)"), in0=new[:, 0, :],
                    scalar=RATIO_MAX, in1=new[:, 1, :], op0=ALU.min, op1=ALU.mult).then_inc(step, 1)

            def recurrence_invert(t):
                dve.wait_ge(step, ONE + 4 * t + 3)
                nc.vector.reciprocal(scan[:, bass.ds(t + 2, 1), 1, :].rearrange("p a c -> p (a c)"),
                                     ratio[:]).then_inc(step, 1)

            def combine(m, t, e, half=None):
                part = slice(0, D) if half is None else slice(half * D // 2, (half + 1) * D // 2)
                xb = x_res[:, TT * (m % B) + t, part]
                return nc.vector.scalar_tensor_tensor(
                    out=xb, in0=ps_y[m % 2][:, t, part],
                    scalar=comb[:, TT * (m % B) + t, bass.ds(e, 1)],
                    in1=xb, op0=ALU.mult, op1=ALU.add)

            def unit(j, m, with_sum):
                u = 2 * B * j + m
                for s in range(UNIT_STEPS):
                    t = UNIT_STEPS * u + s
                    recurrence(t)
                    if with_sum:
                        if s == 0:
                            dve.wait_ge(down_done, ONE + u + 1)
                        combine(m - 2, s, 2 * j + (m - 2) // B, 0)
                    recurrence_close(t)
                    if with_sum:
                        last = combine(m - 2, s, 2 * j + (m - 2) // B, 1)
                        if s == UNIT_STEPS - 1:
                            last.then_inc(y_free, 1)
                    recurrence_invert(t)
                    dve.wait_ge(step, ONE + 4 * t + 4)

            pairs, units = EXPERTS0 // 2, 2 * B
            unit(0, 0, False)
            unit(0, 1, False)
            with dve.Fori(0, pairs - 1) as j:
                for m in range(2, units + 2):
                    unit(j, m, True)
            for m in range(2, units):
                unit(pairs - 1, m, True)
            for m in (units - 2, units - 1):
                dve.wait_ge(down_done, ONE + units * (pairs - 1) + m + 3)
                for t in range(TT):
                    last = combine(m, t, 2 * (pairs - 1) + 1)
                last.then_inc(y_free, 1)

        @block.gpsimd
        def _(pool):
            pool.sem_inc(hidden_ready, 2)
            with pool.Fori(0, EXPERTS0 // 2) as j:
                for m in range(2 * B):
                    u = 2 * B * j + m
                    pool.wait_ge(silu_ready, ONE + u + 1)
                    pool.wait_ge(down_done, ONE + u + 1)
                    nc.gpsimd.tensor_tensor(hidden[m % 2][:], silu_g[m % 2][:], up_rows[m % 2][:],
                                            ALU.mult).then_inc(hidden_ready, 1)

        @block.scalar
        def _(act):
            act.sem_inc(gu_free, 2)
            with act.Fori(0, EXPERTS0 // 2) as j:
                for m in range(2 * B):
                    u = 2 * B * j + m
                    act.wait_ge(up_done, ONE + u + 1)
                    act.wait_ge(hidden_ready, ONE + u + 1)
                    nc.scalar.activation(silu_g[m % 2][:], ps_gu[m % 2][:, 0, :], ACT.Silu)
                    nc.scalar.copy(up_rows[m % 2][:], ps_gu[m % 2][:, 1, :]).then_inc(silu_ready, 1)
                    act.wait_ge(silu_ready, ONE + u + 1)
                    act.sem_inc(gu_free, 1)

        @block.tensor
        def _(pe):
            pe.sem_inc(down_done, 2)

            def up(j, m, n):
                pe.wait_ge(gu_free, ONE + 2 * B * j + m + 1)
                for half in range(2):
                    for k in range(KD):
                        last = nc.tensor.matmul(ps_gu[m % 2][:, half, :], w13[n][:, k, half * INTER0:(half + 1) * INTER0],
                                                xnT_all[:, k, (m % B) * T:(m % B + 1) * T],
                                                start=(k == 0), stop=(k == KD - 1))
                last.then_inc(up_done, 1)

            def down(j, m, n):
                pe.wait_ge(hidden_ready, ONE + 2 * B * j + m + 3)
                pe.wait_ge(y_free, ONE + 2 * B * j + m + 1)
                for t in range(TT):
                    last = nc.tensor.matmul(ps_y[m % 2][:, t, :], hidden[m % 2][:, t * P:(t + 1) * P], w2[n][:],
                                            start=True, stop=True)
                last.then_inc(down_done, 1)

            def unit(j, m, with_next):
                if with_next:
                    after = m + 1
                    if after % B == 0:
                        pe.wait_ge(weights_in[after // B % 2], ONE + 2 * DMA * (j + 1 + after // (2 * B)))
                    up(j, after, after // B % 2)
                down(j, m, m // B)

            pairs, units = EXPERTS0 // 2, 2 * B
            pe.wait_ge(weights_in[0], ONE + 2 * DMA)
            up(0, 0, 0)
            with pe.Fori(0, pairs - 1) as j:
                for m in range(units):
                    unit(j, m, True)
            for m in range(units):
                unit(pairs - 1, m, m < units - 1)


def layer0_mix(nc, io, keep):
    FF = 4 * D
    NF = FF // P
    with ExitStack() as stack:
        room = Room(nc, stack, "p2")
        ident, x_res, scan = keep.ident, keep.x_res, keep.scan
        w_ck = room.sb("w_ck", KD, FF)
        w_cv = room.sb("w_cv", NF, D)
        w_cr = room.sb("w_cr", KD, D)
        cols = room.sb("cols", KD, 4)
        bonus = room.sb("bonus", KD)
        ones = room.sb("ones", 1)
        v_sb = room.sb("v_sb", KD, T)
        r_sb = room.sb("r_sb", KD, T)
        xn = room.sb("xn", TT, D)
        inv = room.sb("inv", KD, T)
        den = room.sb("den", KD, T)
        total = room.sb("total", KD, T + 1)
        y = room.sb("y", KD, T)
        x1 = room.sb("x1", TT, D)
        hn = room.sb("hn", TT, D)
        hT = room.sb("hT", KD, T + 1)
        kk = room.sb("kk", NF, T)
        rr = room.sb("rr", TT, D)
        mixed = room.sb("mixed", TT, D)
        ps_t = room.ps("ps_t", 2 * T)
        ps_kk = [room.ps(f"ps_kk{n}", T) for n in range(2)]
        ps_rr = room.ps("ps_rr", TT, D)
        ps_kv = room.ps("ps_kv", TT, D)
        ln = LayerNorm(nc, room, "ln", keep)
        weights_in, cols_in, setup_done = room.sem("weights_in"), room.sem("cols_in"), room.sem("setup_done")
        v_in, r_in, xn_in = room.sem("v_in"), room.sem("r_in"), room.sem("xn_in")
        q_read = room.sem("q_read")
        chain = room.sem("chain")
        y_ready, y_turned, x1_ready = room.sem("y_ready"), room.sem("y_turned"), room.sem("x1_ready")
        hn_ready, hn_turned, hT_ready = room.sem("hn_ready"), room.sem("hn_turned"), room.sem("hT_ready")
        kk_done, kk_relu, kk_ready = room.sem("kk_done"), room.sem("kk_relu"), room.sem("kk_ready")
        rr_done, rr_ready, kv_done = room.sem("rr_done"), room.sem("rr_ready"), room.sem("kv_done")
        mix_step, x1_added, batch_done = room.sem("mix_step"), room.sem("x1_added"), room.sem("batch_done")
        CHAIN = 6
        block = room.block()

        def q_at(i, k, first):
            return scan[:, first:first + T, 0, bass.ds(B * k + i, 1)].rearrange("p t a -> p (t a)")

        @block.sync
        def _(sp):
            def load_batch(i):
                sp.wait_ge(y_ready, ONE + i)
                sp.dma_start(v_sb[:], io.v_scratch[bass.ds(i, 1)].rearrange("a p k t -> p (a k) t")).then_inc(v_in, DMA)
                sp.dma_start(r_sb[:], io.r_scratch[bass.ds(i, 1)].rearrange("a p k t -> p (a k) t")).then_inc(r_in, DMA)
                sp.wait_ge(x1_ready, ONE + i)
                sp.dma_start(xn[:], io.xn_scratch[bass.ds(i, 1)].rearrange("a p t d -> p (a t) d")).then_inc(xn_in, DMA)

            sp.dma_start(cols[:], io.l0_cols2).then_inc(cols_in, DMA)
            load_batch(0)
            for dst, src in ((w_ck[:], io.l0_w_ck), (w_cr[:], io.l0_w_cr), (w_cv[:], io.l0_w_cv)):
                sp.dma_start(dst, src).then_inc(weights_in, DMA)
            with sp.Fori(1, B) as i:
                load_batch(i)

        @block.gpsimd
        def _(pool):
            pool.wait_ge(setup_done, ONE + 4)

            def read_q(i):
                pool.wait_ge(y_ready, ONE + i)
                for k in range(KD):
                    nc.gpsimd.tensor_tensor(inv[:, k, :], q_at(i, k, 0), ones[:, 0:1].broadcast_to([P, T]), ALU.add)
                    last = nc.gpsimd.tensor_tensor(den[:, k, :], q_at(i, k, 0),
                                                   bonus[:, k:k + 1].broadcast_to([P, T]), ALU.add)
                last.then_inc(q_read, 1)

            with pool.Fori(0, B) as i:
                read_q(i)
                ln.pool_rstd(pool, i)

        @block.vector
        def _(dve):
            dve.wait_ge(cols_in, ONE + DMA)
            nc.vector.tensor_copy(hT[:, :, 0:1], cols[:, :, 2:3]).then_inc(setup_done, 1)
            nc.vector.memset(total[:, :, 0:1], 0.0).then_inc(setup_done, 1)
            nc.vector.memset(ones[:], 1.0).then_inc(setup_done, 1)

            def values(i):
                dve.wait_ge(q_read, ONE + i + 1)
                dve.wait_ge(v_in, ONE + DMA * (i + 1))
                nc.vector.reciprocal(inv[:], inv[:]).then_inc(chain, 1)
                dve.wait_ge(chain, ONE + CHAIN * i + 1)
                for k in range(KD):
                    last = nc.vector.tensor_tensor(inv[:, k, :], inv[:, k, :], q_at(i, k, 1), ALU.mult)
                last.then_inc(chain, 1)
                nc.vector.reciprocal(den[:], den[:]).then_inc(chain, 1)
                dve.wait_ge(chain, ONE + CHAIN * i + 2)
                for k in range(KD):
                    last = nc.vector.tensor_tensor_scan(total[:, k, 1:T + 1], v_sb[:, k, :], inv[:, k, :], 0.0,
                                                        ALU.add, ALU.mult)
                last.then_inc(chain, 1)
                dve.wait_ge(chain, ONE + CHAIN * i + 4)
                dve.wait_ge(y_turned, ONE + i)
                for k in range(KD):
                    last = nc.vector.scalar_tensor_tensor(out=y[:, k, :], in0=v_sb[:, k, :], scalar=bonus[:, k:k + 1],
                                                          in1=total[:, k, 0:T], op0=ALU.mult, op1=ALU.add)
                last.then_inc(chain, 1)
                dve.wait_ge(chain, ONE + CHAIN * i + 5)
                nc.vector.tensor_tensor(y[:], y[:], den[:], ALU.mult).then_inc(chain, 1)
                dve.wait_ge(chain, ONE + CHAIN * i + 6)
                dve.wait_ge(r_in, ONE + DMA * (i + 1))
                nc.vector.tensor_tensor(y[:], y[:], r_sb[:], ALU.mult).then_inc(y_ready, 1)

            def rest(i):
                dve.wait_ge(y_turned, ONE + i + 1)
                dve.wait_ge(xn_in, ONE + DMA * (i + 1))
                dve.wait_ge(x1_added, ONE + i)
                nc.vector.tensor_tensor(x1[:].rearrange("p a d -> p (a d)"), ps_t[:],
                                        xn[:].rearrange("p a d -> p (a d)"), ALU.add).then_inc(x1_ready, 1)
                dve.wait_ge(x1_ready, ONE + i + 1)
                ln.vector_moments(dve, lambda t: x1[:, t, :], i)
                dve.wait_ge(hn_turned, ONE + i)
                ln.vector_apply(dve, lambda t: x1[:, t, :], lambda t: hn[:, t, :], i).then_inc(hn_ready, 1)
                xb = x_res[:, bass.ds(TT * i, TT), :]
                nc.vector.tensor_tensor(xb, xb, x1[:], ALU.add).then_inc(x1_added, 1)
                dve.wait_ge(hn_turned, ONE + i + 1)
                dve.wait_ge(rr_done, ONE + i)
                for k in range(KD):
                    last = nc.vector.tensor_scalar(hT[:, k, 1:T + 1], ps_t[:, k * T:(k + 1) * T], cols[:, k, 0:1],
                                                   cols[:, k, 1:2], ALU.mult, ALU.add)
                last.then_inc(hT_ready, 1)

            def finish(i):
                dve.wait_ge(rr_ready, ONE + i + 1)
                dve.wait_ge(kv_done, ONE + i + 1)
                xb = x_res[:, bass.ds(TT * i, TT), :]
                nc.vector.tensor_tensor(mixed[:], ps_kv[:], rr[:], ALU.mult).then_inc(mix_step, 1)
                dve.wait_ge(x1_added, ONE + i + 1)
                dve.wait_ge(mix_step, ONE + i + 1)
                nc.vector.tensor_tensor(xb, xb, mixed[:], ALU.add).then_inc(batch_done, 1)

            dve.wait_ge(setup_done, ONE + 4)
            values(0)
            rest(0)
            with dve.Fori(0, B - 1) as i:
                values(i + 1)
                rest(i + 1)
                finish(i)
            finish(B - 1)

        @block.scalar
        def _(act):
            act.wait_ge(cols_in, ONE + DMA)
            nc.scalar.activation(bonus[:], cols[:, :, 3], ACT.Exp).then_inc(setup_done, 1)
            with act.Fori(0, B) as i:
                def square(n):
                    act.wait_ge(kk_relu, ONE + NF * i + n + 1)
                    nc.scalar.activation(kk[:, n, :], kk[:, n, :], ACT.Square).then_inc(kk_ready, 1)

                for n in range(NF):
                    act.wait_ge(kk_done, ONE + NF * i + n + 1)
                    if n == 0:
                        act.wait_ge(kv_done, ONE + i)
                    nc.scalar.activation(kk[:, n, :], ps_kk[n % 2][:], ACT.Relu).then_inc(kk_relu, 1)
                    if n:
                        square(n - 1)
                square(NF - 1)
                act.wait_ge(rr_done, ONE + i + 1)
                act.wait_ge(batch_done, ONE + i)
                nc.scalar.activation(rr[:], ps_rr[:], ACT.Sigmoid).then_inc(rr_ready, 1)

        @block.tensor
        def _(pe):
            pe.wait_ge(setup_done, ONE + 4)

            def turn_y(i):
                pe.wait_ge(y_ready, ONE + i + 1)
                pe.wait_ge(hT_ready, ONE + i)
                for t in range(TT):
                    for k in range(KD):
                        last = nc.tensor.transpose(ps_t[:, t * D + k * P:t * D + (k + 1) * P],
                                                   y[:, k, t * P:(t + 1) * P], ident[:])
                last.then_inc(y_turned, 1)

            def turn_hn(i):
                pe.wait_ge(hn_ready, ONE + i + 1)
                for k in range(KD):
                    for t in range(TT):
                        last = nc.tensor.transpose(ps_t[:, k * T + t * P:k * T + (t + 1) * P],
                                                   hn[:, t, k * P:(k + 1) * P], ident[:])
                last.then_inc(hn_turned, 1)

            def mix(i, another):
                pe.wait_ge(hT_ready, ONE + i + 1)
                for n in range(NF):
                    if n >= 2:
                        pe.wait_ge(kk_relu, ONE + NF * i + n - 1)
                    for k in range(KD):
                        last = nc.tensor.matmul(ps_kk[n % 2][:], w_ck[:, k, n * P:(n + 1) * P], hT[:, k, 0:T],
                                                start=(k == 0), stop=(k == KD - 1))
                    last.then_inc(kk_done, 1)
                pe.wait_ge(rr_ready, ONE + i)
                for t in range(TT):
                    for k in range(KD):
                        last = nc.tensor.matmul(ps_rr[:, t, :], hT[:, k, t * P:(t + 1) * P], w_cr[:, k, :],
                                                start=(k == 0), stop=(k == KD - 1))
                last.then_inc(rr_done, 1)
                pe.wait_ge(kk_ready, ONE + NF * (i + 1))
                pe.wait_ge(batch_done, ONE + i)
                for t in range(TT):
                    if another and t == 1:
                        turn_y(i + 1)
                    if another and t == 3:
                        turn_hn(i + 1)
                    for n in range(NF):
                        last = nc.tensor.matmul(ps_kv[:, t, :], kk[:, n, t * P:(t + 1) * P], w_cv[:, n, :],
                                                start=(n == 0), stop=(n == NF - 1))
                last.then_inc(kv_done, 1)

            turn_y(0)
            turn_hn(0)
            pe.wait_ge(weights_in, ONE + 3 * DMA)
            with pe.Fori(0, B - 1) as i:
                mix(i, True)
            mix(B - 1, False)



HEADS, HD = 16, 16
PER_BLOCK = P // HD
SLOT = 32
GROUP = P // SLOT
SCORE_AT = (0, 512, 1024, 896)
SCORE_LEN = T + 3 * P + 2 * P + P


def causal_scores(nc, ps, key, query, wait_free, signal):
    for bank, tiles in enumerate(((0,), (1, 3), (2,))):
        wait_free(bank)
        for s in tiles:
            at = SCORE_AT[s] - 512 * bank
            last = nc.tensor.matmul(ps[:, bank, at:at + T - s * P], key[:, s * P:(s + 1) * P],
                                    query[:, s * P:T], start=True, stop=True)
        signal(last)


def values_sum(nc, ps, probs, v, h):
    j = h % GROUP
    for s in range(TT):
        last = nc.tensor.matmul(ps[SLOT * j:SLOT * (j + 1), s * P:T], v[:, s, h, :],
                                probs[:, SCORE_AT[s]:SCORE_AT[s] + T - s * P],
                                start=(s == 0), stop=(s == TT - 1))
    return last


def layer1(nc, io, keep):
    with ExitStack() as stack:
        room = Room(nc, stack, "a1")
        ident, x_res = keep.ident, keep.x_res
        w_qkv = room.sb("w_qkv", KD, 3 * D)
        w_o = room.sb("w_o", KD, D)
        weight = room.sb("weight", KD, D)
        w_eff = room.sb("w_eff", KD, D)
        bias = room.sb("bias", D)
        consts = room.sb("consts", 3)
        head_mask = room.sb("head_mask", PER_BLOCK)
        causal = room.sb("causal", P)
        ones = room.sb("ones", P)
        eps = room.sb("eps", TT * 2 * HEADS)
        gain = room.sb("gain", 1 + PER_BLOCK)
        shift = room.sb("shift", 1 + PER_BLOCK)
        abs_w = room.sb("abs_w", KD * D)
        abs_sum = room.sb("abs_sum", 1)
        limit = room.sb("limit", 2)
        ternary = room.sb("ternary", 2, KD * D)
        xn = room.sb("xn", TT, D)
        xnT = room.sb("xnT", KD, T)
        xnT_kept = room.sb("xnT_kept", KD, T)
        sums = room.sb("sums", TT, 2 * HEADS)
        centred = room.sb("centred", TT, 2 * D)
        squares = room.sb("squares", TT, 2 * D)
        spread = room.sb("spread", TT * 2 * HEADS)
        root = room.sb("root", TT * 2 * HEADS)
        rough = room.sb("rough", TT * 2 * HEADS)
        minus_half_error = room.sb("minus_half_error", 2, TT * 2 * HEADS)
        rstd = room.sb("rstd", TT * 2 * HEADS)
        qT = room.sb("qT", KD, T)
        kT = room.sb("kT", HEADS, T)
        v_sb = room.sb("v_sb", TT, HEADS, SLOT)
        probs = [room.sb(f"probs{n}", SCORE_LEN) for n in range(2)]
        yT = room.sb("yT", HEADS // GROUP, T)
        den = room.sb("den", TT, HEADS)
        y = room.sb("y", TT, D)
        ynT = room.sb("ynT", KD, T)
        ps_a = room.ps("ps_a", 2, T)
        ps_s = room.ps("ps_s", 3, T)
        ps_y = room.ps("ps_y", 2, T)
        ps_v = room.ps("ps_v", 1, T)
        ln = LayerNorm(nc, room, "ln", keep)
        weights_in, setup = room.sem("weights_in"), room.sem("setup")
        abs_done, abs_summed, limit_done = room.sem("abs_done"), room.sem("abs_summed"), room.sem("limit_done")
        xn_ready, xn_turned, xnT_ready = room.sem("xn_ready"), room.sem("xn_turned"), room.sem("xnT_ready")
        qk_done, v_done, v_ready = room.sem("qk_done"), room.sem("v_done"), room.sem("v_ready")
        qk_sum, qk_centred = room.sem("qk_sum"), room.sem("qk_centred")
        squared, spread_done, spread_eps, rstd_done = (room.sem("squared"), room.sem("spread_done"),
                                                       room.sem("spread_eps"), room.sem("rstd_done"))
        qk_ready, q_turned, k_turned = room.sem("qk_ready"), room.sem("q_turned"), room.sem("k_turned")
        qT_ready = room.sem("qT_ready")
        k0_ready, k1_ready = room.sem("k0_ready"), room.sem("k1_ready")
        scored, score_squared, masked = room.sem("scored"), room.sem("score_squared"), room.sem("masked")
        head_done, group_out = room.sem("head_done"), room.sem("group_out")
        y_back, den_step, y_ready = room.sem("y_back"), room.sem("den_step"), room.sem("y_ready")
        y_turned, ynT_ready = room.sem("y_turned"), room.sem("ynT_ready")
        out_done, bias_added, x_added = room.sem("out_done"), room.sem("bias_added"), room.sem("x_added")
        rooted, newton, kept = room.sem("rooted"), room.sem("newton"), room.sem("kept")
        block = room.block()
        SETUP = 8

        @block.sync
        def _(sp):
            n = 0
            for dst, src in ((weight[:], io.l1_weight), (consts[:], io.l1_consts), (head_mask[:], io.head_mask),
                             (bias[:], io.l1_bias), (causal[:], io.causal), (w_qkv[:], io.l1_w_qkv),
                             (w_o[:], io.l1_w_o)):
                sp.dma_start(dst, src).then_inc(weights_in, DMA)
                n += 1
            assert n == 7

        @block.gpsimd
        def _(pool):

            def add_bias(i):
                xb = x_res[:, bass.ds(TT * i, TT), :]
                pool.wait_ge(xn_ready, ONE + i + 1)
                nc.gpsimd.tensor_tensor(xb, xb, bias[:].rearrange("p (a d) -> p a d", a=1).broadcast_to([P, TT, D]),
                                        ALU.add).then_inc(bias_added, 1)

            def heads(i, after):
                for h in range(HEADS):
                    pool.wait_ge(score_squared, ONE + 3 * (HEADS * i + h + 1))
                    pr = probs[h % 2]
                    lead = pr[:, 0:SCORE_LEN].rearrange("p (a c) -> p a c", c=256)[:, 0:5:2, 0:P]
                    nc.gpsimd.tensor_tensor(lead, lead, causal[:].rearrange("p (a c) -> p a c", a=1).broadcast_to([P, 3, P]),
                                            ALU.mult)
                    nc.gpsimd.tensor_tensor(pr[:, 896:1024], pr[:, 896:1024], causal[:], ALU.mult).then_inc(masked, 1)
                    if after and h == 0:
                        ln.pool_rstd(pool, i + 1)
                if after:
                    add_bias(i + 1)

            ln.pool_rstd(pool, 0)
            pool.wait_ge(weights_in, ONE + 7 * DMA)
            add_bias(0)
            with pool.Fori(0, B - 1) as i:
                heads(i, True)
            heads(B - 1, False)

        @block.vector
        def _(dve):
            nc.vector.memset(ones[:], 1.0).then_inc(setup, 1)
            nc.vector.memset(eps[:], HD * LN_EPS).then_inc(setup, 1)
            nc.vector.memset(v_sb[:], 0.0).then_inc(setup, 1)
            dve.wait_ge(setup, ONE + 3)
            nc.vector.memset(v_sb[:, :, :, HD:HD + 1], 1.0).then_inc(setup, 1)

            def norms(i):
                def x_tile(t):
                    return x_res[:, bass.ds(TT * i + t, 1), :].rearrange("p a d -> p (a d)")
                ln.vector_moments(dve, x_tile, i)
                dve.wait_ge(xn_turned, ONE + i)
                ln.vector_apply(dve, x_tile, lambda t: xn[:, t, :], i).then_inc(xn_ready, 1)

            def head_norms(i):
                for t in range(TT):
                    dve.wait_ge(qk_done, ONE + TT * i + t + 1)
                    qk = ps_a[:, t % 2, :].rearrange("p (h c) -> p h c", c=HD)
                    nc.vector.tensor_reduce(sums[:, t, :], qk, AX.X, ALU.add).then_inc(qk_sum, 1)
                    dve.wait_ge(qk_sum, ONE + TT * i + t + 1)
                    if t == 0:
                        dve.wait_ge(q_turned, ONE + i)
                        dve.wait_ge(k_turned, ONE + i)
                        dve.wait_ge(squared, ONE + i)
                    nc.vector.scalar_tensor_tensor(
                        out=centred[:, t, :].rearrange("p (h c) -> p h c", c=HD),
                        in0=sums[:, t, :].rearrange("p (h a) -> p h a", a=1).broadcast_to([P, 2 * HEADS, HD]),
                        scalar=-1.0 / HD, in1=qk, op0=ALU.mult, op1=ALU.add).then_inc(qk_centred, 1)
                dve.wait_ge(squared, ONE + i + 1)
                nc.vector.tensor_reduce(spread[:], squares[:].rearrange("p t (h c) -> p (t h) c", c=HD),
                                        AX.X, ALU.add).then_inc(spread_done, 1)
                dve.wait_ge(spread_done, ONE + i + 1)
                nc.vector.tensor_tensor(spread[:], spread[:], eps[:], ALU.add).then_inc(spread_eps, 1)
                dve.wait_ge(rooted, ONE + i + 1)
                nc.vector.reciprocal(rough[:], root[:]).then_inc(newton, 1)
                dve.wait_ge(newton, ONE + 3 * i + 1)
                nc.vector.scalar_tensor_tensor(out=minus_half_error[:, 0], in0=rough[:], scalar=-0.5, in1=rough[:],
                                               op0=ALU.mult, op1=ALU.mult).then_inc(newton, 1)
                dve.wait_ge(newton, ONE + 3 * i + 2)
                nc.vector.tensor_tensor(minus_half_error[:, 1], minus_half_error[:, 0], spread[:], ALU.mult).then_inc(newton, 1)
                dve.wait_ge(newton, ONE + 3 * i + 3)
                nc.vector.scalar_tensor_tensor(out=rstd[:], in0=minus_half_error[:, 1], scalar=1.5, in1=rough[:],
                                               op0=ALU.add, op1=ALU.mult).then_inc(rstd_done, 1)
                dve.wait_ge(rstd_done, ONE + i + 1)
                rows = centred[:].rearrange("p t (h c) -> p (t h) c", c=HD)
                nc.vector.tensor_tensor(rows, rows, rstd[:].rearrange("p (h a) -> p h a", a=1)
                                        .broadcast_to([P, TT * 2 * HEADS, HD]), ALU.mult).then_inc(qk_ready, 1)

            def late_keys(i, heads):
                if heads[0] == PER_BLOCK:
                    dve.wait_ge(k_turned, ONE + i + 1)
                    dve.wait_ge(scored, ONE + 3 * HEADS * i)
                for h in heads:
                    m = 1 + h - PER_BLOCK
                    nc.vector.tensor_scalar(kT[:, h, :], ps_a[:, 1, :], gain[:, m:m + 1], shift[:, m:m + 1],
                                            ALU.mult, ALU.add).then_inc(k1_ready, 1)

            def finish(i, after):
                if after:
                    late_keys(i + 1, range(PER_BLOCK, PER_BLOCK + 3))
                for t in range(TT):
                    dve.wait_ge(y_back, ONE + TT * i + t + 1)
                    sums_t = ps_y[:, t % 2, :].rearrange("p (h c) -> p h c", c=SLOT)
                    nc.vector.tensor_scalar(den[:, t, :], sums_t[:, :, HD], LN_EPS, None, ALU.add).then_inc(den_step, 1)
                    dve.wait_ge(den_step, ONE + 2 * (TT * i + t) + 1)
                    nc.vector.reciprocal(den[:, t, :], den[:, t, :]).then_inc(den_step, 1)
                    dve.wait_ge(den_step, ONE + 2 * (TT * i + t) + 2)
                    nc.vector.tensor_tensor(y[:, t, :].rearrange("p (h c) -> p h c", c=HD), sums_t[:, :, 0:HD],
                                            den[:, t, :].rearrange("p (h a) -> p h a", a=1).broadcast_to([P, HEADS, HD]),
                                            ALU.mult).then_inc(y_ready, 1)
                if after:
                    late_keys(i + 1, range(PER_BLOCK + 3, HEADS))
                dve.wait_ge(out_done, ONE + i + 1)
                dve.wait_ge(bias_added, ONE + i + 1)
                xb = x_res[:, bass.ds(TT * i, TT), :].rearrange("p a d -> p (a d)")
                nc.vector.tensor_tensor(xb, xb, ps_y[:].rearrange("p a d -> p (a d)"), ALU.add).then_inc(x_added, 1)

            norms(0)
            dve.wait_ge(weights_in, ONE + 7 * DMA)
            nc.vector.tensor_scalar(gain[:, 0:1], consts[:, 0:1], HD ** 0.5, None, ALU.mult).then_inc(setup, 1)
            nc.vector.tensor_scalar(gain[:, 1:], head_mask[:], consts[:, 0:1], HD ** 0.5, ALU.mult, ALU.mult).then_inc(setup, 1)
            nc.vector.tensor_copy(shift[:, 0:1], consts[:, 1:2]).then_inc(setup, 1)
            nc.vector.tensor_scalar(shift[:, 1:], head_mask[:], consts[:, 1:2], None, ALU.mult).then_inc(setup, 1)
            dve.wait_ge(abs_summed, ONE + 1)
            nc.vector.tensor_scalar(limit[:, 0:1], ps_v[:, 0, 0:1], 0.7 / (D * D), None, ALU.mult).then_inc(limit_done, 1)
            nc.vector.tensor_scalar(limit[:, 1:2], ps_v[:, 0, 0:1], -0.7 / (D * D), None, ALU.mult).then_inc(limit_done, 1)
            dve.wait_ge(limit_done, ONE + 2)
            w_row = weight[:].rearrange("p k d -> p (k d)")
            nc.vector.tensor_scalar(ternary[:, 0, :], w_row, limit[:, 0:1], consts[:, 2:3], ALU.is_gt, ALU.mult).then_inc(limit_done, 1)
            nc.vector.tensor_scalar(ternary[:, 1, :], w_row, limit[:, 1:2], consts[:, 2:3], ALU.is_lt, ALU.mult).then_inc(limit_done, 1)
            dve.wait_ge(limit_done, ONE + 4)
            nc.vector.tensor_tensor(w_eff[:].rearrange("p k d -> p (k d)"), ternary[:, 0, :], ternary[:, 1, :],
                                    ALU.subtract).then_inc(limit_done, 1)
            head_norms(0)
            late_keys(0, range(PER_BLOCK, HEADS))
            with dve.Fori(0, B - 1) as i:
                norms(i + 1)
                head_norms(i + 1)
                finish(i, True)
            finish(B - 1, False)

        @block.scalar
        def _(act):
            act.wait_ge(weights_in, ONE + 7 * DMA)
            nc.scalar.activation(abs_w[:], weight[:].rearrange("p k d -> p (k d)"), ACT.Abs,
                                 accum_out=abs_sum[:]).then_inc(abs_done, 1)
            act.wait_ge(setup, ONE + SETUP)

            def rows_turned(i):
                act.wait_ge(xn_turned, ONE + i + 1)
                act.wait_ge(kept, ONE + i)
                nc.scalar.copy(xnT[:], ps_a[:]).then_inc(xnT_ready, 1)

            def square_centred(i):
                act.wait_ge(qk_centred, ONE + TT * (i + 1))
                act.wait_ge(spread_done, ONE + i)
                nc.scalar.activation(squares[:], centred[:], ACT.Square).then_inc(squared, 1)

            def spread_roots(i):
                act.wait_ge(spread_eps, ONE + i + 1)
                nc.scalar.activation(root[:], spread[:], ACT.Sqrt).then_inc(rooted, 1)

            def keep_rows(i):
                act.wait_ge(out_done, ONE + i)
                act.wait_ge(xnT_ready, ONE + i + 1)
                nc.scalar.copy(xnT_kept[:], xnT[:]).then_inc(kept, 1)

            def operands(i, before):
                act.wait_ge(q_turned, ONE + i + 1)
                nc.scalar.activation(qT[:], ps_s[:, 0:2, :], ACT.Identity, bias=shift[:, 0:1], scale=gain[:, 0:1]).then_inc(qT_ready, 1)
                act.wait_ge(k_turned, ONE + i + 1)

                def key(h):
                    nc.scalar.activation(kT[:, h, :], ps_a[:, 0, :], ACT.Identity, bias=shift[:, 1 + h:2 + h],
                                         scale=gain[:, 1 + h:2 + h]).then_inc(k0_ready, 1)

                def value(t):
                    act.wait_ge(v_done, ONE + TT * i + t + 1)
                    ps = ps_v[:, 0, 0:D] if t % 2 else ps_s[:, 2, 0:D]
                    nc.scalar.copy(v_sb[:, t, :, 0:HD], ps.rearrange("p (h c) -> p h c", c=HD)).then_inc(v_ready, 1)

                for keys, t in (((0, 1), 0), ((), 1), ((2,), 2), ((), 3)):
                    for h in keys:
                        key(h)
                    value(t)
                key(3)
                if before:
                    output_rows(i - 1)
                for h in range(4, PER_BLOCK):
                    key(h)

            def output_rows(i):
                act.wait_ge(y_turned, ONE + i + 1)
                nc.scalar.copy(ynT[:], ps_s[:, 0:2, :]).then_inc(ynT_ready, 1)

            def heads(i, after):
                for h in range(HEADS):
                    if h >= 2:
                        act.wait_ge(head_done, ONE + HEADS * i + h - 1)
                    pr = probs[h % 2]
                    for bank, width in enumerate((T, T, 2 * P)):
                        act.wait_ge(scored, ONE + 3 * (HEADS * i + h) + bank + 1)
                        nc.scalar.activation(pr[:, 512 * bank:512 * bank + width], ps_s[:, bank, 0:width],
                                             ACT.Square, scale=HD ** -0.5).then_inc(score_squared, 1)
                    if h % GROUP == 0 and h:
                        act.wait_ge(head_done, ONE + HEADS * i + h)
                        g = h // GROUP - 1
                        nc.scalar.copy(yT[:, g, :], ps_y[:, g % 2, :]).then_inc(group_out, 1)
                    if h == 1:
                        keep_rows(i)
                    if after and h == 3:
                        rows_turned(i + 1)
                    if after and h == 9:
                        square_centred(i + 1)
                    if after and h == 11:
                        spread_roots(i + 1)
                act.wait_ge(head_done, ONE + HEADS * (i + 1))
                g = HEADS // GROUP - 1
                nc.scalar.copy(yT[:, g, :], ps_y[:, g % 2, :]).then_inc(group_out, 1)

            rows_turned(0)
            square_centred(0)
            spread_roots(0)
            operands(0, False)
            with act.Fori(0, B - 1) as i:
                heads(i, True)
                operands(i + 1, True)
            heads(B - 1, False)
            output_rows(B - 1)

        @block.tensor
        def _(pe):
            G = HEADS // GROUP
            pe.wait_ge(abs_done, ONE + 1)
            pe.wait_ge(setup, ONE + SETUP)
            nc.tensor.matmul(ps_v[:, 0, 0:1], ones[:], abs_sum[:], start=True, stop=True).then_inc(abs_summed, 1)

            def turn_rows(i):
                pe.wait_ge(xn_ready, ONE + i + 1)
                for k in range(KD):
                    for t in range(TT):
                        last = nc.tensor.transpose(ps_a[:, k, t * P:(t + 1) * P], xn[:, t, k * P:(k + 1) * P], ident[:])
                last.then_inc(xn_turned, 1)

            def queries_keys(i, t):
                if t == 0:
                    pe.wait_ge(xnT_ready, ONE + i + 1)
                if t >= 2:
                    pe.wait_ge(qk_centred, ONE + TT * i + t - 1)
                for k in range(KD):
                    last = nc.tensor.matmul(ps_a[:, t % 2, :], xnT[:, k, t * P:(t + 1) * P], w_qkv[:, k, 0:2 * D],
                                            start=(k == 0), stop=(k == KD - 1))
                last.then_inc(qk_done, 1)

            def values(i, t):
                if t >= 2:
                    pe.wait_ge(v_ready, ONE + TT * i + t - 1)
                ps = ps_v[:, 0, 0:D] if t % 2 else ps_s[:, 2, 0:D]
                for k in range(KD):
                    last = nc.tensor.matmul(ps, xnT[:, k, t * P:(t + 1) * P], w_qkv[:, k, 2 * D:3 * D],
                                            start=(k == 0), stop=(k == KD - 1))
                last.then_inc(v_done, 1)

            def turn_back(i, t):
                if t >= 2:
                    pe.wait_ge(y_ready, ONE + TT * i + t - 1)
                for g in range(G):
                    last = nc.tensor.transpose(ps_y[:, t % 2, g * P:(g + 1) * P], yT[:, g, t * P:(t + 1) * P], ident[:])
                last.then_inc(y_back, 1)

            def output(i):
                pe.wait_ge(y_ready, ONE + TT * (i + 1))
                for k in range(KD):
                    for t in range(TT):
                        last = nc.tensor.transpose(ps_s[:, k, t * P:(t + 1) * P], y[:, t, k * P:(k + 1) * P], ident[:])
                last.then_inc(y_turned, 1)
                pe.wait_ge(kept, ONE + i + 1)
                out = ps_y[:].rearrange("p a (b d) -> p (a b) d", d=D)
                for t in range(TT):
                    for k in range(KD):
                        nc.tensor.matmul(out[:, t, :], xnT_kept[:, k, t * P:(t + 1) * P], w_eff[:, k, :], start=(k == 0), stop=False)
                    if t == 0:
                        pe.wait_ge(ynT_ready, ONE + i + 1)
                    for k in range(KD):
                        last = nc.tensor.matmul(out[:, t, :], ynT[:, k, t * P:(t + 1) * P], w_o[:, k, :],
                                                start=False, stop=(k == KD - 1))
                last.then_inc(out_done, 1)

            def turn_keys(i):
                pe.wait_ge(qk_ready, ONE + i + 1)
                for k in range(KD):
                    for t in range(TT):
                        last = nc.tensor.transpose(ps_a[:, k, t * P:(t + 1) * P],
                                                   centred[:, t, D + k * P:D + (k + 1) * P], ident[:])
                last.then_inc(k_turned, 1)

            def operands(i, before):
                pe.wait_ge(limit_done, ONE + 5)
                pe.wait_ge(score_squared, ONE + 3 * HEADS * i)
                for k in range(KD):
                    for t in range(TT):
                        last = nc.tensor.transpose(ps_s[:, k, t * P:(t + 1) * P], centred[:, t, k * P:(k + 1) * P], ident[:])
                last.then_inc(q_turned, 1)
                if before:
                    pe.wait_ge(group_out, ONE + G * i)
                for t in range(TT):
                    if before:
                        turn_back(i - 1, t)
                    values(i, t)
                pe.wait_ge(qT_ready, ONE + i + 1)
                if before:
                    output(i - 1)
                pe.wait_ge(v_ready, ONE + TT * (i + 1))

            def heads(i, before, after):
                def attend(h):
                    pe.wait_ge(masked, ONE + HEADS * i + h + 1)
                    if h % GROUP == 0 and h >= 2 * GROUP:
                        pe.wait_ge(group_out, ONE + G * i + h // GROUP - 1)
                    values_sum(nc, ps_y[:, (h // GROUP) % 2, :], probs[h % 2], v_sb, h).then_inc(head_done, 1)

                for h in range(HEADS):
                    if h < PER_BLOCK:
                        pe.wait_ge(k0_ready, ONE + PER_BLOCK * i + h + 1)
                    else:
                        pe.wait_ge(k1_ready, ONE + PER_BLOCK * i + h - PER_BLOCK + 1)
                    causal_scores(nc, ps_s, kT[:, h, :], qT[:, h // PER_BLOCK, :],
                                  lambda bank: pe.wait_ge(score_squared, ONE + 3 * (HEADS * i + h - 1) + bank + 1) if h else None,
                                  lambda last: last.then_inc(scored, 1))
                    if h == 1 and before:
                        pe.wait_ge(x_added, ONE + i)
                    if h:
                        attend(h - 1)
                    if after and h == 3:
                        pe.wait_ge(k0_ready, ONE + PER_BLOCK * (i + 1))
                        pe.wait_ge(k1_ready, ONE + PER_BLOCK * (i + 1))
                        turn_rows(i + 1)
                    if after and 5 <= h < 5 + TT:
                        queries_keys(i + 1, h - 5)
                if after:
                    turn_keys(i + 1)
                attend(HEADS - 1)

            turn_rows(0)
            for t in range(TT):
                queries_keys(0, t)
            turn_keys(0)
            operands(0, False)
            heads(0, False, True)
            with pe.Fori(1, B - 1) as i:
                operands(i, True)
                heads(i, True, True)
            operands(B - 1, True)
            heads(B - 1, True, False)
            pe.wait_ge(group_out, ONE + G * B)
            for t in range(TT):
                turn_back(B - 1, t)
            output(B - 1)



FUTURE = 4
EXPERTS2 = 8
NEG = -1e30
QUERY_AT = (896, 1024, 512, 0)
BANK_TILES = ((3,), (2, 0), (1,))


def layer2_attend(nc, io, keep):
    with ExitStack() as stack:
        room = Room(nc, stack, "a2")
        ident, x_res = keep.ident, keep.x_res
        w_fqvk = room.sb("w_fqvk", KD, 4 * D)
        w_proj = room.sb("w_proj", KD, D)
        conv = room.sb("conv", FUTURE, P)
        cols = room.sb("cols", KD, 2)
        head_mask = room.sb("head_mask", PER_BLOCK)
        hide_later = room.sb("hide_later", P)
        xn = room.sb("xn", TT, D)
        hn = room.sb("hn", TT, D)
        hT = room.sb("hT", KD, T)
        w_fT = room.sb("w_fT", KD, D)
        w_fold = room.sb("w_fold", FUTURE, KD, 2 * D)
        qT = room.sb("qT", KD, T)
        kT = room.sb("kT", HEADS, T)
        q_tok = room.sb("q_tok", TT, D)
        v_sb = room.sb("v_sb", TT, HEADS, SLOT)
        prod = [room.sb(f"prod{n}", D) for n in range(2)]
        v_future = room.sb("v_future", TT, FUTURE, D)
        future = room.sb("future", TT, HEADS, FUTURE)
        neg_fmax = room.sb("neg_fmax", HEADS, TT)
        row_max = room.sb("row_max", HEADS, TT)
        neg_max = room.sb("neg_max", HEADS, TT)
        probs = [room.sb(f"probs{n}", SCORE_LEN) for n in range(2)]
        probsT = [room.sb(f"probsT{n}", SCORE_LEN) for n in range(2)]
        yT = room.sb("yT", HEADS // GROUP, T)
        future_sum = room.sb("future_sum", TT, HEADS)
        future_x = room.sb("future_x", TT, D)
        den = room.sb("den", TT, HEADS)
        y = room.sb("y", TT, D)
        ynT = room.sb("ynT", KD, T)
        x1 = room.sb("x1", TT, D)
        ps_a = room.ps("ps_a", 3, T)
        ps_s = room.ps("ps_s", 3, T)
        ps_y = room.ps("ps_y", 2, T)
        ln_a = LayerNorm(nc, room, "ln_a", keep)
        ln_b = LayerNorm(nc, room, "ln_b", keep)
        first_in, later_in = room.sem("first_in"), room.sem("later_in")
        setup, conv_zeroed = room.sem("setup"), room.sem("conv_zeroed")
        xn_ready, hn_ready, hn_turned = room.sem("xn_ready"), room.sem("hn_ready"), room.sem("hn_turned")
        hT_ready = room.sem("hT_ready")
        q_done, k_done = room.sem("q_done"), room.sem("k_done")
        qT_ready = room.sem("qT_ready")
        k0_ready, k1_ready = room.sem("k0_ready"), room.sem("k1_ready")
        qv_done, qv_ready = room.sem("qv_done"), room.sem("qv_ready")
        w_f_turned, w_fT_ready = room.sem("w_f_turned"), room.sem("w_fT_ready")
        w_up_done, w_up_ready = room.sem("w_up_done"), room.sem("w_up_ready")
        folded, w_fold_ready = room.sem("folded"), room.sem("w_fold_ready")
        kvf_done, vf_ready = room.sem("kvf_done"), room.sem("vf_ready")
        prod_done, logit_done, fmax_done = room.sem("prod_done"), room.sem("logit_done"), room.sem("fmax_done")
        scored, hidden_later = room.sem("scored"), room.sem("hidden_later")
        maxed, neg_max_ready = room.sem("maxed"), room.sem("neg_max_ready")
        exped, turned, turned_out = room.sem("exped"), room.sem("turned"), room.sem("turned_out")
        odd_turned_out = room.sem("odd_turned_out")
        head_done, group_out = room.sem("head_done"), room.sem("group_out")
        shifted, future_exped = room.sem("shifted"), room.sem("future_exped")
        weighted, future_step = room.sem("weighted"), room.sem("future_step")
        y_back, den_step, y_ready = room.sem("y_back"), room.sem("den_step"), room.sem("y_ready")
        y_turned, ynT_ready, out_done = room.sem("y_turned"), room.sem("ynT_ready"), room.sem("out_done")
        x1_ready, x1_saved = room.sem("x1_ready"), room.sem("x1_saved")
        xn_kept = room.sem("xn_kept")
        TURN_BACK_AT, DIVIDE_AT, TURN_AT, OUTPUT_AT = (3, 4, 6, 8), (4, 5, 7, 9), 10, 13
        block = room.block()
        G = HEADS // GROUP

        def up_bank(f):
            return ps_s[:, f, :] if f < 3 else ps_y[:, 0, :]

        FIRST, LATER = 3 * DMA, (2 + PER_BLOCK) * DMA

        @block.sync
        def _(sp):
            for dst, src in ((cols[:], io.l2_cols), (head_mask[:], io.head_mask), (w_fqvk[:], io.l2_w_fqvk)):
                sp.dma_start(dst, src).then_inc(first_in, DMA)
            sp.dma_start(hide_later[:], io.hide_later).then_inc(later_in, DMA)
            sp.wait_ge(conv_zeroed, ONE + 1)
            for h in range(PER_BLOCK):
                rows = slice(h * HD, (h + 1) * HD)
                sp.dma_start(conv[rows, :, rows], io.l2_conv).then_inc(later_in, DMA)
            sp.dma_start(w_proj[:], io.l2_w_proj).then_inc(later_in, DMA)
            with sp.Fori(0, B) as i:
                sp.wait_ge(x1_ready, ONE + i + 1)
                sp.dma_start(io.x1_scratch[bass.ds(i, 1)].rearrange("a p t d -> p (a t) d"), x1[:]).then_inc(x1_saved, DMA)
            sp.wait_ge(x1_saved, ONE + DMA * B)

        @block.gpsimd
        def _(pool):
            nc.gpsimd.memset(conv[:], 0.0).then_inc(conv_zeroed, 1)

            def norms(i):
                ln_a.pool_rstd(pool, i)
                ln_b.pool_rstd(pool, i)

            def keep_xn(i):
                wait_apart(pool, keep.always, xn_ready, i + 1)
                wait_apart(pool, keep.always, x1_saved, DMA * i)
                nc.gpsimd.tensor_copy(x1[:], xn[:]).then_inc(xn_kept, 1)

            def weigh(i):
                pool.wait_ge(future_exped, ONE + i + 1)
                for t in range(TT):
                    vf = v_future[:, t].rearrange("p f (h d) -> p f h d", d=HD)
                    for f in range(FUTURE):
                        last = nc.gpsimd.tensor_tensor(
                            vf[:, f], vf[:, f],
                            future[:, t, :, f:f + 1].broadcast_to([P, HEADS, HD]), ALU.mult)
                last.then_inc(weighted, 1)

            norms(0)
            keep_xn(0)
            with pool.Fori(0, B - 1) as i:
                norms(i + 1)
                weigh(i)
                keep_xn(i + 1)
            weigh(B - 1)

        @block.vector
        def _(dve):
            nc.vector.memset(v_sb[:], 0.0).then_inc(setup, 1)
            dve.wait_ge(setup, ONE + 1)
            nc.vector.memset(v_sb[:, :, :, HD:HD + 1], 1.0).then_inc(setup, 1)

            def x_tile(i, t):
                return x_res[:, bass.ds(TT * i + t, 1), :].rearrange("p a d -> p (a d)")

            def norm_a(i):
                ln_a.vector_moments(dve, lambda t: x_tile(i, t), i)

            def norm_b(i):
                dve.wait_ge(xn_kept, ONE + i)
                ln_a.vector_apply(dve, lambda t: x_tile(i, t), lambda t: xn[:, t, :], i).then_inc(xn_ready, 1)

            def norm_c(i):
                dve.wait_ge(xn_ready, ONE + i + 1)
                ln_b.vector_moments(dve, lambda t: xn[:, t, :], i)

            def norm_d(i):
                dve.wait_ge(hn_turned, ONE + i)
                ln_b.vector_apply(dve, lambda t: xn[:, t, :], lambda t: hn[:, t, :], i).then_inc(hn_ready, 1)

            def prepare(i, before):
                dve.wait_ge(k_done, ONE + i + 1)
                dve.wait_ge(scored, ONE + 3 * HEADS * i)
                for h in range(PER_BLOCK, HEADS):
                    nc.vector.tensor_scalar(kT[:, h, :], ps_y[:, 1, :], head_mask[:, h - PER_BLOCK:h - PER_BLOCK + 1],
                                            None, ALU.mult).then_inc(k1_ready, 1)
                if before:
                    future_sums(i - 1)
                for t in range(TT):
                    for f in range(FUTURE):
                        n = FUTURE * t + f
                        at = FUTURE * TT * i + n
                        dve.wait_ge(kvf_done, ONE + at + 1)
                        if n == 0:
                            dve.wait_ge(qv_ready, ONE + 2 * TT * (i + 1))
                            dve.wait_ge(weighted, ONE + i)
                            dve.wait_ge(future_step, ONE + 2 * i)
                        if n >= 2:
                            dve.wait_ge(logit_done, ONE + at - 1)
                        nc.vector.tensor_tensor(prod[n % 2][:], ps_a[:, n % 3, D:2 * D], q_tok[:, t, :],
                                                ALU.mult).then_inc(prod_done, 1)
                        if n >= 1:
                            logit(i, n - 1)
                        if before and n in DIVIDE_AT:
                            divide(i - 1, DIVIDE_AT.index(n))
                logit(i, FUTURE * TT - 1)
                if before:
                    add_output(i - 1)
                dve.wait_ge(logit_done, ONE + FUTURE * TT * (i + 1))
                dve.wait_ge(neg_max_ready, ONE + 3 * HEADS * i)
                nc.vector.tensor_reduce(neg_fmax[:].rearrange("p h t -> p t h"), future[:], AX.X, ALU.max,
                                        negate=True).then_inc(fmax_done, 1)

            def logit(i, n):
                dve.wait_ge(prod_done, ONE + FUTURE * TT * i + n + 1)
                nc.vector.tensor_reduce(future[:, n // FUTURE, :, n % FUTURE],
                                        prod[n % 2][:].rearrange("p (h d) -> p h d", d=HD),
                                        AX.X, ALU.add).then_inc(logit_done, 1)

            def head_max(i, h):
                u = HEADS * i + h
                flat = ps_s[:].rearrange("p a c -> p (a c)")

                def hide(bank, at, blocks):
                    dve.wait_ge(scored, ONE + 3 * u + bank + 1)
                    there = flat[:, at:at + blocks * P].rearrange("p (a c) -> p a c", c=P)
                    nc.vector.tensor_tensor(there, there, hide_later[:].rearrange("p (a c) -> p a c", a=1)
                                            .broadcast_to([P, blocks, P]), ALU.add).then_inc(hidden_later, 1)

                def maxima(bank, tiles):
                    dve.wait_ge(hidden_later, ONE + 3 * u + bank + 1)
                    for t in tiles:
                        last = nc.vector.tensor_reduce(row_max[:, h, t:t + 1], flat[:, QUERY_AT[t]:QUERY_AT[t] + (t + 1) * P],
                                                       AX.X, ALU.max)
                    last.then_inc(maxed, 1)

                def negate(bank, tiles):
                    dve.wait_ge(maxed, ONE + 3 * u + bank + 1)
                    nc.vector.scalar_tensor_tensor(out=neg_max[:, h, tiles], in0=row_max[:, h, tiles], scalar=-HD ** -0.5,
                                                   in1=neg_fmax[:, h, tiles], op0=ALU.mult, op1=ALU.min
                                                   ).then_inc(neg_max_ready, 1)

                hide(0, QUERY_AT[3] + 3 * P, 1)
                if h == 0:
                    dve.wait_ge(shifted, ONE + i)
                    dve.wait_ge(exped, ONE + 4 * HEADS * i)
                    dve.wait_ge(fmax_done, ONE + i + 1)
                maxima(0, (3,))
                hide(1, QUERY_AT[2] + 2 * P, 2)
                negate(0, slice(3, 4))
                maxima(1, (2, 0))
                hide(2, QUERY_AT[1] + P, 1)
                negate(1, slice(0, 3, 2))
                maxima(2, (1,))
                negate(2, slice(1, 2))

            def head_copy(i, h):
                u = HEADS * i + h
                dve.wait_ge(turned, ONE + 3 * u + 2)
                if h >= 2:
                    dve.wait_ge(head_done, ONE + u - 1)
                nc.vector.tensor_copy(probsT[h % 2][:, 512:1024], ps_a[:, 1, :]).then_inc(odd_turned_out, 1)

            def future_exponents(i):
                dve.wait_ge(neg_max_ready, ONE + 3 * HEADS * (i + 1))
                nc.vector.tensor_tensor(
                    future[:].rearrange("p t h f -> p t h f"), future[:],
                    neg_max[:].rearrange("p h (t a) -> p t h a", a=1).broadcast_to([P, TT, HEADS, FUTURE]),
                    ALU.add).then_inc(shifted, 1)

            def future_sums(i):
                dve.wait_ge(future_exped, ONE + i + 1)
                nc.vector.tensor_reduce(future_sum[:], future[:], AX.X, ALU.add).then_inc(future_step, 1)
                dve.wait_ge(weighted, ONE + i + 1)
                for t in range(TT):
                    last = nc.vector.tensor_reduce(future_x[:, t, :], v_future[:, t].rearrange("p f d -> p d f"),
                                                   AX.X, ALU.add)
                last.then_inc(future_step, 1)

            def divide(i, t):
                at = 3 * (TT * i + t)
                if t == 0:
                    dve.wait_ge(future_step, ONE + 2 * i + 2)
                dve.wait_ge(y_back, ONE + TT * i + t + 1)
                sums_t = ps_y[:, t % 2, :].rearrange("p (h c) -> p h c", c=SLOT)
                rows = y[:, t, :].rearrange("p (h c) -> p h c", c=HD)
                nc.vector.tensor_tensor(den[:, t, :], sums_t[:, :, HD], future_sum[:, t, :], ALU.add).then_inc(den_step, 1)
                nc.vector.tensor_tensor(rows, sums_t[:, :, 0:HD], future_x[:, t, :].rearrange("p (h c) -> p h c", c=HD),
                                        ALU.add).then_inc(den_step, 1)
                dve.wait_ge(den_step, ONE + at + 1)
                nc.vector.reciprocal(den[:, t, :], den[:, t, :]).then_inc(den_step, 1)
                dve.wait_ge(den_step, ONE + at + 3)
                nc.vector.tensor_tensor(rows, rows, den[:, t, :].rearrange("p (h a) -> p h a", a=1)
                                        .broadcast_to([P, HEADS, HD]), ALU.mult).then_inc(y_ready, 1)

            def add_output(i):
                dve.wait_ge(out_done, ONE + i + 1)
                dve.wait_ge(xn_kept, ONE + i + 1)
                nc.vector.tensor_tensor(x1[:].rearrange("p t d -> p (t d)"), ps_y[:].rearrange("p a d -> p (a d)"),
                                        x1[:].rearrange("p t d -> p (t d)"), ALU.add).then_inc(x1_ready, 1)

            def heads(i, after):
                head_max(i, 0)
                for h in range(1, HEADS):
                    head_max(i, h)
                    head_copy(i, h - 1)
                    if after and h in (3, 6, 9, 12):
                        (norm_a, norm_b, norm_c, norm_d)[h // 3 - 1](i + 1)
                future_exponents(i)
                head_copy(i, HEADS - 1)

            norm_a(0)
            norm_b(0)
            norm_c(0)
            norm_d(0)
            dve.wait_ge(first_in, ONE + FIRST)
            dve.wait_ge(later_in, ONE + LATER)
            prepare(0, False)
            with dve.Fori(0, B - 1) as i:
                heads(i, True)
                prepare(i + 1, True)
            heads(B - 1, False)
            future_sums(B - 1)
            for t in range(TT):
                divide(B - 1, t)
            add_output(B - 1)

        @block.scalar
        def _(act):
            act.wait_ge(first_in, ONE + FIRST)
            act.wait_ge(setup, ONE + 2)

            def fold():
                act.wait_ge(w_f_turned, ONE + 1)
                nc.scalar.copy(w_fT[:], ps_a[:, 0:KD, 0:D]).then_inc(w_fT_ready, 1)
                for f in range(FUTURE):
                    act.wait_ge(w_up_done, ONE + f + 1)
                    nc.scalar.copy(v_future[:, 0:KD, f, :], up_bank(f).rearrange("p (m c) -> p m c", c=D)).then_inc(w_up_ready, 1)
                for n in range(FUTURE * KD):
                    act.wait_ge(folded, ONE + n + 1)
                    nc.scalar.copy(w_fold[:, n // KD, n % KD, :], ps_a[:, n % 3, :]).then_inc(w_fold_ready, 1)

            def output_rows(i):
                act.wait_ge(y_turned, ONE + i + 1)
                nc.scalar.copy(ynT[:], ps_s[:, 0:2, :]).then_inc(ynT_ready, 1)

            def front(i, before):
                act.wait_ge(hn_turned, ONE + i + 1)
                for k in range(KD):
                    last = nc.scalar.activation(hT[:, k, :], ps_a[:, k, :], ACT.Identity, bias=cols[:, k, 1:2],
                                                scale=cols[:, k, 0:1])
                last.then_inc(hT_ready, 1)
                act.wait_ge(q_done, ONE + i + 1)
                nc.scalar.copy(qT[:], ps_s[:, 0:2, :]).then_inc(qT_ready, 1)
                act.wait_ge(k_done, ONE + i + 1)
                for h in range(PER_BLOCK):
                    nc.scalar.activation(kT[:, h, :], ps_y[:, 0, :], ACT.Copy, scale=head_mask[:, h:h + 1]).then_inc(k0_ready, 1)
                for t in range(TT):
                    act.wait_ge(qv_done, ONE + TT * i + t + 1)
                    nc.scalar.copy(q_tok[:, t, :], ps_s[:, t % 3, 0:D]).then_inc(qv_ready, 1)
                    nc.scalar.copy(v_sb[:, t, :, 0:HD], ps_s[:, t % 3, D:2 * D].rearrange("p (h c) -> p h c", c=HD)).then_inc(qv_ready, 1)
                for t in range(TT):
                    for f in range(FUTURE):
                        n = FUTURE * t + f
                        act.wait_ge(prod_done, ONE + FUTURE * TT * i + n + 1)
                        if before and n == 0:
                            act.wait_ge(future_step, ONE + 2 * i)
                        nc.scalar.copy(v_future[:, t, f, :], ps_a[:, n % 3, 0:D]).then_inc(vf_ready, 1)
                        if before and n == TURN_AT:
                            output_rows(i - 1)

            def heads(i):
                def exponents(h):
                    u = HEADS * i + h
                    pr = probs[h % 2]
                    if h >= 2:
                        act.wait_ge(turned, ONE + 3 * (u - 1))
                    for bank, tiles in enumerate(BANK_TILES):
                        act.wait_ge(neg_max_ready, ONE + 3 * u + bank + 1)
                        for t in tiles:
                            at = QUERY_AT[t]
                            nc.scalar.activation(pr[:, at:at + (t + 1) * P],
                                                 ps_s[:].rearrange("p a c -> p (a c)")[:, at:at + (t + 1) * P],
                                                 ACT.Exp, bias=neg_max[:, h, t:t + 1], scale=HD ** -0.5).then_inc(exped, 1)

                def copies(h):
                    u = HEADS * i + h
                    if h >= 2:
                        act.wait_ge(head_done, ONE + u - 1)
                    for bank, width in ((0, T), (2, 2 * P)):
                        act.wait_ge(turned, ONE + 3 * u + bank + 1)
                        nc.scalar.copy(probsT[h % 2][:, 512 * bank:512 * bank + width], ps_a[:, bank, 0:width]).then_inc(turned_out, 1)

                def group(g):
                    act.wait_ge(head_done, ONE + HEADS * i + GROUP * (g + 1))
                    nc.scalar.copy(yT[:, g, :], ps_y[:, g % 2, :]).then_inc(group_out, 1)

                exponents(0)
                for h in range(1, HEADS):
                    exponents(h)
                    copies(h - 1)
                    if h >= 5 and (h - 1) % GROUP == 0:
                        group((h - 1) // GROUP - 1)
                copies(HEADS - 1)
                act.wait_ge(shifted, ONE + i + 1)
                nc.scalar.activation(future[:], future[:], ACT.Exp).then_inc(future_exped, 1)
                group(G - 1)

            fold()
            front(0, False)
            with act.Fori(0, B - 1) as i:
                heads(i)
                front(i + 1, True)
            heads(B - 1)
            output_rows(B - 1)

        @block.tensor
        def _(pe):
            pe.wait_ge(first_in, ONE + FIRST)
            pe.wait_ge(setup, ONE + 2)
            w_f, w_q, w_vk = 0, D, 2 * D

            def fold():
                for m in range(KD):
                    for k in range(KD):
                        last = nc.tensor.transpose(ps_a[:, m, k * P:(k + 1) * P],
                                                   w_fqvk[:, k, w_f + m * P:w_f + (m + 1) * P], ident[:])
                last.then_inc(w_f_turned, 1)
                pe.wait_ge(w_fT_ready, ONE + 1)
                pe.wait_ge(later_in, ONE + LATER)
                for f in range(FUTURE):
                    nc.tensor.matmul(up_bank(f), conv[:, f, :], w_fT[:].rearrange("p m c -> p (m c)"),
                                     start=True, stop=True).then_inc(w_up_done, 1)
                for f in range(FUTURE):
                    pe.wait_ge(w_up_ready, ONE + f + 1)
                    for c in range(KD):
                        n = KD * f + c
                        if n >= 3:
                            pe.wait_ge(w_fold_ready, ONE + n - 2)
                        for m in range(KD):
                            last = nc.tensor.matmul(ps_a[:, n % 3, :], v_future[:, m, f, c * P:(c + 1) * P],
                                                    w_fqvk[:, m, w_vk:w_vk + 2 * D], start=(m == 0), stop=(m == KD - 1))
                        last.then_inc(folded, 1)
                pe.wait_ge(w_fold_ready, ONE + FUTURE * KD)

            def projections_read(i):
                pe.wait_ge(k0_ready, ONE + PER_BLOCK * (i + 1))
                pe.wait_ge(k1_ready, ONE + PER_BLOCK * (i + 1))
                pe.wait_ge(qv_ready, ONE + 2 * TT * (i + 1))

            def turn_back(i, t):
                if t >= 2:
                    pe.wait_ge(y_ready, ONE + TT * i + t - 1)
                for g in range(G):
                    last = nc.tensor.transpose(ps_y[:, t % 2, g * P:(g + 1) * P], yT[:, g, t * P:(t + 1) * P], ident[:])
                last.then_inc(y_back, 1)

            def turn_rows(i):
                pe.wait_ge(y_ready, ONE + TT * (i + 1))
                for k in range(KD):
                    for t in range(TT):
                        last = nc.tensor.transpose(ps_s[:, k, t * P:(t + 1) * P], y[:, t, k * P:(k + 1) * P], ident[:])
                last.then_inc(y_turned, 1)

            def output(i):
                pe.wait_ge(ynT_ready, ONE + i + 1)
                out = ps_y[:].rearrange("p a (b d) -> p (a b) d", d=D)
                for t in range(TT):
                    for k in range(KD):
                        last = nc.tensor.matmul(out[:, t, :], ynT[:, k, t * P:(t + 1) * P], w_proj[:, k, :],
                                                start=(k == 0), stop=(k == KD - 1))
                last.then_inc(out_done, 1)

            def front(i, before):
                pe.wait_ge(hn_ready, ONE + i + 1)
                for k in range(KD):
                    for t in range(TT):
                        last = nc.tensor.transpose(ps_a[:, k, t * P:(t + 1) * P], hn[:, t, k * P:(k + 1) * P], ident[:])
                last.then_inc(hn_turned, 1)
                pe.wait_ge(hT_ready, ONE + i + 1)
                pe.wait_ge(group_out, ONE + G * i)
                for done, ps, w0 in ((q_done, ps_s, w_q), (k_done, ps_y, w_vk + D)):
                    for m in range(KD):
                        for k in range(KD):
                            last = nc.tensor.matmul(ps[:, m, :], w_fqvk[:, k, w0 + m * P:w0 + (m + 1) * P], hT[:, k, :],
                                                    start=(k == 0), stop=(k == KD - 1))
                    last.then_inc(done, 1)
                pe.wait_ge(qT_ready, ONE + i + 1)
                for t in range(TT):
                    if t == 3:
                        pe.wait_ge(qv_ready, ONE + 2 * (TT * i + 1))
                    for k in range(KD):
                        last = nc.tensor.matmul(ps_s[:, t % 3, :], hT[:, k, t * P:(t + 1) * P], w_fqvk[:, k, w_q:w_q + 2 * D],
                                                start=(k == 0), stop=(k == KD - 1))
                    last.then_inc(qv_done, 1)
                for t in range(TT):
                    for f in range(FUTURE):
                        n = FUTURE * t + f
                        if n >= 3:
                            pe.wait_ge(vf_ready, ONE + FUTURE * TT * i + n - 2)
                        for k in range(KD):
                            last = nc.tensor.matmul(ps_a[:, n % 3, :], hT[:, k, t * P:(t + 1) * P],
                                                    w_fold[:, f, k, :], start=(k == 0), stop=(k == KD - 1))
                        last.then_inc(kvf_done, 1)
                        if before:
                            if n == TURN_BACK_AT[0]:
                                projections_read(i)
                            if n in TURN_BACK_AT:
                                turn_back(i - 1, TURN_BACK_AT.index(n))
                            if n == TURN_AT:
                                turn_rows(i - 1)
                            if n == OUTPUT_AT:
                                output(i - 1)

            def heads(i, before):
                def score(h):
                    for bank, tiles in enumerate(BANK_TILES):
                        if h:
                            pe.wait_ge(exped, ONE + 4 * (HEADS * i + h - 1) + (1, 3, 4)[bank])
                        for t in tiles:
                            at = QUERY_AT[t] - 512 * bank
                            last = nc.tensor.matmul(ps_s[:, bank, at:at + (t + 1) * P],
                                                    qT[:, h // PER_BLOCK, t * P:(t + 1) * P], kT[:, h, 0:(t + 1) * P],
                                                    start=True, stop=True)
                        last.then_inc(scored, 1)

                def turn(h):
                    u = HEADS * i + h
                    if h == 0:
                        pe.wait_ge(vf_ready, ONE + FUTURE * TT * (i + 1))
                    for bank, tiles in enumerate(((0,), (1, 3), (2,))):
                        if h:
                            if bank == 1:
                                pe.wait_ge(odd_turned_out, ONE + u)
                            else:
                                pe.wait_ge(turned_out, ONE + (2 * u - (1 if bank == 0 else 0)))
                        if bank == 0:
                            pe.wait_ge(exped, ONE + 4 * (u + 1))
                        for s in tiles:
                            for t in range(s, TT):
                                at = SCORE_AT[s] - 512 * bank + (t - s) * P
                                last = nc.tensor.transpose(ps_a[:, bank, at:at + P],
                                                           probs[h % 2][:, QUERY_AT[t] + s * P:QUERY_AT[t] + (s + 1) * P],
                                                           ident[:])
                        last.then_inc(turned, 1)

                def attend(h):
                    u = HEADS * i + h
                    pe.wait_ge(turned_out, ONE + 2 * (u + 1))
                    pe.wait_ge(odd_turned_out, ONE + u + 1)
                    if h % GROUP == 0 and h >= 2 * GROUP:
                        pe.wait_ge(group_out, ONE + G * i + h // GROUP - 1)
                    values_sum(nc, ps_y[:, (h // GROUP) % 2, :], probsT[h % 2], v_sb, h).then_inc(head_done, 1)

                projections_read(i)
                score(0)
                for h in range(HEADS):
                    if h + 1 < HEADS:
                        score(h + 1)
                    turn(h)
                    if h == 1 and before:
                        pe.wait_ge(x1_ready, ONE + i)
                    if h:
                        attend(h - 1)
                attend(HEADS - 1)

            fold()
            front(0, False)
            heads(0, False)
            with pe.Fori(1, B) as i:
                front(i, True)
                heads(i, True)
            pe.wait_ge(group_out, ONE + G * B)
            for t in range(TT):
                turn_back(B - 1, t)
            turn_rows(B - 1)
            output(B - 1)


def layer2_mix(nc, io, keep):
    FF = 4 * D
    NF = FF // P
    with ExitStack() as stack:
        room = Room(nc, stack, "b2")
        ident, x_res = keep.ident, keep.x_res
        w_router = room.sb("w_router", KD, EXPERTS2)
        w_up = room.sb("w_up", EXPERTS2, KD, 2 * D)
        w_down = room.sb("w_down", EXPERTS2, KD, D)
        w_ff1 = room.sb("w_ff1", KD, FF)
        w_ff2 = room.sb("w_ff2", NF, D)
        cols = room.sb("cols", KD, 2)
        xn = room.sb("xn", TT, D)
        x1 = room.sb("x1", TT, D)
        hn = room.sb("hn", TT, D)
        xnT = room.sb("xnT", KD, T)
        hT = room.sb("hT", KD, T)
        top_logit = room.sb("top_logit", TT)
        logits = room.sb("logits", TT, EXPERTS2)
        top = room.sb("top", TT, 8)
        picked = room.sb("picked", TT, EXPERTS2)
        picked_sum = room.sb("picked_sum", TT)
        gate = room.sb("gate", TT, EXPERTS2)
        silu_g = [room.sb(f"silu_g{n}", T) for n in range(2)]
        hidden = [room.sb(f"hidden{n}", KD, T) for n in range(2)]
        gelu = room.sb("gelu", NF, T)
        ps_a = room.ps("ps_a", 2, T)
        ps_gu = [room.ps(f"ps_gu{n}", 2, T) for n in range(2)]
        ps_y = room.ps("ps_y", TT, D)
        ln_a = LayerNorm(nc, room, "ln_a", keep)
        ln_b = LayerNorm(nc, room, "ln_b", keep)
        first_in, ff_in, x1_in = room.sem("first_in"), room.sem("ff_in"), room.sem("x1_in")
        expert_in = [room.sem(f"expert_in{e}") for e in range(EXPERTS2)]
        x1_added = room.sem("x1_added")
        xn_ready, hn_ready = room.sem("xn_ready"), room.sem("hn_ready")
        xn_turned, hn_turned = room.sem("xn_turned"), room.sem("hn_turned")
        xnT_ready, hT_ready = room.sem("xnT_ready"), room.sem("hT_ready")
        routed_logits, route_step, exped = room.sem("routed_logits"), room.sem("route_step"), room.sem("exped")
        up_done, silu_ready, hidden_ready = room.sem("up_done"), room.sem("silu_ready"), room.sem("hidden_ready")
        down_done, expert_added = room.sem("down_done"), room.sem("expert_added")
        ff1_done, gelu_ready, ff2_done = room.sem("ff1_done"), room.sem("gelu_ready"), room.sem("ff2_done")
        batch_done = room.sem("batch_done")
        block = room.block()
        STEPS = 6

        @block.sync
        def _(sp):
            sp.dma_start(w_router[:], io.l2_w_router).then_inc(first_in, DMA)
            sp.dma_start(cols[:], io.l2_cols2).then_inc(first_in, DMA)

            def load_x1(i):
                sp.wait_ge(x1_added, ONE + i)
                sp.dma_start(x1[:], io.x1_scratch[bass.ds(i, 1)].rearrange("a p t d -> p (a t) d")).then_inc(x1_in, DMA)

            load_x1(0)
            for e in range(EXPERTS2):
                sp.dma_start(w_up[:, e], io.l2_w_up[:, e]).then_inc(expert_in[e], DMA)
                sp.dma_start(w_down[:, e], io.l2_w_down[:, e]).then_inc(expert_in[e], DMA)
            sp.dma_start(w_ff1[:], io.l2_w_ff1).then_inc(ff_in, DMA)
            sp.dma_start(w_ff2[:], io.l2_w_ff2).then_inc(ff_in, DMA)
            with sp.Fori(1, B) as i:
                load_x1(i)

        @block.gpsimd
        def _(pool):
            with pool.Fori(0, B) as i:
                ln_a.pool_rstd(pool, i)
                ln_b.pool_rstd(pool, i)

        @block.vector
        def _(dve):
            def norm_x(i):
                def x_tile(t):
                    return x_res[:, bass.ds(TT * i + t, 1), :].rearrange("p a d -> p (a d)")
                ln_a.vector_moments(dve, x_tile, i)
                dve.wait_ge(xn_turned, ONE + i)
                ln_a.vector_apply(dve, x_tile, lambda t: xn[:, t, :], i).then_inc(xn_ready, 1)

            def norm_x1(i):
                dve.wait_ge(x1_in, ONE + DMA * (i + 1))
                ln_b.vector_moments(dve, lambda t: x1[:, t, :], i)
                dve.wait_ge(hn_turned, ONE + i)
                ln_b.vector_apply(dve, lambda t: x1[:, t, :], lambda t: hn[:, t, :], i).then_inc(hn_ready, 1)
                xb = x_res[:, bass.ds(TT * i, TT), :]
                nc.vector.tensor_tensor(xb, xb, x1[:], ALU.add).then_inc(x1_added, 1)

            def route(i):
                at = STEPS * i
                dve.wait_ge(routed_logits, ONE + i + 1)
                raw = ps_a[:, 0, 0:TT * EXPERTS2].rearrange("p (t e) -> p t e", t=TT)
                nc.vector.tensor_reduce(top_logit[:], raw, AX.X, ALU.max).then_inc(route_step, 1)
                dve.wait_ge(route_step, ONE + at + 1)
                nc.vector.tensor_tensor(logits[:], raw, top_logit[:].rearrange("p (t a) -> p t a", a=1)
                                        .broadcast_to([P, TT, EXPERTS2]), ALU.subtract).then_inc(route_step, 1)
                wait_apart(dve, keep.always, exped, i + 1)
                for t in range(TT):
                    last = nc.vector.max(top[:, t, :], logits[:, t, :])
                last.then_inc(route_step, 1)
                dve.wait_ge(route_step, ONE + at + 3)
                for t in range(TT):
                    last = nc.vector.scalar_tensor_tensor(
                        out=picked[:, t, :], in0=logits[:, t, :], scalar=top[:, t, 1:2], in1=logits[:, t, :],
                        op0=ALU.is_ge, op1=ALU.mult, accum_out=picked_sum[:, t:t + 1])
                last.then_inc(route_step, 1)
                dve.wait_ge(route_step, ONE + at + 4)
                nc.vector.reciprocal(picked_sum[:], picked_sum[:]).then_inc(route_step, 1)
                dve.wait_ge(route_step, ONE + at + 5)
                nc.vector.tensor_tensor(gate[:], picked[:], picked_sum[:].rearrange("p (t a) -> p t a", a=1)
                                        .broadcast_to([P, TT, EXPERTS2]), ALU.mult).then_inc(route_step, 1)
                dve.wait_ge(route_step, ONE + at + 6)

            def experts(i):
                def combine(e):
                    dve.wait_ge(down_done, ONE + EXPERTS2 * i + e + 1)
                    if e == 0:
                        dve.wait_ge(batch_done, ONE + i)
                        dve.wait_ge(x1_added, ONE + i + 1)
                    else:
                        dve.wait_ge(expert_added, ONE + EXPERTS2 * i + e)
                    for t in range(TT):
                        xb = x_res[:, bass.ds(TT * i + t, 1), :].rearrange("p a d -> p (a d)")
                        last = nc.vector.scalar_tensor_tensor(out=xb, in0=ps_y[:, t, :], scalar=gate[:, t, e:e + 1],
                                                              in1=xb, op0=ALU.mult, op1=ALU.add)
                    last.then_inc(expert_added, 1)

                for e in range(EXPERTS2):
                    for m in range(KD):
                        at = KD * (EXPERTS2 * i + e) + m
                        dve.wait_ge(silu_ready, ONE + at + 1)
                        if m == 0 and e >= 2:
                            dve.wait_ge(down_done, ONE + EXPERTS2 * i + e - 1)
                        nc.vector.tensor_tensor(hidden[e % 2][:, m, :], silu_g[m][:], ps_gu[m][:, 1, :],
                                                ALU.mult).then_inc(hidden_ready, 1)
                    if e:
                        combine(e - 1)
                combine(EXPERTS2 - 1)

            def finish(i):
                xb = x_res[:, bass.ds(TT * i, TT), :]
                dve.wait_ge(expert_added, ONE + EXPERTS2 * (i + 1))
                dve.wait_ge(ff2_done, ONE + i + 1)
                nc.vector.tensor_tensor(xb, xb, ps_y[:], ALU.add).then_inc(batch_done, 1)

            norm_x(0)
            norm_x1(0)
            with dve.Fori(0, B - 1) as i:
                route(i)
                experts(i)
                norm_x(i + 1)
                norm_x1(i + 1)
                finish(i)
            route(B - 1)
            experts(B - 1)
            finish(B - 1)

        @block.scalar
        def _(act):
            act.wait_ge(first_in, ONE + 2 * DMA)

            def columns(i):
                act.wait_ge(xn_turned, ONE + i + 1)
                nc.scalar.copy(xnT[:], ps_a[:]).then_inc(xnT_ready, 1)
                act.wait_ge(hn_turned, ONE + i + 1)
                for k in range(KD):
                    last = nc.scalar.activation(hT[:, k, :], ps_gu[0][:, k, :], ACT.Identity, bias=cols[:, k, 1:2],
                                                scale=cols[:, k, 0:1])
                last.then_inc(hT_ready, 1)
                act.wait_ge(route_step, ONE + STEPS * i + 2)
                nc.scalar.activation(logits[:], logits[:], ACT.Exp).then_inc(exped, 1)

            def hidden_rows(i):
                for e in range(EXPERTS2):
                    for m in range(KD):
                        at = KD * (EXPERTS2 * i + e) + m
                        act.wait_ge(up_done, ONE + at + 1)
                        if e:
                            act.wait_ge(hidden_ready, ONE + at - 1)
                        nc.scalar.activation(silu_g[m][:], ps_gu[m][:, 0, :], ACT.Silu).then_inc(silu_ready, 1)
                for n in range(NF):
                    act.wait_ge(ff1_done, ONE + NF * i + n + 1)
                    nc.scalar.activation(gelu[:, n, :], ps_gu[n % 2][:, (n // 2) % 2, :], ACT.Gelu).then_inc(gelu_ready, 1)

            columns(0)
            with act.Fori(0, B - 1) as i:
                hidden_rows(i)
                columns(i + 1)
            hidden_rows(B - 1)

        @block.tensor
        def _(pe):
            pe.wait_ge(first_in, ONE + 2 * DMA)

            def turn(i):
                pe.wait_ge(xn_ready, ONE + i + 1)
                pe.wait_ge(route_step, ONE + STEPS * i)
                for k in range(KD):
                    for t in range(TT):
                        last = nc.tensor.transpose(ps_a[:, k, t * P:(t + 1) * P], xn[:, t, k * P:(k + 1) * P], ident[:])
                last.then_inc(xn_turned, 1)
                pe.wait_ge(hn_ready, ONE + i + 1)
                pe.wait_ge(gelu_ready, ONE + NF * i)
                for k in range(KD):
                    for t in range(TT):
                        last = nc.tensor.transpose(ps_gu[0][:, k, t * P:(t + 1) * P], hn[:, t, k * P:(k + 1) * P], ident[:])
                last.then_inc(hn_turned, 1)

            def batch(i, another):
                pe.wait_ge(xnT_ready, ONE + i + 1)
                for t in range(TT):
                    for k in range(KD):
                        last = nc.tensor.matmul(ps_a[:, 0, t * EXPERTS2:(t + 1) * EXPERTS2], xnT[:, k, t * P:(t + 1) * P],
                                                w_router[:, k, :], start=(k == 0), stop=(k == KD - 1))
                last.then_inc(routed_logits, 1)
                pe.wait_ge(hT_ready, ONE + i + 1)

                def up(e):
                    pe.wait_ge(expert_in[e], ONE + 2 * DMA)
                    for m in range(KD):
                        if e:
                            pe.wait_ge(hidden_ready, ONE + KD * (EXPERTS2 * i + e - 1) + m + 1)
                        for half in range(2):
                            for k in range(KD):
                                last = nc.tensor.matmul(ps_gu[m][:, half, :], w_up[:, e, k, half * D + m * P:half * D + (m + 1) * P],
                                                        xnT[:, k, :], start=(k == 0), stop=(k == KD - 1))
                        last.then_inc(up_done, 1)

                def down(e):
                    pe.wait_ge(hidden_ready, ONE + KD * (EXPERTS2 * i + e + 1))
                    if e:
                        pe.wait_ge(expert_added, ONE + EXPERTS2 * i + e)
                    else:
                        pe.wait_ge(batch_done, ONE + i)
                    for t in range(TT):
                        for k in range(KD):
                            last = nc.tensor.matmul(ps_y[:, t, :], hidden[e % 2][:, k, t * P:(t + 1) * P], w_down[:, e, k, :],
                                                    start=(k == 0), stop=(k == KD - 1))
                    last.then_inc(down_done, 1)

                for e in range(EXPERTS2):
                    up(e)
                    if e:
                        down(e - 1)

                pe.wait_ge(ff_in, ONE + 2 * DMA)
                for n in range(NF):
                    if n == 0:
                        pe.wait_ge(hidden_ready, ONE + KD * EXPERTS2 * (i + 1))
                    if n >= 4:
                        pe.wait_ge(gelu_ready, ONE + NF * i + n - 3)
                    for k in range(KD):
                        last = nc.tensor.matmul(ps_gu[n % 2][:, (n // 2) % 2, :], w_ff1[:, k, n * P:(n + 1) * P], hT[:, k, :],
                                                start=(k == 0), stop=(k == KD - 1))
                    last.then_inc(ff1_done, 1)
                    if n == 0:
                        down(EXPERTS2 - 1)
                pe.wait_ge(gelu_ready, ONE + NF * (i + 1))
                pe.wait_ge(expert_added, ONE + EXPERTS2 * (i + 1))
                if another:
                    turn(i + 1)
                for t in range(TT):
                    for n in range(NF):
                        last = nc.tensor.matmul(ps_y[:, t, :], gelu[:, n, t * P:(t + 1) * P], w_ff2[:, n, :],
                                                start=(n == 0), stop=(n == NF - 1))
                last.then_inc(ff2_done, 1)

            turn(0)
            with pe.Fori(0, B - 1) as i:
                batch(i, True)
            batch(B - 1, False)



EXPERTS3, LATENT = 8, 64
RMS_EPS = 1e-6


def layer3_attend(nc, io, keep):
    with ExitStack() as stack:
        room = Room(nc, stack, "a3")
        ident, x_res = keep.ident, keep.x_res
        w_qkv = room.sb("w_qkv", KD, 3 * D)
        cols = room.sb("cols", KD, 6)
        hide_later = room.sb("hide_later", P)
        xn = room.sb("xn", TT, D)
        xnT = room.sb("xnT", KD, T)
        qT = room.sb("qT", KD, T)
        kT = room.sb("kT", KD, T)
        vT = room.sb("vT", KD, T + 2)
        mixT = room.sb("mixT", KD, T)
        nextT = room.sb("nextT", KD, T)
        mix = room.sb("mix", TT, D)
        nxt = room.sb("nxt", TT, D)
        row_max = room.sb("row_max", TT)
        neg_max = room.sb("neg_max", TT)
        row_sum = room.sb("row_sum", TT)
        row_inv = room.sb("row_inv", TT)
        neg_diag = room.sb("neg_diag", TT)
        scrap = room.sb("scrap", TT, P)
        probs = room.sb("probs", SCORE_LEN)
        probsT = room.sb("probsT", SCORE_LEN)
        summed = room.sb("summed", TT, D)
        ps_a = room.ps("ps_a", 3, T)
        ps_s = room.ps("ps_s", 3, T)
        ps_o = room.ps("ps_o", 2, T)
        ln = LayerNorm(nc, room, "ln", keep)
        weights_in, setup, xn_saved = room.sem("weights_in"), room.sem("setup"), room.sem("xn_saved")
        xn_ready, xn_turned, xnT_ready = room.sem("xn_ready"), room.sem("xn_turned"), room.sem("xnT_ready")
        q_done, k_done, v_done = room.sem("q_done"), room.sem("k_done"), room.sem("v_done")
        qT_ready, kT_ready, vT_ready = room.sem("qT_ready"), room.sem("kT_ready"), room.sem("vT_ready")
        mix_step, mixT_ready = room.sem("mix_step"), room.sem("mixT_ready")
        mix_turned, next_turned = room.sem("mix_turned"), room.sem("next_turned")
        mix_ready, next_ready = room.sem("mix_ready"), room.sem("next_ready")
        scored, hidden_later, maxed, neg_max_ready = (room.sem("scored"), room.sem("hidden_later"),
                                                      room.sem("maxed"), room.sem("neg_max_ready"))
        exped, diag_done, turned = room.sem("exped"), room.sem("diag_done"), room.sem("turned")
        turned_out, odd_turned_out = room.sem("turned_out"), room.sem("odd_turned_out")
        inverted, out_done, out_step = room.sem("inverted"), room.sem("out_done"), room.sem("out_step")
        batch_done = room.sem("batch_done")
        block = room.block()
        NLOAD = 3

        @block.sync
        def _(sp):
            n = 0
            for dst, src in ((cols[:], io.l3_cols), (hide_later[:], io.hide_later), (w_qkv[:], io.l3_w_qkv)):
                sp.dma_start(dst, src).then_inc(weights_in, DMA)
                n += 1
            assert n == NLOAD
            with sp.Fori(0, B) as i:
                sp.wait_ge(xn_ready, ONE + i + 1)
                sp.dma_start(io.xn3_scratch[bass.ds(i, 1)].rearrange("a p t d -> p (a t) d"), xn[:]).then_inc(xn_saved, DMA)
            sp.wait_ge(xn_saved, ONE + DMA * B)

        @block.gpsimd
        def _(pool):
            with pool.Fori(0, B) as i:
                ln.pool_rstd(pool, i)

        @block.vector
        def _(dve):
            nc.vector.memset(vT[:, :, 0:1], 0.0).then_inc(setup, 1)
            nc.vector.memset(vT[:, :, T + 1:T + 2], 0.0).then_inc(setup, 1)
            dve.wait_ge(setup, ONE + 2)
            flat = ps_s[:].rearrange("p a c -> p (a c)")

            def norms(i):
                def x_tile(t):
                    return x_res[:, bass.ds(TT * i + t, 1), :].rearrange("p a d -> p (a d)")
                ln.vector_moments(dve, x_tile, i)
                dve.wait_ge(xn_turned, ONE + i)
                dve.wait_ge(xn_saved, ONE + DMA * i)
                ln.vector_apply(dve, x_tile, lambda t: xn[:, t, :], i).then_inc(xn_ready, 1)

            def convolve(i):
                dve.wait_ge(vT_ready, ONE + i + 1)
                dve.wait_ge(next_turned, ONE + i)
                for k in range(KD):
                    nc.vector.tensor_scalar(mixT[:, k, :], vT[:, k, 1:T + 1], cols[:, k, 4:5], None, ALU.mult)
                    last = nc.vector.tensor_scalar(nextT[:, k, :], vT[:, k, 2:T + 2], cols[:, k, 5:6], None, ALU.mult)
                last.then_inc(mix_step, 1)
                dve.wait_ge(mix_step, ONE + 2 * i + 1)
                for k in range(KD):
                    last = nc.vector.scalar_tensor_tensor(out=mixT[:, k, :], in0=vT[:, k, 0:T], scalar=cols[:, k, 3:4],
                                                          in1=mixT[:, k, :], op0=ALU.mult, op1=ALU.add)
                last.then_inc(mix_step, 1)
                dve.wait_ge(mix_step, ONE + 2 * i + 2)
                nc.vector.tensor_tensor(mixT[:], mixT[:], nextT[:], ALU.add).then_inc(mixT_ready, 1)

            def maxima(i):
                dve.wait_ge(scored, ONE + 3 * (i + 1))
                lead = flat[:, 384:384 + 3 * 384].rearrange("p (a c) -> p a c", c=384)[:, :, 0:P]
                nc.vector.tensor_tensor(lead, lead, hide_later[:].rearrange("p (a c) -> p a c", a=1)
                                        .broadcast_to([P, 3, P]), ALU.add)
                at = QUERY_AT[0]
                nc.vector.tensor_tensor(flat[:, at:at + P], flat[:, at:at + P], hide_later[:], ALU.add).then_inc(hidden_later, 1)
                dve.wait_ge(hidden_later, ONE + i + 1)
                for t in range(TT):
                    last = nc.vector.tensor_reduce(row_max[:, t:t + 1], flat[:, QUERY_AT[t]:QUERY_AT[t] + (t + 1) * P],
                                                   AX.X, ALU.max)
                last.then_inc(maxed, 1)
                dve.wait_ge(maxed, ONE + i + 1)
                nc.vector.tensor_scalar(neg_max[:], row_max[:], -D ** -0.5, None, ALU.mult).then_inc(neg_max_ready, 1)

            def combine(i):
                dve.wait_ge(next_turned, ONE + i + 1)
                nc.vector.tensor_copy(nxt[:].rearrange("p t d -> p (t d)"),
                                      ps_a[:, 0:2, :].rearrange("p a d -> p (a d)")).then_inc(next_ready, 1)
                dve.wait_ge(exped, ONE + TT * (i + 1))
                for t in range(TT):
                    at = QUERY_AT[t] + t * P
                    last = nc.vector.scalar_tensor_tensor(out=scrap[:, t, :], in0=probs[:, at:at + P], scalar=-1.0,
                                                          in1=ident[:], op0=ALU.mult, op1=ALU.mult,
                                                          accum_out=neg_diag[:, t:t + 1])
                last.then_inc(diag_done, 1)
                nc.vector.reciprocal(row_inv[:], row_sum[:]).then_inc(inverted, 1)
                dve.wait_ge(turned, ONE + 3 * i + 2)
                nc.vector.tensor_copy(probsT[:, 512:1024], ps_a[:, 1, :]).then_inc(odd_turned_out, 1)

            def finish(i):
                dve.wait_ge(diag_done, ONE + i + 1)
                dve.wait_ge(next_ready, ONE + i + 1)
                dve.wait_ge(inverted, ONE + i + 1)
                dve.wait_ge(out_done, ONE + i + 1)
                out = ps_o[:].rearrange("p a (b d) -> p (a b) d", d=D)
                for t in range(TT):
                    last = nc.vector.scalar_tensor_tensor(out=summed[:, t, :], in0=nxt[:, t, :], scalar=neg_diag[:, t:t + 1],
                                                          in1=out[:, t, :], op0=ALU.mult, op1=ALU.add)
                last.then_inc(out_step, 1)
                dve.wait_ge(out_step, ONE + i + 1)
                for t in range(TT):
                    xb = x_res[:, bass.ds(TT * i + t, 1), :].rearrange("p a d -> p (a d)")
                    last = nc.vector.scalar_tensor_tensor(out=xb, in0=summed[:, t, :], scalar=row_inv[:, t:t + 1],
                                                          in1=xb, op0=ALU.mult, op1=ALU.add)
                last.then_inc(batch_done, 1)

            norms(0)
            dve.wait_ge(weights_in, ONE + NLOAD * DMA)
            with dve.Fori(0, B - 1) as i:
                convolve(i)
                maxima(i)
                combine(i)
                norms(i + 1)
                finish(i)
            convolve(B - 1)
            maxima(B - 1)
            combine(B - 1)
            finish(B - 1)

        @block.scalar
        def _(act):
            act.wait_ge(weights_in, ONE + NLOAD * DMA)
            act.wait_ge(setup, ONE + 2)
            with act.Fori(0, B) as i:
                act.wait_ge(xn_turned, ONE + i + 1)
                nc.scalar.copy(xnT[:], ps_a[:, 0:2, :]).then_inc(xnT_ready, 1)
                for done, ready, ps, out, c, at in ((q_done, qT_ready, ps_s, qT, 0, 0), (v_done, vT_ready, ps_o, vT, 2, 1),
                                                    (k_done, kT_ready, ps_a, kT, 1, 0)):
                    act.wait_ge(done, ONE + i + 1)
                    if out is vT:
                        act.wait_ge(mixT_ready, ONE + i)
                    for k in range(KD):
                        last = nc.scalar.activation(out[:, k, at:at + T], ps[:, k, :], ACT.Identity, bias=cols[:, k, c:c + 1])
                    last.then_inc(ready, 1)
                act.wait_ge(neg_max_ready, ONE + i + 1)
                act.wait_ge(turned, ONE + 3 * i)
                act.wait_ge(diag_done, ONE + i)
                act.wait_ge(inverted, ONE + i)
                for tiles in BANK_TILES:
                    for t in tiles:
                        at = QUERY_AT[t]
                        nc.scalar.activation(probs[:, at:at + (t + 1) * P],
                                             ps_s[:].rearrange("p a c -> p (a c)")[:, at:at + (t + 1) * P],
                                             ACT.Exp, bias=neg_max[:, t:t + 1], scale=D ** -0.5,
                                             accum_out=row_sum[:, t:t + 1]).then_inc(exped, 1)
                act.wait_ge(mix_turned, ONE + i + 1)
                nc.scalar.copy(mix[:].rearrange("p t d -> p (t d)"), ps_o[:].rearrange("p a d -> p (a d)")).then_inc(mix_ready, 1)
                for bank, width in ((0, T), (2, 2 * P)):
                    act.wait_ge(turned, ONE + 3 * i + bank + 1)
                    nc.scalar.copy(probsT[:, 512 * bank:512 * bank + width], ps_a[:, bank, 0:width]).then_inc(turned_out, 1)

        @block.tensor
        def _(pe):
            pe.wait_ge(weights_in, ONE + NLOAD * DMA)
            with pe.Fori(0, B) as i:
                pe.wait_ge(xn_ready, ONE + i + 1)
                pe.wait_ge(turned_out, ONE + 2 * i)
                pe.wait_ge(odd_turned_out, ONE + i)
                for k in range(KD):
                    for t in range(TT):
                        last = nc.tensor.transpose(ps_a[:, k, t * P:(t + 1) * P], xn[:, t, k * P:(k + 1) * P], ident[:])
                last.then_inc(xn_turned, 1)
                pe.wait_ge(xnT_ready, ONE + i + 1)
                for done, ps, c in ((q_done, ps_s, 0), (v_done, ps_o, 2), (k_done, ps_a, 1)):
                    if c == 0:
                        pe.wait_ge(exped, ONE + TT * i)
                    if c == 2:
                        pe.wait_ge(batch_done, ONE + i)
                    for m in range(KD):
                        for k in range(KD):
                            last = nc.tensor.matmul(ps[:, m, :], w_qkv[:, k, c * D + m * P:c * D + (m + 1) * P], xnT[:, k, :],
                                                    start=(k == 0), stop=(k == KD - 1))
                    last.then_inc(done, 1)
                pe.wait_ge(qT_ready, ONE + i + 1)
                pe.wait_ge(kT_ready, ONE + i + 1)
                for bank, tiles in enumerate(BANK_TILES):
                    for t in tiles:
                        at = QUERY_AT[t] - 512 * bank
                        for k in range(KD):
                            last = nc.tensor.matmul(ps_s[:, bank, at:at + (t + 1) * P], qT[:, k, t * P:(t + 1) * P],
                                                    kT[:, k, 0:(t + 1) * P], start=(k == 0), stop=(k == KD - 1))
                    last.then_inc(scored, 1)
                pe.wait_ge(mixT_ready, ONE + i + 1)
                for ps, rows, done in ((ps_o, mixT, mix_turned), (ps_a, nextT, next_turned)):
                    for t in range(TT):
                        for k in range(KD):
                            at = (t % 2) * D + k * P
                            last = nc.tensor.transpose(ps[:, t // 2, at:at + P], rows[:, k, t * P:(t + 1) * P], ident[:])
                    last.then_inc(done, 1)
                pe.wait_ge(exped, ONE + TT * (i + 1))
                pe.wait_ge(next_ready, ONE + i + 1)
                for bank, tiles in enumerate(((0,), (1, 3), (2,))):
                    for s in tiles:
                        for t in range(s, TT):
                            at = SCORE_AT[s] - 512 * bank + (t - s) * P
                            last = nc.tensor.transpose(ps_a[:, bank, at:at + P],
                                                       probs[:, QUERY_AT[t] + s * P:QUERY_AT[t] + (s + 1) * P], ident[:])
                    last.then_inc(turned, 1)
                pe.wait_ge(mix_ready, ONE + i + 1)
                pe.wait_ge(turned_out, ONE + 2 * (i + 1))
                pe.wait_ge(odd_turned_out, ONE + i + 1)
                out = ps_o[:].rearrange("p a (b d) -> p (a b) d", d=D)
                for t in range(TT):
                    for s in range(t + 1):
                        at = SCORE_AT[s] + (t - s) * P
                        last = nc.tensor.matmul(out[:, t, :], probsT[:, at:at + P], mix[:, s, :], start=(s == 0), stop=(s == t))
                last.then_inc(out_done, 1)


def layer3_mix(nc, io, keep):
    with ExitStack() as stack:
        room = Room(nc, stack, "b3")
        ident, x_res = keep.ident, keep.x_res
        w_q = room.sb("w_q", KD, D)
        w_down = room.sb("w_down", KD, P)
        w_up = room.sb("w_up", 2 * D)
        w_o = room.sb("w_o", KD, D)
        w_g = room.sb("w_g", KD, EXPERTS3)
        w_e = room.sb("w_e", KD, EXPERTS3 * D)
        rows = room.sb("rows", 2 * D + EXPERTS3)
        cols = room.sb("cols", KD, 2)
        b_down = room.sb("b_down", 1)
        gains = room.sb("gains", KD, 2)
        eps = room.sb("eps", TT)
        xn = room.sb("xn", TT, D)
        xn_again = room.sb("xn_again", TT, D)
        x1 = room.sb("x1", TT, D)
        hn = [room.sb(f"hn{n}", TT, D) for n in range(2)]
        hT = [room.sb(f"hT{n}", KD, T) for n in range(2)]
        downT = room.sb("downT", T)
        q = room.sb("q", TT, D)
        kv = room.sb("kv", TT, 2 * D)
        prod = [room.sb(f"prod{n}", HEADS * HEADS * HD) for n in range(3)]
        att = room.sb("att", TT, HEADS * HEADS)
        att_max = room.sb("att_max", TT * HEADS)
        att_inv = room.sb("att_inv", TT * HEADS)
        y = room.sb("y", TT, D)
        ynT = room.sb("ynT", KD, T)
        squares = room.sb("squares", 2, TT, D)
        square_sum = room.sb("square_sum", 2, TT)
        spread = room.sb("spread", 2, TT)
        rstd = room.sb("rstd", 2, TT)
        gate = room.sb("gate", TT, EXPERTS3)
        gate_max = room.sb("gate_max", TT)
        ps_t = room.ps("ps_t", 2, T)
        ps_q = room.ps("ps_q", TT, D)
        ps_kv = [room.ps(f"ps_kv{n}", T) for n in range(2)]
        ps_e = [room.ps(f"ps_e{n}", T) for n in range(2)] + ps_kv
        weights_in, setup, zeroed, xn_in = room.sem("weights_in"), room.sem("setup"), room.sem("zeroed"), room.sem("xn_in")
        experts_in, xn_again_in = room.sem("experts_in"), room.sem("xn_again_in")
        square_done = [room.sem(f"square_done{n}") for n in range(2)]
        eps_added = [room.sem(f"eps_added{n}") for n in range(2)]
        rstd_done = [room.sem(f"rstd_done{n}") for n in range(2)]
        h1_ready, h1_turned, h1T_ready = room.sem("h1_ready"), room.sem("h1_turned"), room.sem("h1T_ready")
        h2_ready, h2_turned, h2T_ready = room.sem("h2_ready"), room.sem("h2_turned"), room.sem("h2T_ready")
        q_done, q_ready = room.sem("q_done"), room.sem("q_ready")
        down_done, downT_ready = room.sem("down_done"), room.sem("downT_ready")
        kv_done, kv_ready = room.sem("kv_done"), room.sem("kv_ready")
        qk_multiplied, qk_summed = room.sem("qk_multiplied"), room.sem("qk_summed")
        soft_step, exped = room.sem("soft_step"), room.sem("exped")
        av_multiplied, av_summed = room.sem("av_multiplied"), room.sem("av_summed")
        y_ready, y_turned, ynT_ready, o_done = room.sem("y_ready"), room.sem("y_turned"), room.sem("ynT_ready"), room.sem("o_done")
        x1_step, x1_ready = room.sem("x1_step"), room.sem("x1_ready")
        gate_logits, gate_step, gate_exped = room.sem("gate_logits"), room.sem("gate_step"), room.sem("gate_exped")
        x1_added, expert_done, expert_added = room.sem("x1_added"), room.sem("expert_done"), room.sem("expert_added")
        block = room.block()
        NLOAD = 8
        PAIRS = EXPERTS3 // 2

        @block.sync
        def _(sp):
            def load_xn(i):
                sp.wait_ge(h1_ready, ONE + i)
                sp.dma_start(xn[:], io.xn3_scratch[bass.ds(i, 1)].rearrange("a p t d -> p (a t) d")).then_inc(xn_in, DMA)

            def load_xn_again(i):
                sp.wait_ge(x1_ready, ONE + i)
                sp.dma_start(xn_again[:], io.xn3_scratch[bass.ds(i, 1)].rearrange("a p t d -> p (a t) d")).then_inc(
                    xn_again_in, DMA)

            load_xn(0)
            n = 0
            for dst, src in ((cols[:], io.l3_cols2), (b_down[:], io.l3_b_down), (rows[:], io.l3_rows),
                             (w_down[:], io.l3_w_down), (w_q[:], io.l3_w_q), (w_up[:], io.l3_w_up),
                             (w_o[:], io.l3_w_o), (w_g[:], io.l3_w_g)):
                sp.dma_start(dst, src).then_inc(weights_in, DMA)
                n += 1
            assert n == NLOAD
            sp.dma_start(w_e[:], io.l3_w_e).then_inc(experts_in, DMA)
            with sp.Fori(0, B - 1) as i:
                load_xn(i + 1)
                load_xn_again(i)
            load_xn_again(B - 1)

        @block.gpsimd
        def _(pool):
            nc.gpsimd.memset(eps[:], D * RMS_EPS).then_inc(zeroed, 1)
            pool.wait_ge(zeroed, ONE + 1)

            def rms(i, n):
                pool.wait_ge(square_done[n], ONE + i + 1)
                nc.gpsimd.tensor_tensor(spread[:, n, :], square_sum[:, n, :], eps[:], ALU.add).then_inc(eps_added[n], 1)
                pool.wait_ge(eps_added[n], ONE + i + 1)
                nc.gpsimd.tensor_tensor(rstd[:, n, :], spread[:, n, :], keep.neg_half[:, 0:TT],
                                        ALU.pow).then_inc(rstd_done[n], 1)

            def products(i, before, after):
                pool.wait_ge(q_ready, ONE + i + 1)
                for t in range(TT):
                    if before and t == 2:
                        rms(i - 1, 1)
                    pool.wait_ge(kv_ready, ONE + TT * i + t + 1)
                    if t == 0 and before:
                        pool.wait_ge(av_summed, ONE + TT * i - 1)
                    if t == 1:
                        pool.wait_ge(av_summed, ONE + TT * i)
                    if t == 3:
                        pool.wait_ge(qk_summed, ONE + TT * i + 1)
                    nc.gpsimd.tensor_tensor(
                        prod[t % 3][:].rearrange("p (h g d) -> p h g d", h=HEADS, g=HEADS),
                        q[:, t, :].rearrange("p (h a d) -> p h a d", a=1, d=HD).broadcast_to([P, HEADS, HEADS, HD]),
                        kv[:, t, :].rearrange("p (a g c) -> p a g c", a=1, c=2 * HD)[:, :, :, 0:HD]
                        .broadcast_to([P, HEADS, HEADS, HD]), ALU.mult).then_inc(qk_multiplied, 1)
                if after:
                    rms(i + 1, 0)
                for t in range(TT):
                    pool.wait_ge(exped, ONE + 2 * i + t // 2 + 1)
                    if t == 3:
                        pool.wait_ge(av_summed, ONE + TT * i + 1)
                    else:
                        pool.wait_ge(qk_summed, ONE + TT * i + t + 2)
                    nc.gpsimd.tensor_tensor(
                        prod[(TT + t) % 3][:].rearrange("p (h d g) -> p h d g", h=HEADS, d=HD),
                        att[:, t, :].rearrange("p (h a g) -> p h a g", a=1, g=HEADS).broadcast_to([P, HEADS, HD, HEADS]),
                        kv[:, t, :].rearrange("p (a g c) -> p a c g", a=1, c=2 * HD)[:, :, HD:2 * HD, :]
                        .broadcast_to([P, HEADS, HD, HEADS]), ALU.mult).then_inc(av_multiplied, 1)

            rms(0, 0)
            products(0, False, True)
            with pool.Fori(1, B - 1) as i:
                products(i, True, True)
            products(B - 1, True, False)
            rms(B - 1, 1)

        @block.vector
        def _(dve):
            dve.wait_ge(weights_in, ONE + NLOAD * DMA)
            nc.vector.tensor_scalar(gains[:], cols[:], D ** 0.5, None, ALU.mult).then_inc(setup, 1)
            b_q, b_o, b_g = rows[:, 0:D], rows[:, D:2 * D], rows[:, 2 * D:]

            def wide(row, n):
                return row.rearrange("p (a d) -> p a d", a=1).broadcast_to([P, TT, n])

            def normalise(i, n, x, ready, turned):
                dve.wait_ge(rstd_done[n], ONE + i + 1)
                dve.wait_ge(turned, ONE + i)
                for t in range(TT):
                    last = nc.vector.tensor_scalar(hn[n][:, t, :], x[:, t, :], rstd[:, n, t:t + 1], None, ALU.mult)
                last.then_inc(ready, 1)

            def heads(i, before, after):
                at = 6 * i
                grid = att[:].rearrange("p (u t) (h g) -> p u (t h) g", u=2, g=HEADS)
                half_max = att_max[:].rearrange("p (u h a) -> p u h a", u=2, a=1)

                def sum_qk(t):
                    dve.wait_ge(qk_multiplied, ONE + TT * i + t + 1)
                    nc.vector.tensor_reduce(att[:, t, :], prod[t % 3][:].rearrange("p (h d) -> p h d", d=HD),
                                            AX.X, ALU.add).then_inc(qk_summed, 1)

                def subtract_max(half):
                    dve.wait_ge(qk_summed, ONE + TT * i + 2 * half + 2)
                    nc.vector.tensor_reduce(att_max[:, 2 * HEADS * half:2 * HEADS * (half + 1)], grid[:, half], AX.X,
                                            ALU.max).then_inc(soft_step, 1)
                    dve.wait_ge(soft_step, ONE + at + 2 * half + 1)
                    nc.vector.tensor_tensor(grid[:, half], grid[:, half], half_max[:, half]
                                            .broadcast_to([P, 2 * HEADS, HEADS]), ALU.subtract).then_inc(soft_step, 1)

                def sum_av(t):
                    dve.wait_ge(av_multiplied, ONE + TT * i + t + 1)
                    nc.vector.tensor_reduce(y[:, t, :], prod[(TT + t) % 3][:].rearrange("p (h g) -> p h g", g=HEADS),
                                            AX.X, ALU.add).then_inc(av_summed, 1)

                def last_experts(start, stop):
                    if before:
                        add_experts(i - 1, start, stop)

                sum_qk(0)
                if before:
                    normalise(i - 1, 1, x1, h2_ready, h2_turned)
                sum_qk(1)
                if before:
                    gates(i - 1)
                subtract_max(0)
                last_experts(0, 3)
                sum_qk(2)
                last_experts(3, 7)
                sum_qk(3)
                subtract_max(1)
                last_experts(7, 11)
                if after:
                    first(i + 1)
                dve.wait_ge(exped, ONE + 2 * (i + 1))
                nc.vector.tensor_reduce(att_inv[:], att[:].rearrange("p t (h g) -> p (t h) g", g=HEADS), AX.X,
                                        ALU.add).then_inc(soft_step, 1)
                dve.wait_ge(soft_step, ONE + at + 5)
                nc.vector.reciprocal(att_inv[:], att_inv[:]).then_inc(soft_step, 1)
                dve.wait_ge(y_turned, ONE + i)
                sum_av(0)
                last_experts(11, PAIRS * TT)
                sum_av(1)
                sum_av(2)
                if after:
                    queries(i + 1)
                sum_av(3)
                dve.wait_ge(av_summed, ONE + TT * (i + 1))
                dve.wait_ge(soft_step, ONE + at + 6)
                yr = y[:].rearrange("p t (h d) -> p (t h) d", d=HD)
                nc.vector.tensor_tensor(yr, yr, att_inv[:].rearrange("p (h a) -> p h a", a=1)
                                        .broadcast_to([P, TT * HEADS, HD]), ALU.mult).then_inc(y_ready, 1)
                output(i)

            def queries(i):
                dve.wait_ge(q_done, ONE + i + 1)
                dve.wait_ge(qk_multiplied, ONE + TT * i)
                nc.vector.tensor_tensor(q[:], ps_q[:], wide(b_q, D), ALU.add).then_inc(q_ready, 1)

            def output(i):
                dve.wait_ge(o_done, ONE + i + 1)
                dve.wait_ge(square_done[1], ONE + i)
                nc.vector.tensor_tensor(x1[:], ps_q[:], wide(b_o, D), ALU.add).then_inc(x1_step, 1)
                dve.wait_ge(x1_step, ONE + i + 1)
                dve.wait_ge(xn_again_in, ONE + DMA * (i + 1))
                nc.vector.tensor_tensor(x1[:], x1[:], xn_again[:], ALU.add).then_inc(x1_ready, 1)
                dve.wait_ge(x1_ready, ONE + i + 1)
                xb = x_res[:, bass.ds(TT * i, TT), :]
                nc.vector.tensor_tensor(xb, xb, x1[:], ALU.add).then_inc(x1_added, 1)

            def gates(i):
                at = 6 * i
                dve.wait_ge(gate_logits, ONE + i + 1)
                raw = ps_t[:, 0, 0:TT * EXPERTS3].rearrange("p (t e) -> p t e", t=TT)
                nc.vector.tensor_tensor(gate[:], raw, wide(b_g, EXPERTS3), ALU.add).then_inc(gate_step, 1)
                dve.wait_ge(gate_step, ONE + at + 1)
                nc.vector.tensor_reduce(gate_max[:], gate[:], AX.X, ALU.max).then_inc(gate_step, 1)
                dve.wait_ge(gate_step, ONE + at + 2)

                def by_tile():
                    return gate_max[:].rearrange("p (t a) -> p t a", a=1).broadcast_to([P, TT, EXPERTS3])
                nc.vector.tensor_tensor(gate[:], gate[:], by_tile(), ALU.subtract).then_inc(gate_step, 1)
                dve.wait_ge(gate_exped, ONE + i + 1)
                nc.vector.tensor_reduce(gate_max[:], gate[:], AX.X, ALU.add).then_inc(gate_step, 1)
                dve.wait_ge(gate_step, ONE + at + 4)
                nc.vector.reciprocal(gate_max[:], gate_max[:]).then_inc(gate_step, 1)
                dve.wait_ge(gate_step, ONE + at + 5)
                nc.vector.tensor_tensor(gate[:], gate[:], by_tile(), ALU.mult).then_inc(gate_step, 1)

            def add_experts(i, start, stop):
                dve.wait_ge(x1_added, ONE + i + 1)
                dve.wait_ge(gate_step, ONE + 6 * (i + 1))
                for n in range(start, stop):
                    pair, t = n // TT, n % TT
                    done = PAIRS * TT * i + n
                    dve.wait_ge(expert_done, ONE + done + 1)
                    xb = x_res[:, bass.ds(TT * i + t, 1), :].rearrange("p a d -> p (a d)")
                    for e in range(2):
                        if n or e:
                            dve.wait_ge(expert_added, ONE + 2 * done + e)
                        nc.vector.scalar_tensor_tensor(out=xb, in0=ps_e[n % 4][:, e * D:(e + 1) * D],
                                                       scalar=gate[:, t, 2 * pair + e:2 * pair + e + 1], in1=xb,
                                                       op0=ALU.mult, op1=ALU.add).then_inc(expert_added, 1)

            def first(i):
                normalise(i, 0, xn, h1_ready, h1_turned)

            first(0)
            queries(0)
            heads(0, False, True)
            with dve.Fori(1, B - 1) as i:
                heads(i, True, True)
            heads(B - 1, True, False)
            normalise(B - 1, 1, x1, h2_ready, h2_turned)
            gates(B - 1)
            add_experts(B - 1, 0, PAIRS * TT)

        @block.scalar
        def _(act):
            act.wait_ge(weights_in, ONE + NLOAD * DMA)
            act.wait_ge(setup, ONE + 1)

            def squares_of(x, n, i):
                act.wait_ge(square_done[n], ONE + i)
                act.wait_ge(rstd_done[n], ONE + i)
                for t in range(TT):
                    last = nc.scalar.activation(squares[:, n, t, :], x[:, t, :], ACT.Square, accum_out=square_sum[:, n, t:t + 1])
                last.then_inc(square_done[n], 1)

            def turned_out(i, n, turned, ready):
                act.wait_ge(turned, ONE + i + 1)
                for k in range(KD):
                    last = nc.scalar.activation(hT[n][:, k, :], ps_t[:, k, :], ACT.Copy, scale=gains[:, k, n:n + 1])
                last.then_inc(ready, 1)

            def squares_of_xn(i):
                act.wait_ge(xn_in, ONE + DMA * (i + 1))
                squares_of(xn, 0, i)

            def first(i):
                turned_out(i, 0, h1_turned, h1T_ready)
                act.wait_ge(down_done, ONE + i + 1)
                nc.scalar.activation(downT[:], ps_kv[0][:], ACT.Identity, bias=b_down[:, 0:1]).then_inc(downT_ready, 1)
                for t in range(TT):
                    act.wait_ge(kv_done, ONE + TT * i + t + 1)
                    if isinstance(i, int) and i == 0:
                        nc.scalar.copy(kv[:, t, :], ps_kv[(t + 1) % 2][:]).then_inc(kv_ready, 1)
                        continue
                    act.wait_ge(av_multiplied, ONE + TT * (i - 1) + t + 1)
                    nc.scalar.copy(kv[:, t, :], ps_kv[(t + 1) % 2][:]).then_inc(kv_ready, 1)

            def gates(i):
                turned_out(i, 1, h2_turned, h2T_ready)
                act.wait_ge(gate_step, ONE + 6 * i + 3)
                nc.scalar.activation(gate[:], gate[:], ACT.Exp).then_inc(gate_exped, 1)

            def exp_half(i, half):
                act.wait_ge(soft_step, ONE + 6 * i + 2 * half + 2)
                nc.scalar.activation(att[:, 2 * half:2 * half + 2, :], att[:, 2 * half:2 * half + 2, :], ACT.Exp,
                                     scale=HD ** -0.5).then_inc(exped, 1)

            def heads(i, before, after):
                if before:
                    gates(i - 1)
                exp_half(i, 0)
                if after:
                    squares_of_xn(i + 1)
                exp_half(i, 1)
                if after:
                    first(i + 1)
                act.wait_ge(y_turned, ONE + i + 1)
                nc.scalar.copy(ynT[:], ps_t[:]).then_inc(ynT_ready, 1)
                act.wait_ge(x1_ready, ONE + i + 1)
                squares_of(x1, 1, i)

            squares_of_xn(0)
            first(0)
            heads(0, False, True)
            with act.Fori(1, B - 1) as i:
                heads(i, True, True)
            heads(B - 1, True, False)
            gates(B - 1)

        @block.tensor
        def _(pe):
            pe.wait_ge(weights_in, ONE + NLOAD * DMA)

            def turn(rows_of, done):
                for k in range(KD):
                    for t in range(TT):
                        last = nc.tensor.transpose(ps_t[:, k, t * P:(t + 1) * P], rows_of[:, t, k * P:(k + 1) * P], ident[:])
                last.then_inc(done, 1)

            def project(rows_T, w, done):
                for t in range(TT):
                    for k in range(KD):
                        last = nc.tensor.matmul(ps_q[:, t, :], rows_T[:, k, t * P:(t + 1) * P], w[:, k, :],
                                                start=(k == 0), stop=(k == KD - 1))
                last.then_inc(done, 1)

            def first(i):
                pe.wait_ge(h1_ready, ONE + i + 1)
                turn(hn[0], h1_turned)
                pe.wait_ge(h1T_ready, ONE + i + 1)
                pe.wait_ge(kv_ready, ONE + TT * i)
                for k in range(KD):
                    last = nc.tensor.matmul(ps_kv[0][:], w_down[:, k, :], hT[0][:, k, :], start=(k == 0), stop=(k == KD - 1))
                last.then_inc(down_done, 1)
                pe.wait_ge(q_ready, ONE + i)
                project(hT[0], w_q, q_done)
                pe.wait_ge(downT_ready, ONE + i + 1)
                for t in range(TT):
                    if t >= 2:
                        pe.wait_ge(kv_ready, ONE + TT * i + t - 1)
                    nc.tensor.matmul(ps_kv[(t + 1) % 2][:], downT[:, t * P:(t + 1) * P], w_up[:],
                                     start=True, stop=True).then_inc(kv_done, 1)

            def heads(i, before, after):
                if before:
                    gates(i - 1)
                    experts(i - 1, i + 1)
                if after:
                    pe.wait_ge(expert_added, ONE + 2 * PAIRS * TT * i)
                    first(i + 1)
                pe.wait_ge(y_ready, ONE + i + 1)
                turn(y, y_turned)
                pe.wait_ge(ynT_ready, ONE + i + 1)
                pe.wait_ge(q_ready, ONE + i + (2 if after else 1))
                project(ynT, w_o, o_done)

            def gates(i):
                pe.wait_ge(h2_ready, ONE + i + 1)
                turn(hn[1], h2_turned)
                pe.wait_ge(h2T_ready, ONE + i + 1)
                for t in range(TT):
                    for k in range(KD):
                        last = nc.tensor.matmul(ps_t[:, 0, t * EXPERTS3:(t + 1) * EXPERTS3], hT[1][:, k, t * P:(t + 1) * P],
                                                w_g[:, k, :], start=(k == 0), stop=(k == KD - 1))
                last.then_inc(gate_logits, 1)

            def experts(i, kv_batches):
                pe.wait_ge(experts_in, ONE + DMA)
                pe.wait_ge(kv_ready, ONE + TT * kv_batches)
                pe.wait_ge(gate_step, ONE + 6 * i + 1)
                for n in range(PAIRS * TT):
                    pair, t = n // TT, n % TT
                    done = PAIRS * TT * i + n
                    if n >= 4:
                        pe.wait_ge(expert_added, ONE + 2 * (done - 3))
                    else:
                        pe.wait_ge(expert_added, ONE + 2 * PAIRS * TT * i)
                    for k in range(KD):
                        last = nc.tensor.matmul(ps_e[n % 4][:], hT[1][:, k, t * P:(t + 1) * P],
                                                w_e[:, k, 2 * pair * D:2 * (pair + 1) * D], start=(k == 0), stop=(k == KD - 1))
                    last.then_inc(expert_done, 1)

            first(0)
            heads(0, False, True)
            with pe.Fori(1, B - 1) as i:
                heads(i, True, True)
            heads(B - 1, True, False)
            gates(B - 1)
            experts(B - 1, B)


class Names:
    pass


def build_program(nc, io):
    with ExitStack() as stack:
        keep = Names()
        room = Room(nc, stack, "all")
        keep.ident = room.sb("ident", P)
        keep.neg_half = room.sb("neg_half", 2 * P)
        keep.eps = room.sb("eps", TT)
        keep.always = room.sem("always")
        keep.x_res = room.sb("x_res", NT, D)
        load_constants(nc, io, keep)
        with ExitStack() as layer0:
            room0 = Room(nc, layer0, "l0")
            keep.scan = room0.sb("scan", T + 2, 2, KD * B)
            keep.comb = room0.sb("comb", NT, EXPERTS0 + 1)
            with ExitStack() as both:
                keep.xnT_all = Room(nc, both, "l0x").sb("xnT_all", KD, B * T)
                layer0_project(nc, io, keep)
                layer0_experts(nc, io, keep)
            layer0_mix(nc, io, keep)
        layer1(nc, io, keep)
        layer2(nc, io, keep)
        layer3(nc, io, keep)
        store_output(nc, io, keep)


def load_constants(nc, io, keep):
    with ExitStack() as stack:
        room = Room(nc, stack, "constants")
        loaded = room.sem("loaded")
        block = room.block()

        @block.sync
        def _(sp):
            sp.dma_start(keep.ident[:], io.ident).then_inc(loaded, DMA)
            sp.wait_ge(loaded, ONE + DMA)

        @block.gpsimd
        def _(pool):
            nc.gpsimd.memset(keep.neg_half[:], -0.5)
            nc.gpsimd.memset(keep.eps[:], LN_EPS).then_inc(keep.always, 1)


def layer2(nc, io, keep):
    layer2_attend(nc, io, keep)
    layer2_mix(nc, io, keep)


def layer3(nc, io, keep):
    layer3_attend(nc, io, keep)
    layer3_mix(nc, io, keep)


def store_output(nc, io, keep):
    with ExitStack() as stack:
        room = Room(nc, stack, "out")
        stored = room.sem("stored")
        block = room.block()

        @block.sync
        def _(sp):
            sp.dma_start(io.out.rearrange("b p t d -> p b t d"),
                         keep.x_res[:].rearrange("p (b t) d -> p b t d", b=B)).then_inc(stored, DMA)
            sp.wait_ge(stored, ONE + DMA)


def kernel(**a):
    from collections import namedtuple
    import numpy as np
    import concourse.bacc as bacc
    from concourse.bass_utils import run_bass_kernel_spmd as run

    a = {n: np.asarray(v) for n, v in a.items()}
    f4 = np.float32

    def k_major(w):
        return np.ascontiguousarray(w.reshape(-1, P, w.shape[-1]).transpose(1, 0, 2))

    def columns(*rows):
        return np.ascontiguousarray(np.stack([r.reshape(-1, P).T for r in rows], -1))

    def all_rows(row):
        return np.ascontiguousarray(np.broadcast_to(row, (P, row.size)))

    x = a["L0_attn_x"].reshape(B, TT, P, D).transpose(0, 2, 1, 3)
    data = {
        "x": x,
        "ident": np.eye(P, dtype=f4),
        "l0_w_kvr": k_major(np.concatenate([a["L0_attn_Wk"], a["L0_attn_Wv"], a["L0_attn_Wr"]], 1)),
        "l0_w_gate": k_major(a["L0_ffn_gate_w"].T),
        "l0_gate_b": all_rows(a["L0_ffn_gate_b"]),
        "l0_w13s": k_major(a["L0_ffn_w13_s"].T),
        "l0_w2s": a["L0_ffn_w2_s"].T,
        "l0_cols": columns(a["L0_attn_ln1_g"], a["L0_attn_ln1_b"], a["L0_attn_time_shift"].reshape(D), a["L0_attn_time_decay"]),
        "l0_w13": a["L0_ffn_w13"].transpose(0, 2, 1).reshape(EXPERTS0, KD, P, 2 * INTER0).transpose(0, 2, 1, 3),
        "l0_w2": a["L0_ffn_w2"].transpose(0, 2, 1),
        "l0_w_ck": k_major(a["L0_attn_Wck"]),
        "l0_w_cv": k_major(a["L0_attn_Wcv"]),
        "l0_w_cr": k_major(a["L0_attn_Wcr"]),
        "l0_cols2": columns(a["L0_attn_ln2_g"], a["L0_attn_ln2_b"], a["L0_attn_time_shift"].reshape(D), a["L0_attn_time_first"]),
    }
    by_head = np.arange(P) // HD
    data.update({
        "head_mask": (by_head[:, None] == np.arange(PER_BLOCK)[None, :]).astype(f4),
        "causal": np.triu(np.ones((P, P), f4)),
        "l1_w_qkv": k_major(np.concatenate([a["L1_attn_Wq"], a["L1_attn_Wk"], a["L1_attn_Wv"]], 0).T),
        "l1_w_o": k_major(a["L1_attn_Wo"].T),
        "l1_weight": k_major(a["L1_ffn_weight"].T),
        "l1_bias": all_rows(a["L1_ffn_bias"]),
        "l1_consts": np.stack([np.tile(a["L1_attn_gamma"], P // HD), np.tile(a["L1_attn_beta"], P // HD),
                               np.repeat(a["L1_ffn_alpha"], P)], -1),
    })
    w_q, w_k, w_v, w_f = np.split(a["L2_attn_W_qkvf"], 4, 0)
    data.update({
        "hide_later": np.triu(np.full((P, P), NEG, f4), 1),
        "l2_w_fqvk": k_major(np.concatenate([w_f, w_q, w_v, w_k], 0).T),
        "l2_w_proj": k_major(a["L2_attn_W_proj"].T),
        "l2_conv": a["L2_attn_W_conv"].transpose(0, 2, 1),
        "l2_cols": columns(a["L2_attn_ln1_g"], a["L2_attn_ln1_b"]),
        "l2_w_router": k_major(a["L2_ffn_router_w"].T),
        "l2_w_up": a["L2_ffn_up_proj"].reshape(EXPERTS2, KD, P, 2 * D).transpose(2, 0, 1, 3),
        "l2_w_down": a["L2_ffn_down_proj"].reshape(EXPERTS2, KD, P, D).transpose(2, 0, 1, 3),
        "l2_w_ff1": k_major(a["L2_attn_W_ff1"]),
        "l2_w_ff2": k_major(a["L2_attn_W_ff2"]),
        "l2_cols2": columns(a["L2_attn_ln2_g"], a["L2_attn_ln2_b"]),
    })
    zeros = np.zeros((P - LATENT - 1, 2 * D), f4)
    data.update({
        "l3_w_qkv": k_major(a["L3_attn_W_qkv"]),
        "l3_cols": columns(*np.split(a["L3_attn_b_qkv"], 3), *a["L3_attn_W_vconv"].T),
        "l3_w_q": k_major(a["L3_ffn_Wq"]),
        "l3_w_down": k_major(np.concatenate([a["L3_ffn_Wdown"], np.zeros((D, P - LATENT), f4)], 1)),
        "l3_w_up": np.concatenate([a["L3_ffn_Wup"], a["L3_ffn_bup"][None], zeros], 0),
        "l3_b_down": np.concatenate([a["L3_ffn_bdown"], np.ones(1, f4), zeros[:, 0]])[:, None],
        "l3_w_o": k_major(a["L3_ffn_Wo"]),
        "l3_w_g": k_major(a["L3_ffn_Wg"]),
        "l3_w_e": k_major(a["L3_ffn_We"].transpose(1, 0, 2).reshape(D, EXPERTS3 * D)),
        "l3_rows": all_rows(np.concatenate([a["L3_ffn_bq"], a["L3_ffn_bo"], a["L3_ffn_bg"]])),
        "l3_cols2": columns(a["L3_ffn_gamma1"], a["L3_ffn_gamma2"]),
    })
    nc = bacc.Bacc("TRN2", target_bir_lowering=False, num_devices=1)
    data = {name: np.ascontiguousarray(value) for name, value in data.items()}
    shapes = {"out": (B, P, TT, D), "xn_scratch": (B, P, TT, D), "x1_scratch": (B, P, TT, D),
              "xn3_scratch": (B, P, TT, D), "v_scratch": (B, P, KD, T), "r_scratch": (B, P, KD, T)}
    dram = {name: nc.dram_tensor(name, value.shape, F32, kind="ExternalInput").ap() for name, value in data.items()}
    dram["out"] = nc.dram_tensor("out", shapes.pop("out"), F32, kind="ExternalOutput").ap()
    dram.update({name: nc.dram_tensor(name, shape, F32).ap() for name, shape in shapes.items()})
    io = namedtuple("Dram", dram)(**dram)
    build_program(nc, io)
    got = run(nc, [data], core_ids=[0]).results[0]["out"]
    return got.reshape(B, P, TT, D).transpose(0, 2, 1, 3).reshape(B, T, D)
```
